# Optimizing a Trainium2 kernel written in Bass

```python
import numpy as np
import jax
import jax.numpy as jnp

def _softmax(x, axis=-1):
    return jax.nn.softmax(x, axis=axis)

def _gelu(x):
    return jax.nn.gelu(x, approximate=True)

def _silu(x):
    return jax.nn.silu(x)

def _sigmoid(x):
    return jax.nn.sigmoid(x)

def _layernorm(x, axis=-1, eps=1e-05):
    m = jnp.mean(x, axis=axis, keepdims=True)
    v = jnp.var(x, axis=axis, keepdims=True)
    return (x - m) / jnp.sqrt(v + eps)

def _scatter_add(tgt, idx, src, axis=0):
    return tgt.at[idx].add(src)

def _segment_sum(src, seg, n):
    return jax.ops.segment_sum(src, seg, n)
kernel_name = 'mk_hybrid_d1_jaxref_r8_a6402f'

def setup_inputs(seed: int=0):
    np.random.seed(seed)
    _w = jnp.asarray

    def _L0_attn_a_setup():
        import jax, jax.numpy as jnp
        import numpy as np
        W_SEG = 256
        R = 4
        OFFSET = 0
        H = 16
        C = 128
        M = W_SEG // R

        def _mha(xi, w_in, b_in, w_out, b_out):
            b, s, m, c = xi.shape
            dh = c // H
            qkv = jnp.einsum('bsmc,ec->bsme', xi, w_in) + b_in
            q, k, v = jnp.split(qkv, 3, axis=-1)
            q = q.reshape(b, s, m, H, dh)
            k = k.reshape(b, s, m, H, dh)
            v = v.reshape(b, s, m, H, dh)
            scores = jnp.einsum('bsqhd,bskhd->bshqk', q, k) / jnp.sqrt(jnp.asarray(dh, xi.dtype))
            causal = jnp.tril(jnp.ones((m, m), dtype=bool))
            scores = jnp.where(causal, scores, jnp.asarray(-1000000000.0, xi.dtype))
            p = jax.nn.softmax(scores, axis=-1)
            o = jnp.einsum('bshqk,bskhd->bsqhd', p, v).reshape(b, s, m, c)
            return jnp.einsum('bsmc,oc->bsmo', o, w_out) + b_out
        key = jax.random.key(seed)
        k1, k2, k3, k4, k5 = jax.random.split(key, 5)
        x = jax.random.normal(k1, (4, 1024, C), dtype=jnp.float32)
        w_in = jax.random.normal(k2, (3 * C, C), dtype=jnp.float32) * C ** (-0.5)
        b_in = jnp.zeros((3 * C,), dtype=jnp.float32)
        w_out = jax.random.normal(k3, (C, C), dtype=jnp.float32) * C ** (-0.5)
        b_out = jnp.zeros((C,), dtype=jnp.float32)
        return {'x': x, 'w_in': w_in, 'b_in': b_in, 'w_out': w_out, 'b_out': b_out}
    _L0_attn_a_in = _L0_attn_a_setup()

    def _L0_attn_b_setup():
        import math
        import jax, jax.numpy as jnp
        import numpy as np
        D_MODEL = 128
        N_HEADS = 16
        D_HEAD = D_MODEL // N_HEADS
        BLOCK = 256
        BATCH = 2
        SEQ = 256

        def _rotate(t, cos, sin):
            t1 = t[..., 0::2]
            t2 = t[..., 1::2]
            r1 = t1 * cos - t2 * sin
            r2 = t1 * sin + t2 * cos
            return jnp.stack([r1, r2], axis=-1).reshape(t.shape)
        key = jax.random.key(seed)
        k1, k2, k3 = jax.random.split(key, 3)
        x = jax.random.normal(k1, (BATCH, SEQ, D_MODEL), dtype=jnp.float32)
        Wqkv = jax.random.normal(k2, (3 * D_MODEL, D_MODEL), dtype=jnp.float32) * 0.02
        Wo = jax.random.normal(k3, (D_MODEL, D_MODEL), dtype=jnp.float32) * 0.02
        log_xi = jnp.full((N_HEADS,), math.log(BLOCK / 2.0), dtype=jnp.float32)
        pi_gate_logit = jnp.full((N_HEADS,), 2.0, dtype=jnp.float32)
        e_gate_logit = jnp.full((N_HEADS,), 2.0, dtype=jnp.float32)
        return {'x': x, 'Wqkv': Wqkv, 'Wo': Wo, 'log_xi': log_xi, 'pi_gate_logit': pi_gate_logit, 'e_gate_logit': e_gate_logit}
    _L0_attn_b_in = _L0_attn_b_setup()

    def _L0_ffn_setup():
        import jax, jax.numpy as jnp
        import numpy as np
        B, S, D = (4, 512, 128)
        E, F_EXP = (16, 256)
        F_C = 2.0
        F_SH = 256
        key = jax.random.key(seed)
        ks = jax.random.split(key, 8)
        s = 0.02
        return {'hidden_states': jax.random.normal(ks[0], (B, S, D), jnp.float32), 'gate_w': jax.random.normal(ks[1], (E, D), jnp.float32) * s, 'Wg': jax.random.normal(ks[2], (E, F_EXP, D), jnp.float32) * s, 'Wu': jax.random.normal(ks[3], (E, F_EXP, D), jnp.float32) * s, 'Wd': jax.random.normal(ks[4], (E, D, F_EXP), jnp.float32) * s, 'Ws_g': jax.random.normal(ks[5], (F_SH, D), jnp.float32) * s, 'Ws_u': jax.random.normal(ks[6], (F_SH, D), jnp.float32) * s, 'Ws_d': jax.random.normal(ks[7], (D, F_SH), jnp.float32) * s}
    _L0_ffn_in = _L0_ffn_setup()
    _d = {'L0_attn_a_x': _L0_attn_a_in['x'], 'L0_attn_a_w_in': _L0_attn_a_in['w_in'], 'L0_attn_a_b_in': _L0_attn_a_in['b_in'], 'L0_attn_a_w_out': _L0_attn_a_in['w_out'], 'L0_attn_a_b_out': _L0_attn_a_in['b_out'], 'L0_attn_b_Wqkv': _L0_attn_b_in['Wqkv'], 'L0_attn_b_Wo': _L0_attn_b_in['Wo'], 'L0_attn_b_log_xi': _L0_attn_b_in['log_xi'], 'L0_attn_b_pi_gate_logit': _L0_attn_b_in['pi_gate_logit'], 'L0_attn_b_e_gate_logit': _L0_attn_b_in['e_gate_logit'], 'L0_ffn_gate_w': _L0_ffn_in['gate_w'], 'L0_ffn_Wg': _L0_ffn_in['Wg'], 'L0_ffn_Wu': _L0_ffn_in['Wu'], 'L0_ffn_Wd': _L0_ffn_in['Wd'], 'L0_ffn_Ws_g': _L0_ffn_in['Ws_g'], 'L0_ffn_Ws_u': _L0_ffn_in['Ws_u'], 'L0_ffn_Ws_d': _L0_ffn_in['Ws_d']}
    _x0 = _d['L0_attn_a_x']
    _d['L0_attn_a_x'] = jax.random.normal(jax.random.fold_in(jax.random.key(seed), 1), (16, 512, 128), dtype=_x0.dtype)
    del _x0
    return _d

def reference(L0_attn_a_x, L0_attn_a_w_in, L0_attn_a_b_in, L0_attn_a_w_out, L0_attn_a_b_out, L0_attn_b_Wqkv, L0_attn_b_Wo, L0_attn_b_log_xi, L0_attn_b_pi_gate_logit, L0_attn_b_e_gate_logit, L0_ffn_gate_w, L0_ffn_Wg, L0_ffn_Wu, L0_ffn_Wd, L0_ffn_Ws_g, L0_ffn_Ws_u, L0_ffn_Ws_d):

    def _L0_attn_a_ref(x, w_in, b_in, w_out, b_out):
        import jax, jax.numpy as jnp
        import numpy as np
        W_SEG = 256
        R = 4
        OFFSET = 0
        H = 16
        C = 128
        M = W_SEG // R

        def _mha(xi, w_in, b_in, w_out, b_out):
            b, s, m, c = xi.shape
            dh = c // H
            qkv = jnp.einsum('bsmc,ec->bsme', xi, w_in) + b_in
            q, k, v = jnp.split(qkv, 3, axis=-1)
            q = q.reshape(b, s, m, H, dh)
            k = k.reshape(b, s, m, H, dh)
            v = v.reshape(b, s, m, H, dh)
            scores = jnp.einsum('bsqhd,bskhd->bshqk', q, k) / jnp.sqrt(jnp.asarray(dh, xi.dtype))
            causal = jnp.tril(jnp.ones((m, m), dtype=bool))
            scores = jnp.where(causal, scores, jnp.asarray(-1000000000.0, xi.dtype))
            p = jax.nn.softmax(scores, axis=-1)
            o = jnp.einsum('bshqk,bskhd->bsqhd', p, v).reshape(b, s, m, c)
            return jnp.einsum('bsmc,oc->bsmo', o, w_out) + b_out
        b, n, c = x.shape
        s = n // W_SEG
        xr = x.reshape(b, s, W_SEG, c)
        xi = xr[:, :, OFFSET::R, :]
        oi = _mha(xi, w_in, b_in, w_out, b_out)
        out = jnp.zeros_like(xr).at[:, :, OFFSET::R, :].set(oi)
        return out.reshape(b, n, c)

    def _L0_attn_b_ref(x, Wqkv, Wo, log_xi, pi_gate_logit, e_gate_logit):
        import math
        import jax, jax.numpy as jnp
        import numpy as np
        D_MODEL = 128
        N_HEADS = 16
        D_HEAD = D_MODEL // N_HEADS
        BLOCK = 256
        BATCH = 2
        SEQ = 256

        def _rotate(t, cos, sin):
            t1 = t[..., 0::2]
            t2 = t[..., 1::2]
            r1 = t1 * cos - t2 * sin
            r2 = t1 * sin + t2 * cos
            return jnp.stack([r1, r2], axis=-1).reshape(t.shape)
        b, n, d = x.shape
        H, dh = (N_HEADS, D_HEAD)
        qkv = (x @ Wqkv.T).reshape(b, n, 3, H, dh)
        q = jnp.transpose(qkv[:, :, 0], (0, 2, 1, 3))
        k = jnp.transpose(qkv[:, :, 1], (0, 2, 1, 3))
        v = jnp.transpose(qkv[:, :, 2], (0, 2, 1, 3))
        pi_g = jax.nn.sigmoid(pi_gate_logit)
        e_g = jax.nn.sigmoid(e_gate_logit)
        kfrac = jnp.arange(0, dh, 2, dtype=jnp.float32) / dh
        pi_inv_freq = jnp.float32(math.pi) ** (1.0 - kfrac)
        pos = jnp.arange(n, dtype=jnp.float32)
        theta = pos[:, None] * pi_inv_freq[None, :]
        theta = theta[None, :, :] * pi_g[:, None, None]
        cos, sin = (jnp.cos(theta), jnp.sin(theta))
        q_rot = _rotate(q, cos, sin)
        k_rot = _rotate(k, cos, sin)
        scores = jnp.einsum('bhqd,bhkd->bhqk', q_rot, k_rot) / jnp.float32(math.sqrt(dh))
        xi = jnp.exp(log_xi)
        i = jnp.arange(n, dtype=jnp.float32)
        d_mat = jnp.abs(i[:, None] - i[None, :])
        decay_bias = -(d_mat[None, :, :] / xi[:, None, None]) * e_g[:, None, None]
        scores = scores + decay_bias[None]
        causal = jnp.tril(jnp.ones((n, n), dtype=bool))
        scores = jnp.where(causal[None, None], scores, jnp.float32(-jnp.inf))
        attn = jax.nn.softmax(scores, axis=-1)
        out = jnp.einsum('bhqk,bhkd->bhqd', attn, v)
        out = jnp.transpose(out, (0, 2, 1, 3)).reshape(b, n, d)
        return out @ Wo.T

    def _L0_ffn_ref(hidden_states, gate_w, Wg, Wu, Wd, Ws_g, Ws_u, Ws_d):
        import jax, jax.numpy as jnp
        import numpy as np
        B, S, D = (4, 512, 128)
        E, F_EXP = (16, 256)
        F_C = 2.0
        F_SH = 256
        b, s, d = hidden_states.shape
        e = gate_w.shape[0]
        cap = int(s * F_C / e)
        logits = jnp.einsum('bsd,ed->bse', hidden_states, gate_w)
        scores = jax.nn.softmax(logits, axis=-1).transpose(0, 2, 1)
        topk_w, topk_idx = jax.lax.top_k(scores, cap)
        x_tok = jnp.take_along_axis(hidden_states[:, None, :, :], topk_idx[..., None], axis=2)
        g = jnp.einsum('becd,efd->becf', x_tok, Wg)
        u = jnp.einsum('becd,efd->becf', x_tok, Wu)
        h = jax.nn.gelu(g, approximate=False) * u
        eo = jnp.einsum('becf,edf->becd', h, Wd) * topk_w[..., None]
        offs = (jnp.arange(b) * s)[:, None, None]
        flat_idx = (topk_idx + offs).reshape(-1)
        flat = jnp.zeros((b * s, d), hidden_states.dtype)
        flat = flat.at[flat_idx].add(eo.reshape(-1, d))
        out = flat.reshape(b, s, d)
        gs = jnp.einsum('bsd,fd->bsf', hidden_states, Ws_g)
        us = jnp.einsum('bsd,fd->bsf', hidden_states, Ws_u)
        shared = jnp.einsum('bsf,df->bsd', jax.nn.gelu(gs, approximate=False) * us, Ws_d)
        return out + shared
    x = L0_attn_a_x
    x = x + _L0_attn_a_ref(_layernorm(x, axis=-1), L0_attn_a_w_in, L0_attn_a_b_in, L0_attn_a_w_out, L0_attn_a_b_out)
    x = x + _L0_ffn_ref(_layernorm(x, axis=-1), L0_ffn_gate_w, L0_ffn_Wg, L0_ffn_Wu, L0_ffn_Wd, L0_ffn_Ws_g, L0_ffn_Ws_u, L0_ffn_Ws_d)
    x = x + _L0_attn_b_ref(_layernorm(x, axis=-1), L0_attn_b_Wqkv, L0_attn_b_Wo, L0_attn_b_log_xi, L0_attn_b_pi_gate_logit, L0_attn_b_e_gate_logit)
    x = x + _L0_ffn_ref(_layernorm(x, axis=-1), L0_ffn_gate_w, L0_ffn_Wg, L0_ffn_Wu, L0_ffn_Wd, L0_ffn_Ws_g, L0_ffn_Ws_u, L0_ffn_Ws_d)
    return x

_drawn_inputs = setup_inputs


def setup_inputs(seed=0):
    import zlib

    import numpy as np

    out = dict(_drawn_inputs(seed))
    spreads = {'L0_attn_a_b_in': (0.0, 0.1),
     'L0_attn_a_b_out': (0.0, 0.1),
     'L0_attn_b_log_xi': (4.852030277252197, 0.6),
     'L0_attn_b_pi_gate_logit': (2.0, 0.6),
     'L0_attn_b_e_gate_logit': (2.0, 0.6)}
    factors = {'L0_attn_b_Wqkv': 8.0,
     'L0_attn_b_Wo': 8.0,
     'L0_ffn_gate_w': 8.0,
     'L0_ffn_Wg': 8.0,
     'L0_ffn_Wu': 8.0,
     'L0_ffn_Wd': 8.0,
     'L0_ffn_Ws_g': 3.466,
     'L0_ffn_Ws_u': 3.389,
     'L0_ffn_Ws_d': 3.408}
    for name, (base, spread) in spreads.items():
        noise = np.random.default_rng([zlib.crc32(name.encode()), seed]).standard_normal(out[name].shape)
        drawn = base * np.exp(spread * noise) if base else spread * noise
        out[name] = jnp.asarray(drawn.astype(out[name].dtype))
    for name, factor in factors.items():
        out[name] = (out[name] * factor).astype(out[name].dtype)
    return out
```

```python
from contextlib import ExitStack
import math

import numpy as np
import concourse.bass as bass
from concourse import mybir

F32 = mybir.dt.float32
BF16 = mybir.dt.bfloat16
U32 = mybir.dt.uint32
I32 = mybir.dt.int32
ALU = mybir.AluOpType
ACT = mybir.ActivationFunctionType
AX = mybir.AxisListType

P = 128
B, N, D = 16, 512, 128
H, DH = 16, 8
T = N // P
E, FE, CAP = 16, 256, 64
FJ = FE // P
EPS = 1e-5
MASKED = -1.0e30
STRIDE_A, SEG_A = 4, 64
SLOT = 64
DECAY_AT, MAX_AT = 6 * DH, 6 * DH + 3
ROWS1, ROWS2 = MAX_AT, MAX_AT + 3
ANGLE_STEPS = (22, 29)
POOL_SETUP = {True: 17, False: 15}
SCALE = 1.0 / math.sqrt(DH)


def need(eng, sem, value):
    if isinstance(value, int) and value <= 0:
        return
    eng.wait_ge(sem, value)


def need_apart(eng, sem, value, least):
    if isinstance(value, int):
        return need(eng, sem, value)
    at = eng.to_reg(value)
    eng.wait_ge(sem, least)
    eng.wait_ge(sem, at)


class Count:

    def __init__(self, sem, per_turn):
        self.sem, self.per_turn = sem, per_turn

    def turn(self, i):
        self.base, self.n = self.per_turn * i, 0

    def add(self, ins):
        ins.then_inc(self.sem, 1)
        self.n += 1

    def wait(self, eng):
        eng.wait_ge(self.sem, self.base + self.n)

    def wait_apart(self, eng):
        need_apart(eng, self.sem, self.base + self.n, self.n)

    def end(self, what):
        assert self.n == self.per_turn, (what, self.n, self.per_turn)


def live(m, count):
    return not isinstance(m, int) or 0 <= m < count


def pipeline(eng, body, count, peel, drain):
    for n in range(peel):
        body(n, n % 2, n // 2)
    with eng.Fori(peel // 2, count // 2) as j:
        body(2 * j, 0, j)
        body(2 * j + 1, 1, j)
    for n in range(count, count + drain):
        body(n, n % 2, n // 2)


def moe_block(nc, tag, src, dst, xn_dram, gate_w, w_exp, w_sh, wd_sh):
    UNITS = 2 * FJ
    PAIRS = B // 2
    xn_rows = xn_dram.rearrange("b n d -> (b n) d")
    dst_rows = dst.rearrange("b n d -> (b n) d")
    with ExitStack() as ctx:
        def sb(name, shape, dt=F32):
            return ctx.enter_context(nc.sbuf_tensor(f"{tag}_{name}", shape, dt))

        def sem(name):
            return ctx.enter_context(nc.semaphore(f"{tag}_{name}"))

        ps = ctx.enter_context(nc.psum_tensor(f"{tag}_ps", [P, 8, 512], F32))
        ident = sb("ident", [P, P])
        xr = sb("xr", [P, B * T, D])
        gw = sb("gw", [P, E])
        wsh = sb("wsh", [P, 2 * FE])
        wdsh = sb("wdsh", [P, FJ, D])
        stats = sb("stats", [P, 2, T, 6])
        mv = sb("mv", [P, 2, T, 2])
        ve = sb("ve", [P, 2, T])
        expo = sb("expo", [P, T])
        rstd = sb("rstd", [P, 2, T])
        xn = sb("xn", [P, 2, T, D])
        xnT = sb("xnT", [P, 2, N])
        gel = sb("gel", [P, 2, 512])
        hT = sb("hT", [P, 2, FJ, 2 * 512])
        y = sb("y", [P, 2, T, D])
        lg = sb("lg", [P, B * T, E])
        pr = sb("pr", [P, 2, T, P])
        red = sb("red", [P, B * T])
        rows = sb("rows", [P, 2, N])
        top = sb("top", [P, 2, CAP])
        pos = sb("pos", [P, 2, CAP], U32)
        topd = sb("topd", [P, 2, 2, CAP])
        posd = sb("posd", [P, 2, 2, CAP])
        roff_i = sb("roff_i", [P, 1], I32)
        roff = sb("roff", [P, 2])
        tokens = sb("tokens", [P, E * PAIRS], U32)
        weight = sb("weight", [P, E, PAIRS])
        xg = sb("xg", [P, 2, PAIRS, D])
        xgT = sb("xgT", [P, 2, 1024])
        wexp = sb("wexp", [P, 2, 2 * FE + FJ * D])
        eo = sb("eo", [P, 2, PAIRS, D])

        consts_loaded = sem("consts_loaded")
        x_loaded = sem("x_loaded")
        pool_setup = sem("pool_setup")
        vchain = sem("vchain")
        var_ready = sem("var_ready")
        rstd_ready = sem("rstd_ready")
        xn_ready = sem("xn_ready")
        xn_stored = [sem(f"xn_stored{s}") for s in range(2)]
        turned = sem("turned")
        xnT_ready = sem("xnT_ready")
        logits_done = sem("logits_done")
        logits_read = sem("logits_read")
        gu_done = sem("gu_done")
        gelu_done = sem("gelu_done")
        h_ready = sem("h_ready")
        down_done = sem("down_done")
        y_ready = sem("y_ready")
        y_stored = [sem(f"y_stored{s}") for s in range(2)]
        shifted = sem("shifted")
        exped = sem("exped")
        probs_ready = sem("probs_ready")
        rows_turned = sem("rows_turned")
        rows_ready = sem("rows_ready")
        top_ready = sem("top_ready")
        top_turned = sem("top_turned")
        tokens_ready = sem("tokens_ready")
        gathered = [sem(f"gathered{s}") for s in range(2)]
        w_loaded = [sem(f"w_loaded{s}") for s in range(2)]
        e_turned = sem("e_turned")
        xgT_ready = sem("xgT_ready")
        e_gu = sem("e_gu")
        e_gelu = sem("e_gelu")
        e_h = sem("e_h")
        e_down = sem("e_down")
        eo_ready = sem("eo_ready")
        scattered = sem("scattered")
        block = ctx.enter_context(nc.Block())

        @block.sync
        def _(sp):
            sp.dma_start(gw[:], gate_w).then_inc(consts_loaded, 16)
            sp.dma_start(wsh[:], w_sh).then_inc(consts_loaded, 16)
            sp.dma_start(wdsh[:], wd_sh.rearrange("(j p) d -> p j d", p=P)).then_inc(consts_loaded, 16)

            def load_x(b):
                sp.dma_start(xr[:, bass.ds(b * T, T), :],
                             src[b].rearrange("(t p) d -> p t d", p=P)).then_inc(x_loaded, 16)

            def shared_step(n, s, half):
                if live(n + 1, B):
                    need(sp, x_loaded, 16 * (n + 1))
                    load_x(n + 1)
                if live(n, B):
                    sp.wait_ge(xn_ready, n + 1)
                    sp.dma_start(xn_dram[n].rearrange("(t p) d -> p t d", p=P), xn[:, s, :, :])\
                        .then_inc(xn_stored[s], 16)
                m = n - 2
                if live(m, B):
                    sp.wait_ge(y_ready, m + 1)
                    sp.dma_start(dst[m].rearrange("(t p) d -> p t d", p=P), y[:, s, :, :])\
                        .then_inc(y_stored[s], 16)

            load_x(0)
            for n in range(4):
                shared_step(n, n % 2, n // 2)
            with sp.Fori(2, B // 2 - 1) as j:
                shared_step(2 * j, 0, j)
                shared_step(2 * j + 1, 1, j)
            for n in range(B - 2, B + 2):
                shared_step(n, n % 2, n // 2)

            def expert_load(n, s, half):
                if live(n, E):
                    need(sp, e_down, n - 1)
                    sp.dma_start(wexp[:, s, :], w_exp[n]).then_inc(w_loaded[s], 16)

            pipeline(sp, expert_load, E, 2, 0)
            sp.wait_ge(scattered, 16 * PAIRS * E)

        @block.gpsimd
        def _(pool):
            nc.gpsimd.memset(ident[:], 0.0).then_inc(pool_setup, 1)
            nc.gpsimd.memset(expo[:], -0.5).then_inc(pool_setup, 1)
            nc.gpsimd.iota(roff_i[:], [[0, 1]], base=0, channel_multiplier=1).then_inc(pool_setup, 1)
            pool.wait_ge(pool_setup, 3)
            nc.gpsimd.affine_select(out=ident[:], in_=ident[:], compare_op=ALU.not_equal, fill=1.0, base=0,
                                    pattern=[[-1, P]], channel_multiplier=1).then_inc(pool_setup, 1)

            def rstd_step(n, s, half):
                if live(n, B):
                    pool.wait_ge(var_ready, n + 1)
                    nc.gpsimd.tensor_tensor(rstd[:, s, :], ve[:, s, :], expo[:], ALU.pow).then_inc(rstd_ready, 1)

            pipeline(pool, rstd_step, B, 2, 0)

            pool.wait_ge(tokens_ready, 1)
            for s in range(2):
                pool.wait_ge(xn_stored[s], 16 * B // 2)
                pool.wait_ge(y_stored[s], 16 * B // 2)

            def indices(e, k):
                return bass.IndirectOffsetOnAxis(ap=tokens[:, e * PAIRS + k:e * PAIRS + k + 1], axis=0)

            def gather(e):
                need(pool, e_turned, e - 1)
                for k in range(PAIRS):
                    nc.gpsimd.indirect_dma_start(xg[:, e % 2, k, :], None, xn_rows, indices(e, k))\
                        .then_inc(gathered[e % 2], 16)

            gather(0)
            gather(1)
            for e in range(E):
                if e + 2 < E:
                    gather(e + 2)
                pool.wait_ge(eo_ready, e + 1)
                need(pool, scattered, 16 * PAIRS * e)
                for k in range(PAIRS):
                    nc.gpsimd.indirect_dma_start(dst_rows, indices(e, k), eo[:, e % 2, k, :], None,
                                                 compute_op=ALU.add).then_inc(scattered, 16)

        @block.scalar
        def _(act):
            def shared_step(n, s, half):
                if not live(n, B):
                    return
                act.wait_ge(turned, n + 1)
                need(act, gu_done, FJ * (n - 1))
                nc.scalar.activation(xnT[:, s, :], ps[:, 0, :], ACT.Copy).then_inc(xnT_ready, 1)
                for j in range(FJ):
                    act.wait_ge(gu_done, FJ * n + j + 1)
                    need(act, h_ready, FJ * (n - 1) + j + 1)
                    nc.scalar.activation(gel[:, j, :], ps[:, 2 + 2 * j, :], ACT.Gelu).then_inc(gelu_done, 1)

            pipeline(act, shared_step, B, 4, 0)
            act.wait_ge(shifted, 1)
            nc.scalar.activation(lg[:, :, :], lg[:, :, :], ACT.Exp).then_inc(exped, 1)

            def expert_step(n, s, half):
                if not live(n, E):
                    return
                act.wait_ge(e_turned, n + 1)
                need(act, e_gu, UNITS * (n - 1))
                nc.scalar.activation(xgT[:, s, :].rearrange("p (a c) -> p a c", a=2), ps[:, 0:2, :], ACT.Copy)\
                    .then_inc(xgT_ready, 1)
                for u in range(UNITS):
                    act.wait_ge(e_gu, UNITS * n + u + 1)
                    if u >= 2 or not isinstance(n, int) or n > 0:
                        act.wait_ge(e_h, UNITS * n + u - 1)
                    elif n == 0:
                        act.wait_ge(h_ready, FJ * B)
                    nc.scalar.activation(gel[:, u % 2, :], ps[:, 2 + 2 * (u % 2), :], ACT.Gelu).then_inc(e_gelu, 1)

            pipeline(act, expert_step, E, 2, 0)

        @block.tensor
        def _(pe):
            pe.wait_ge(pool_setup, 4)
            pe.wait_ge(consts_loaded, 48)

            def shared_step(n, s, half):
                if live(n, B):
                    pe.wait_ge(xn_ready, n + 1)
                    need(pe, xnT_ready, n)
                    for t in range(T):
                        last = nc.tensor.transpose(ps[:, 0, t * P:(t + 1) * P], xn[:, s, t, :], ident[:])
                    last.then_inc(turned, 1)
                m, ms = n - 1, 1 - s
                if live(m, B):
                    pe.wait_ge(h_ready, FJ * (m + 1))
                    need(pe, y_ready, m - 1)
                    for t in range(T):
                        for j in range(FJ):
                            last = nc.tensor.matmul(ps[:, 6 + ms, t * D:(t + 1) * D],
                                                    hT[:, ms, j, t * P:(t + 1) * P], wdsh[:, j, :],
                                                    start=(j == 0), stop=(j == FJ - 1))
                    last.then_inc(down_done, 1)
                if live(n, B):
                    pe.wait_ge(xnT_ready, n + 1)
                    need(pe, logits_read, n)
                    for t in range(T):
                        last = nc.tensor.matmul(ps[:, 1, t * E:(t + 1) * E], xnT[:, s, t * P:(t + 1) * P], gw[:],
                                                start=True, stop=True)
                    last.then_inc(logits_done, 1)
                    for j in range(FJ):
                        need(pe, h_ready, FJ * (n - 1) + j + 1)
                        for half_w in range(2):
                            last = nc.tensor.matmul(ps[:, 2 + 2 * j + half_w, :],
                                                    wsh[:, half_w * FE + j * P:half_w * FE + (j + 1) * P],
                                                    xnT[:, s, :], start=True, stop=True)
                        last.then_inc(gu_done, 1)

            pipeline(pe, shared_step, B, 4, 2)

            pe.wait_ge(probs_ready, 1)
            for g in range(2):
                for t in range(T):
                    last = nc.tensor.transpose(ps[:, g, t * P:(t + 1) * P], pr[:, g, t, :], ident[:])
            last.then_inc(rows_turned, 1)
            pe.wait_ge(top_ready, 1)
            for g in range(2):
                nc.tensor.transpose(ps[:, 2, g * P:(g + 1) * P],
                                    topd[:, g, :, :].rearrange("p a c -> p (a c)"), ident[:])
                last = nc.tensor.transpose(ps[:, 3, g * P:(g + 1) * P],
                                           posd[:, g, :, :].rearrange("p a c -> p (a c)"), ident[:])
            last.then_inc(top_turned, 1)

            def expert_step(n, s, half):
                if live(n, E):
                    pe.wait_ge(gathered[s], 16 * PAIRS * (half + 1))
                    need(pe, xgT_ready, n)
                    if isinstance(n, int) and n == 0:
                        pe.wait_ge(tokens_ready, 1)
                    for k in range(PAIRS):
                        last = nc.tensor.transpose(ps[:, k // 4, (k % 4) * P:(k % 4 + 1) * P], xg[:, s, k, :],
                                                   ident[:])
                    last.then_inc(e_turned, 1)
                m, ms = n - 1, 1 - s
                if live(m, E):
                    pe.wait_ge(e_h, UNITS * (m + 1))
                    need(pe, eo_ready, m)
                    for k in range(PAIRS):
                        for j in range(FJ):
                            last = nc.tensor.matmul(ps[:, 6 + k // 4, (k % 4) * D:(k % 4 + 1) * D],
                                                    hT[:, ms, j, k * P:(k + 1) * P],
                                                    wexp[:, ms, 2 * FE + j * D:2 * FE + (j + 1) * D],
                                                    start=(j == 0), stop=(j == FJ - 1))
                    last.then_inc(e_down, 1)
                if live(n, E):
                    pe.wait_ge(xgT_ready, n + 1)
                    pe.wait_ge(w_loaded[s], 16 * (half + 1))
                    for u in range(UNITS):
                        a, j = u // FJ, u % FJ
                        if u >= 2 or not isinstance(n, int) or n > 0:
                            pe.wait_ge(e_h, UNITS * n + u - 1)
                        for half_w in range(2):
                            last = nc.tensor.matmul(ps[:, 2 + 2 * (u % 2) + half_w, :],
                                                    wexp[:, s, half_w * FE + j * P:half_w * FE + (j + 1) * P],
                                                    xgT[:, s, a * 512:(a + 1) * 512], start=True, stop=True)
                        last.then_inc(e_gu, 1)

            pipeline(pe, expert_step, E, 2, 2)

        @block.vector
        def _(dve):
            chain = Count(vchain, 2 * T)

            def shared_step(n, s, half):
                if live(n, B):
                    chain.turn(n)
                    dve.wait_ge(x_loaded, 16 * (n + 1))
                    for t in range(T):
                        chain.add(nc.vector.bn_stats(stats[:, s, t, :], xr[:, bass.ds(n * T + t, 1), :]
                                                     .rearrange("p a d -> p (a d)")))
                    chain.wait_apart(dve)
                    for t in range(T):
                        chain.add(nc.vector.bn_aggr(mv[:, s, t, :], stats[:, s, t, :]))
                    chain.wait(dve)
                    nc.vector.tensor_scalar(ve[:, s, :], mv[:, s, :, 1], EPS, None, ALU.add).then_inc(var_ready, 1)
                    dve.wait_ge(rstd_ready, n + 1)
                    need(dve, turned, n - 1)
                    need(dve, xn_stored[s], 16 * half)
                    for t in range(T):
                        last = nc.vector.tensor_scalar(xn[:, s, t, :], xr[:, bass.ds(n * T + t, 1), :]
                                                       .rearrange("p a d -> p (a d)"),
                                                       mv[:, s, t, 0:1], rstd[:, s, t:t + 1],
                                                       ALU.subtract, ALU.mult)
                    last.then_inc(xn_ready, 1)
                    chain.end("normalisation")
                m, ms = n - 1, 1 - s
                if live(m, B):
                    dve.wait_ge(logits_done, m + 1)
                    nc.vector.tensor_copy(lg[:, bass.ds(m * T, T), :],
                                          ps[:, 1, 0:T * E].rearrange("p (t e) -> p t e", e=E))\
                        .then_inc(logits_read, 1)
                    need(dve, down_done, m - 1)
                    for j in range(FJ):
                        dve.wait_ge(gelu_done, FJ * m + j + 1)
                        nc.vector.tensor_tensor(hT[:, ms, j, 0:512], gel[:, j, :], ps[:, 3 + 2 * j, :], ALU.mult)\
                            .then_inc(h_ready, 1)
                m, ms = n - 2, s
                if live(m, B):
                    dve.wait_ge(down_done, m + 1)
                    if not isinstance(half, int) or half >= 2:
                        dve.wait_ge(y_stored[ms], 16 * (half - 1))
                    nc.vector.tensor_tensor(y[:, ms, :, :], ps[:, 6 + ms, :].rearrange("p (t d) -> p t d", d=D),
                                            xr[:, bass.ds(m * T, T), :], ALU.add).then_inc(y_ready, 1)

            pipeline(dve, shared_step, B, 4, 2)

            at = [2 * T * B]

            def link(ins):
                ins.then_inc(vchain, 1)
                at[0] += 1
                dve.wait_ge(vchain, at[0])

            dve.wait_ge(logits_read, B)
            link(nc.vector.tensor_reduce(red[:], lg[:, :, :], AX.X, ALU.max))
            nc.vector.tensor_tensor(lg[:, :, :], lg[:, :, :], red[:].unsqueeze(2).to_broadcast([P, B * T, E]),
                                    ALU.subtract).then_inc(shifted, 1)
            dve.wait_ge(exped, 1)
            link(nc.vector.tensor_reduce(red[:], lg[:, :, :], AX.X, ALU.add))
            link(nc.vector.reciprocal(red[:], red[:]))
            for g in range(2):
                half_b = slice(g * B // 2 * T, (g + 1) * B // 2 * T)
                last = nc.vector.tensor_tensor(
                    pr[:, g, :, :].rearrange("p t (b e) -> p b t e", e=E),
                    lg[:, half_b, :].rearrange("p (b t) e -> p b t e", t=T),
                    red[:, half_b].rearrange("p (b t) -> p b t", t=T).unsqueeze(3).to_broadcast([P, B // 2, T, E]),
                    ALU.mult)
            last.then_inc(probs_ready, 1)
            dve.wait_ge(pool_setup, 4)
            link(nc.vector.tensor_scalar(roff_i[:], roff_i[:], int(math.log2(E)), int(math.log2(N)),
                                         ALU.logical_shift_right, ALU.logical_shift_left))
            for g in range(2):
                link(nc.vector.tensor_scalar(roff[:, g:g + 1], roff_i[:], float(g * B // 2 * N), None, ALU.add))
            dve.wait_ge(rows_turned, 1)
            link(nc.vector.tensor_copy(rows[:], ps[:, 0:2, :]))
            for r in range(CAP // 8):
                at8 = slice(8 * r, 8 * r + 8)
                for g in range(2):
                    last = nc.vector.max(top[:, g, at8], rows[:, g, :])
                    last.then_inc(vchain, 1)
                    at[0] += 1
                for g in range(2):
                    dve.wait_ge(vchain, at[0] - 1 + g)
                    nc.vector.max_index(pos[:, g, at8], top[:, g, at8], rows[:, g, :]).then_inc(vchain, 1)
                at[0] += 2
                if r < CAP // 8 - 1:
                    for g in range(2):
                        dve.wait_ge(vchain, at[0] - 1 + g)
                        nc.vector.match_replace(rows[:, g, :], top[:, g, at8], rows[:, g, :], -1.0)\
                            .then_inc(vchain, 1)
                    at[0] += 2
                dve.wait_ge(vchain, at[0])
            for g in range(2):
                for a in range(2):
                    nc.vector.tensor_copy(topd[:, g, a, :], top[:, g, :])
                    last = nc.vector.tensor_scalar(posd[:, g, a, :], pos[:, g, :], roff[:, g:g + 1], None, ALU.add)
            last.then_inc(top_ready, 1)
            dve.wait_ge(top_turned, 1)
            tok_v = tokens[:].rearrange("p (e k) -> p e k", k=PAIRS)
            for g in range(2):
                for a in range(2):
                    rows_a = slice(a * CAP, (a + 1) * CAP)
                    for bank, out in ((2, weight), (3, tok_v)):
                        v = ps[rows_a, bank, g * P:(g + 1) * P].rearrange("p (k a e) -> p a e k", a=2, e=E)
                        last = nc.vector.tensor_copy(out[rows_a, :, g * 4:(g + 1) * 4], v[:, a, :, :])
                        link(last)
            nc.vector.tensor_copy(red[:, 0:1], red[:, 1:2]).then_inc(tokens_ready, 1)

            def expert_step(n, s, half):
                m, ms = n - 1, 1 - s
                if live(m, E):
                    dve.wait_ge(e_down, m + 1)
                    if not isinstance(m, int) or m >= 2:
                        dve.wait_ge(scattered, 16 * PAIRS * (m - 1))
                    for c in range(2):
                        last = nc.vector.tensor_tensor(
                            eo[:, ms, 4 * c:4 * c + 4, :], ps[:, 6 + c, :].rearrange("p (k d) -> p k d", d=D),
                            weight[:, bass.ds(m, 1), 4 * c:4 * c + 4].rearrange("p a k -> p (a k)")
                            .unsqueeze(2).to_broadcast([P, 4, D]), ALU.mult)
                    last.then_inc(eo_ready, 1)
                if live(n, E):
                    need(dve, e_down, n - 1)
                    for u in range(UNITS):
                        a, j = u // FJ, u % FJ
                        dve.wait_ge(e_gelu, UNITS * n + u + 1)
                        nc.vector.tensor_tensor(hT[:, s, j, a * 512:(a + 1) * 512], gel[:, u % 2, :],
                                                ps[:, 3 + 2 * (u % 2), :], ALU.mult).then_inc(e_h, 1)

            pipeline(dve, expert_step, E, 4, 2)


class Turn:

    def __init__(self, uses, filled0, read0):
        self.k = {label: k for k, (label, _) in enumerate(uses)}
        self.uses, self.filled0, self.read0 = uses, filled0, read0

    def slot(self, label):
        return self.k[label] % 3

    def filled(self, label):
        return self.filled0 + self.k[label] + 1

    def read(self, label):
        k = self.k[label]
        reader = self.uses[k][1]
        return reader, self.read0[reader] + sum(r == reader for _, r in self.uses[:k + 1])


def attention_block(nc, tag, src, dst, turns, w_qkv, w_o, causal_tiles, bias=None, gates=None, keep=None):
    whole = causal_tiles
    seen = (lambda t: range(t + 1)) if whole else (lambda t: range(t, t + 1))
    askers = (lambda k: range(k, T)) if whole else (lambda k: range(k, k + 1))
    max_groups = []
    for t in range(T):
        n_keys = P * len(seen(t))
        pitch = {128: 128, 256: 256}.get(n_keys, 512)
        heads = 1024 // pitch
        max_groups += [(t, h, heads, n_keys, pitch) for h in range(0, H, heads)]
    exp_groups, pv_after = [], []
    where = {}
    if whole:
        for s in range(H // 4):
            heads = range(4 * s, 4 * s + 4)
            exp_groups.append([(h, 2, 512 * (h % 2) + 256 * (h % 4 // 2)) for h in heads])
            for h in heads:
                exp_groups.append([(h, 0, 0), (h, 1, 512), (h, 3, 896)])
                pv_after.append((len(exp_groups) - 1, [(h, range(T))]))
    else:
        for t in range(T):
            for h0 in range(0, H, 8):
                exp_groups.append([(h, t, 512 * (h % 2) + P * ((h - h0) // 2)) for h in range(h0, h0 + 8)])
                pv_after.append((len(exp_groups) - 1, [(h, range(t, t + 1)) for h in range(h0, h0 + 8)]))
    for g, parts in enumerate(exp_groups):
        for h, k, col in parts:
            where[h, k] = (g, col)
    NG, NM, NPV = len(exp_groups), len(max_groups), len(pv_after)
    RING = 10 if whole else NG
    XN_AT, QKV_AT = (4, 9) if whole else (1, 4)

    def uses(with_next):
        out = [("k0", "act"), ("k1", "dve"), ("q0", "act"), ("q1", "dve")]
        out += [(f"max{g}", "dve") for g in range(NM)]
        out += [("r0", "act"), ("r1", "dve")]
        for g in range(NG):
            out.append((f"exp{g}", "act"))
            if with_next and g == XN_AT:
                out.append(("xnT", "dve"))
            if with_next and g == QKV_AT:
                out += [("qkv0", "act"), ("qkv1", "act")]
        return out + [("oT", "act"), ("proj", "dve")]

    first_uses = [("xnT", "dve"), ("qkv0", "act"), ("qkv1", "act")]
    loop_uses = uses(True)
    per_turn = {r: sum(x == r for _, x in loop_uses) for r in ("act", "dve")}
    read_first = {"act": 2, "dve": 1}

    def turn_at(i, with_next):
        return Turn(uses(with_next), len(first_uses) + len(loop_uses) * i,
                    {r: read_first[r] + per_turn[r] * i for r in per_turn})

    prologue = Turn(first_uses, 0, {"act": 0, "dve": 0})

    def run(eng, first, main):
        first()
        with eng.Fori(0, turns - 1) as i:
            main(i, True)
        main(turns - 1, False)

    with ExitStack() as ctx:
        def sb(name, shape, dt=F32):
            return ctx.enter_context(nc.sbuf_tensor(f"{tag}_{name}", shape, dt))

        def sem(name):
            return ctx.enter_context(nc.semaphore(f"{tag}_{name}"))

        ps = ctx.enter_context(nc.psum_tensor(f"{tag}_ps", [P, 8, 512], F32))
        ident = sb("ident", [P, P])
        identb = sb("identb", [P, P], BF16)
        mask_q = sb("mask_q", [P, P], BF16)
        mask_k = sb("mask_k", [P, P], BF16)
        wqkv = sb("wqkv", [P, 3 * D])
        wo = sb("wo", [P, D])
        xr = sb("xr", [P, turns * T, D])
        stats = sb("stats", [P, T, 6])
        mv = sb("mv", [P, T, 2])
        ve = sb("ve", [P, T])
        expo = sb("expo", [P, T])
        rstd = sb("rstd", [P, T])
        xn = sb("xn", [P, T, D])
        xnT = sb("xnT", [P, T * P])
        qkv = sb("qkv", [P, T, 3 * D])
        rest = sb("rest", [P, 2, T, D])
        stk = sb("stk", [P, 2, T * H, SLOT], BF16)
        qT = sb("qT", [P, H // 2, T * P], BF16)
        kT = sb("kT", [P, H // 2, T * P], BF16)
        v1 = sb("v1", [P, T, H, DH + 1])
        mx = sb("mx", [P, T * H])
        mrest = sb("mrest", [P, 2, T * H])
        pT = sb("pT", [P, RING, 1024])
        osum = sb("osum", [P, 2, T * H // 2])
        on = sb("on", [P, T, D])
        oT = sb("oT", [P, T * P])
        y = sb("y", [P, T, D])
        consts_loaded = sem("consts_loaded")
        pool_setup = sem("pool_setup")
        setup_chain = sem("setup_chain")
        setup_act = sem("setup_act")
        setup_done = sem("setup_done")
        x_loaded = sem("x_loaded")
        vchain = sem("vchain")
        max_chain = sem("max_chain")
        var_ready = sem("var_ready")
        rstd_ready = sem("rstd_ready")
        xn_ready = sem("xn_ready")
        psum_filled = sem("psum_filled")
        psum_read = {"act": sem("psum_read_by_scalar"), "dve": sem("psum_read_by_vector")}
        v_copied = sem("v_copied")
        pool_chain = sem("pool_chain")
        rotated = sem("rotated")
        split_done = sem("split_done")
        stack_ready = sem("stack_ready")
        neg_max_ready = sem("neg_max_ready")
        pv_done = sem("pv_done")
        o_ready = sem("o_ready")
        y_free = sem("y_free")
        kept = sem("kept")
        y_stored = sem("y_stored")
        if whole:
            lin = sb("lin", [P, 3, H])
            gts = sb("gts", [P, 3, H])
            pos_i = sb("pos_i", [P, T], I32)
            posf = sb("posf", [P, T])
            freq = sb("freq", [P, DH // 2])
            th0 = sb("th0", [P, T, DH // 2])
            th = sb("th", [P, T, H, DH // 2])
            turnsf = sb("turnsf", [P, T * H * DH // 2])
            ang = sb("ang", [P, T * H * DH // 2])
            cs = sb("cs", [P, 2, T, 2, H * DH // 2])
            rot = sb("rot", [P, T, 2 * D])
            tmp = sb("tmp", [P, 4, T, D])
            dec = sb("dec", [P, T * H])
            decr = sb("decr", [P, 2, T * H])
        else:
            brow = sb("brow", [1, 4 * D])
            ones1 = sb("ones1", [1, P])
        block = ctx.enter_context(nc.Block())

        def slot(k):
            return ps[:, 2 * k:2 * k + 2, :].rearrange("p a c -> p (a c)")

        def wait_read(eng, turn, label, first_turn=None):
            reader, value = turn.read(label)
            if first_turn is None:
                eng.wait_ge(psum_read[reader], value)
            else:
                need_apart(eng, psum_read[reader], value, first_turn.read(label)[1])

        @block.sync
        def _(sp):
            sp.dma_start(wqkv[:], w_qkv).then_inc(consts_loaded, 16)
            sp.dma_start(wo[:], w_o).then_inc(consts_loaded, 16)
            if whole:
                for c in range(3):
                    sp.dma_start(lin[:, c, :], gates[c].unsqueeze(0).to_broadcast([P, H]))\
                        .then_inc(consts_loaded, 16)
            else:
                sp.dma_start(brow[:], bias).then_inc(consts_loaded, 16)

            def load(i):
                sp.dma_start(xr[:, bass.ds(i * T, T), :], src(i)).then_inc(x_loaded, 16)

            load(0)
            if keep:
                sp.dma_start(*keep).then_inc(kept, 16)
            sp.sem_inc(y_free, 1)

            def main(i, with_next):
                if with_next:
                    sp.wait_ge(x_loaded, 16 * (i + 1))
                    load(i + 1)
                wait_read(sp, turn_at(i, with_next), "proj")
                sp.dma_start(dst(i), y[:, :, :]).then_inc(y_stored, 16)
                sp.wait_ge(y_stored, 16 * (i + 1))
                sp.sem_inc(y_free, 1)

            run(sp, lambda: None, main)
            if keep:
                sp.wait_ge(kept, 16)

        @block.gpsimd
        def _(pool):
            nc.gpsimd.memset(ident[:], 0.0).then_inc(pool_setup, 1)
            nc.gpsimd.memset(mask_q[:], 0.0).then_inc(pool_setup, 1)
            nc.gpsimd.memset(mask_k[:], 0.0).then_inc(pool_setup, 1)
            nc.gpsimd.memset(expo[:], -0.5).then_inc(pool_setup, 1)
            nc.gpsimd.memset(v1[:, :, :, DH:DH + 1], 1.0).then_inc(pool_setup, 1)
            nc.gpsimd.memset(stk[:], 0.0).then_inc(pool_setup, 1)
            pool.wait_ge(pool_setup, 6)
            nc.gpsimd.affine_select(out=ident[:], in_=ident[:], compare_op=ALU.not_equal, fill=1.0, base=0,
                                    pattern=[[-1, P]], channel_multiplier=1).then_inc(pool_setup, 1)
            nc.gpsimd.affine_select(out=mask_q[:], in_=mask_q[:], compare_op=ALU.is_ge, fill=MASKED, base=0,
                                    pattern=[[-1, P]], channel_multiplier=1).then_inc(pool_setup, 1)
            nc.gpsimd.affine_select(out=mask_k[:], in_=mask_k[:], compare_op=ALU.is_ge, fill=MASKED, base=0,
                                    pattern=[[1, P]], channel_multiplier=-1).then_inc(pool_setup, 1)
            nc.gpsimd.memset(stk[:, 0, :, DECAY_AT:DECAY_AT + 3], 1.0).then_inc(pool_setup, 1)
            nc.gpsimd.memset(stk[:, 1, :, MAX_AT:MAX_AT + 3], 1.0).then_inc(pool_setup, 1)
            pool.wait_ge(pool_setup, 11)
            nc.gpsimd.tensor_copy(identb[:], ident[:]).then_inc(pool_setup, 1)
            if whole:
                nc.gpsimd.iota(pos_i[:], [[P, T]], base=0, channel_multiplier=1).then_inc(pool_setup, 1)
                for f in range(DH // 2):
                    value = float(np.float32(math.pi) ** np.float32(1.0 - 2 * f / DH))
                    nc.gpsimd.memset(freq[:, f:f + 1], value).then_inc(pool_setup, 1)
            else:
                nc.gpsimd.memset(ones1[:], 1.0).then_inc(pool_setup, 1)
                pool.wait_ge(pool_setup, 13)
                nc.gpsimd.memset(mask_q[SEG_A:P, 0:SEG_A], MASKED).then_inc(pool_setup, 1)
                pool.wait_ge(pool_setup, 14)
                nc.gpsimd.memset(mask_k[0:SEG_A, SEG_A:P], MASKED).then_inc(pool_setup, 1)
            chain = Count(pool_chain, 4)

            def prepare(turn, first_turn, j):
                pool.wait_ge(var_ready, j + 1)
                nc.gpsimd.tensor_tensor(rstd[:], ve[:], expo[:], ALU.pow).then_inc(rstd_ready, 1)
                if not whole:
                    return
                if isinstance(j, int) and j == 0:
                    pool.wait_ge(setup_done, 1)
                chain.turn(j)
                wait_read(pool, turn, "qkv1")
                even, odd = (qkv[:, :, bass.ds(o, D, step=2)] for o in range(2))
                cos, sin = (cs[:, c, :, :, :].rearrange("p t a x -> p t (a x)") for c in range(2))
                for c, (a, b) in enumerate(((even, cos), (odd, sin), (even, sin), (odd, cos))):
                    chain.add(nc.gpsimd.tensor_tensor(tmp[:, c, :, :], a, b, ALU.mult))
                chain.wait(pool)
                need(pool, split_done, j)
                nc.gpsimd.tensor_tensor(rot[:, :, bass.ds(0, D, step=2)], tmp[:, 0, :, :], tmp[:, 1, :, :],
                                        ALU.subtract)
                nc.gpsimd.tensor_tensor(rot[:, :, bass.ds(1, D, step=2)], tmp[:, 2, :, :], tmp[:, 3, :, :],
                                        ALU.add).then_inc(rotated, 1)
                chain.end("rotation")

            def main(i, with_next):
                turn, turn0 = turn_at(i, with_next), turn_at(0, with_next)
                need_apart(pool, psum_filled, turn.filled("k0"), turn0.filled("k0"))
                for t in range(T):
                    last = nc.gpsimd.tensor_copy(v1[:, t, :, 0:DH],
                                                 qkv[:, t, 2 * D:3 * D].rearrange("p (h e) -> p h e", e=DH))
                last.then_inc(v_copied, 1)
                if with_next:
                    prepare(turn, turn0, i + 1)

            run(pool, lambda: prepare(prologue, prologue, 0), main)

        @block.scalar
        def _(act):
            if whole:
                act.wait_ge(consts_loaded, 80)
                nc.scalar.activation(gts[:, :, :], lin[:, :, :], ACT.Exp, scale=-1.0).then_inc(setup_act, 1)
                for c in range(2):
                    act.wait_ge(setup_chain, ANGLE_STEPS[c])
                    nc.scalar.activation(cs[:, c, :, 0, :], ang[:].rearrange("p (t x) -> p t x", t=T), ACT.Sin)
                    nc.scalar.activation(cs[:, c, :, 1, :], ang[:].rearrange("p (t x) -> p t x", t=T), ACT.Sin)\
                        .then_inc(setup_act, 1)

            def prepare(turn, j):
                for c in range(2):
                    act.wait_ge(psum_filled, turn.filled(f"qkv{c}"))
                    if c == 0:
                        need(act, v_copied, j)
                        need(act, split_done, j)
                    nc.scalar.activation(qkv[:, 2 * c:2 * c + 2, :],
                                         slot(turn.slot(f"qkv{c}")).rearrange("p (a x) -> p a x", a=2)[:, :, 0:3 * D],
                                         ACT.Copy).then_inc(psum_read["act"], 1)

            def stack(j):
                act.wait_ge(split_done, j + 1)
                for c, copies in ((0, ((0, 1), (0, 2), (4, 3))), (1, ((0, 3), (0, 5), (4, 1)))):
                    for a, b in copies:
                        last = nc.scalar.activation(stk[:, c, :, b * DH:(b + 1) * DH],
                                                    stk[:, c, :, a * DH:(a + 1) * DH], ACT.Copy)
                last.then_inc(stack_ready, 1)

            def turned(turn, label, out, c):
                act.wait_ge(psum_filled, turn.filled(label))
                nc.scalar.activation(out[:, 4 * c:4 * c + 4, :],
                                     slot(turn.slot(label)).bitcast(BF16).rearrange("p (a x) -> p a x", a=4),
                                     ACT.Copy).then_inc(psum_read["act"], 1)

            def main(i, with_next):
                turn = turn_at(i, with_next)
                turned(turn, "k0", kT, 0)
                turned(turn, "q0", qT, 0)
                turned(turn, "r0", qT, 0)
                for g in range(NG):
                    act.wait_ge(psum_filled, turn.filled(f"exp{g}"))
                    if whole and g // 5 >= 2:
                        act.wait_ge(pv_done, NPV * i + 4 * (g // 5 - 1))
                    nc.scalar.activation(pT[:, g % RING, :], slot(turn.slot(f"exp{g}")), ACT.Exp, scale=SCALE)\
                        .then_inc(psum_read["act"], 1)
                    if with_next and g == QKV_AT:
                        prepare(turn, i + 1)
                if with_next:
                    stack(i + 1)
                act.wait_ge(psum_filled, turn.filled("oT"))
                nc.scalar.activation(oT[:], slot(turn.slot("oT"))[:, 0:T * P], ACT.Copy)\
                    .then_inc(psum_read["act"], 1)

            def first():
                prepare(prologue, 0)
                stack(0)

            run(act, first, main)

        @block.tensor
        def _(pe):
            pe.wait_ge(pool_setup, POOL_SETUP[whole])
            pe.wait_ge(consts_loaded, 80 if whole else 48)

            def open_slot(turn, label, apart=None):
                k = turn.k[label]
                if k >= 3:
                    wait_read(pe, turn, turn.uses[k - 3][0], apart)
                elif k == 0 and turn is not prologue:
                    for r in psum_read:
                        pe.wait_ge(psum_read[r], turn.read0[r])
                return slot(turn.slot(label))

            def turn_x(turn, j):
                out = open_slot(turn, "xnT")
                pe.wait_ge(xn_ready, j + 1)
                for t in range(T):
                    last = nc.tensor.transpose(out[:, t * P:(t + 1) * P], xn[:, t, :], ident[:])
                last.then_inc(psum_filled, 1)

            def project(turn):
                for c in range(2):
                    out = open_slot(turn, f"qkv{c}")
                    if c == 0:
                        wait_read(pe, turn, "xnT")
                    for a in range(2):
                        t = 2 * c + a
                        part = out[:, 512 * a:512 * a + 3 * D]
                        last = nc.tensor.matmul(part, xnT[:, t * P:(t + 1) * P], wqkv[:], start=True, stop=whole)
                        if not whole:
                            last = nc.tensor.matmul(part, ones1[:], brow[0:1, 0:3 * D], start=False, stop=True)
                    last.then_inc(psum_filled, 1)

            def stacks_turned(turn, label, which, c):
                out = open_slot(turn, label).bitcast(BF16)
                for pair in range(4 * c, 4 * c + 4):
                    for t in range(T):
                        last = nc.tensor.transpose(
                            out[:, ((pair % 4) * T + t) * P:((pair % 4) * T + t + 1) * P],
                            stk[:, which, t * H + 2 * pair:t * H + 2 * pair + 2, :].rearrange("p a s -> p (a s)"),
                            identb[:])
                last.then_inc(psum_filled, 1)

            def side(x, h, rows, c0, n):
                r0 = SLOT * (h % 2)
                return x[r0:r0 + rows, h // 2, c0:c0 + n]

            def main(i, with_next):
                turn, turn0 = turn_at(i, with_next), turn_at(0, with_next)
                pe.wait_ge(stack_ready, i + 1)
                for c in range(2):
                    stacks_turned(turn, f"k{c}", 1, c)
                for c in range(2):
                    stacks_turned(turn, f"q{c}", 0, c)
                wait_read(pe, turn, "q0")
                wait_read(pe, turn, "q1")
                for g, (t, h0, heads, n_keys, pitch) in enumerate(max_groups):
                    out = open_slot(turn, f"max{g}", turn0)
                    for n in range(heads):
                        h, k0 = h0 + n, seen(t)[0] * P
                        col = 512 * (n % 2) + pitch * (n // 2)
                        nc.tensor.matmul(out[:, col:col + n_keys], side(qT, h, ROWS1, t * P, P),
                                         side(kT, h, ROWS1, k0, n_keys), start=True, stop=False)
                        diag = col + n_keys - P
                        last = nc.tensor.matmul(out[:, diag:diag + P], identb[:], mask_q[:], start=False, stop=True)
                    last.then_inc(psum_filled, 1)
                pe.wait_ge(neg_max_ready, i + 1)
                for c in range(2):
                    stacks_turned(turn, f"r{c}", 0, c)
                wait_read(pe, turn, "r0")
                wait_read(pe, turn, "r1", turn0)
                pv = list(pv_after)

                def weighted_sums(upto):
                    while pv and pv[0][0] <= upto:
                        g, work = pv.pop(0)
                        wait_read(pe, turn, f"exp{g}")
                        if g == pv_after[0][0]:
                            pe.wait_ge(v_copied, i + 1)
                        for h, tiles in work:
                            for t in tiles:
                                out = ps[:, 6 + t // 2, ((t % 2) * H + h) * (DH + 1):((t % 2) * H + h + 1) * (DH + 1)]
                                for k in seen(t):
                                    gk, col = where[h, k]
                                    col += (t - askers(k)[0]) * P
                                    last = nc.tensor.matmul(out, pT[:, gk % RING, col:col + P], v1[:, k, h, :],
                                                            start=(k == seen(t)[0]), stop=(k == t))
                        last.then_inc(pv_done, 1)

                for g, parts in enumerate(exp_groups):
                    out = open_slot(turn, f"exp{g}", turn0)
                    for h, k, col in parts:
                        n_q = len(askers(k)) * P
                        nc.tensor.matmul(out[:, col:col + n_q], side(kT, h, ROWS2, k * P, P),
                                         side(qT, h, ROWS2, k * P, n_q), start=True, stop=False)
                        last = nc.tensor.matmul(out[:, col:col + P], identb[:], mask_k[:], start=False, stop=True)
                    last.then_inc(psum_filled, 1)
                    if with_next and g == XN_AT:
                        turn_x(turn, i + 1)
                    if with_next and g == QKV_AT:
                        project(turn)
                    weighted_sums(g - 2)
                weighted_sums(NG)
                out = open_slot(turn, "oT")
                pe.wait_ge(o_ready, i + 1)
                for t in range(T):
                    last = nc.tensor.transpose(out[:, t * P:(t + 1) * P], on[:, t, :], ident[:])
                last.then_inc(psum_filled, 1)
                out = open_slot(turn, "proj")
                wait_read(pe, turn, "oT")
                for t in range(T):
                    part = out[:, t * D:(t + 1) * D]
                    last = nc.tensor.matmul(part, oT[:, t * P:(t + 1) * P], wo[:], start=True, stop=whole)
                    if not whole:
                        last = nc.tensor.matmul(part, ones1[:], brow[0:1, 3 * D:4 * D], start=False, stop=True)
                last.then_inc(psum_filled, 1)

            def first():
                turn_x(prologue, 0)
                project(prologue)

            run(pe, first, main)

        @block.vector
        def _(dve):
            if whole:
                at = [0]

                def link(ins):
                    ins.then_inc(setup_chain, 1)
                    at[0] += 1
                    dve.wait_ge(setup_chain, at[0])

                dve.wait_ge(setup_act, 1)
                link(nc.vector.tensor_scalar(gts[:, 1:3, :], gts[:, 1:3, :], 1.0, None, ALU.add))
                link(nc.vector.reciprocal(gts[:, 1:3, :], gts[:, 1:3, :]))
                dve.wait_ge(pool_setup, POOL_SETUP[whole])
                link(nc.vector.tensor_copy(posf[:], pos_i[:]))
                link(nc.vector.tensor_tensor(gts[:, 0, :], gts[:, 0, :], gts[:, 2, :], ALU.mult))
                dec_v = dec[:].rearrange("p (t h) -> p t h", h=H)
                link(nc.vector.tensor_tensor(dec_v, posf[:].unsqueeze(2).to_broadcast([P, T, H]),
                                             gts[:, 0:1, :].to_broadcast([P, T, H]), ALU.mult))
                link(nc.vector.tensor_scalar(dec[:], dec[:], 1.0 / SCALE, None, ALU.mult))
                k_dec = [stk[:, 1, :, DECAY_AT + c] for c in range(3)]
                link(nc.vector.tensor_copy(k_dec[0], dec[:]))
                link(nc.vector.tensor_tensor(decr[:, 0, :], dec[:], k_dec[0], ALU.subtract))
                link(nc.vector.tensor_copy(k_dec[1], decr[:, 0, :]))
                link(nc.vector.tensor_tensor(k_dec[2], decr[:, 0, :], k_dec[1], ALU.subtract))
                link(nc.vector.tensor_tensor(th0[:, :, :], posf[:].unsqueeze(2).to_broadcast([P, T, DH // 2]),
                                             freq[:].unsqueeze(1).to_broadcast([P, T, DH // 2]), ALU.mult))
                for t in range(T):
                    link(nc.vector.tensor_tensor(th[:, t, :, :], th0[:, t:t + 1, :].to_broadcast([P, H, DH // 2]),
                                                 gts[:, 1, :].unsqueeze(2).to_broadcast([P, H, DH // 2]), ALU.mult))
                flat = th[:, :, :, :].rearrange("p t h f -> p (t h f)")
                turn_hi = 6.28125
                turn_lo = float(np.float32(2 * math.pi - turn_hi))
                for c, quarter in enumerate((0.25, 0.0)):
                    if c:
                        dve.wait_ge(setup_act, 2)
                    link(nc.vector.tensor_scalar(turnsf[:], flat, 1.0 / (2 * math.pi), quarter, ALU.mult, ALU.add))
                    link(nc.vector.tensor_scalar(turnsf[:], turnsf[:], 12582912.0, None, ALU.add))
                    link(nc.vector.tensor_scalar(turnsf[:], turnsf[:], 12582912.0, None, ALU.subtract))
                    link(nc.vector.scalar_tensor_tensor(ang[:], turnsf[:], -turn_hi, flat, ALU.mult, ALU.add))
                    link(nc.vector.scalar_tensor_tensor(ang[:], turnsf[:], -turn_lo, ang[:], ALU.mult, ALU.add))
                    link(nc.vector.tensor_scalar(ang[:], ang[:], quarter * 2 * math.pi, None, ALU.add))
                    link(nc.vector.tensor_scalar(ang[:], ang[:], 3.1415925, -3.1415925, ALU.min, ALU.max))
                    assert at[0] == ANGLE_STEPS[c], at
                dve.wait_ge(setup_act, 3)
                nc.vector.tensor_copy(decr[:, 1, 0:1], decr[:, 0, 0:1]).then_inc(setup_done, 1)
            else:
                dve.wait_ge(pool_setup, POOL_SETUP[whole])
            chain = Count(vchain, 2 * T + 6)
            main_chain = Count(max_chain, 5)

            def normalise(j):
                chain.turn(j)
                dve.wait_ge(x_loaded, 16 * (j + 1))
                for t in range(T):
                    chain.add(nc.vector.bn_stats(stats[:, t, :], xr[:, bass.ds(j * T + t, 1), :]
                                                 .rearrange("p a d -> p (a d)")))
                chain.wait_apart(dve)
                for t in range(T):
                    chain.add(nc.vector.bn_aggr(mv[:, t, :], stats[:, t, :]))
                chain.wait(dve)
                nc.vector.tensor_scalar(ve[:], mv[:, :, 1], EPS, None, ALU.add).then_inc(var_ready, 1)
                dve.wait_ge(rstd_ready, j + 1)
                for t in range(T):
                    last = nc.vector.tensor_scalar(xn[:, t, :], xr[:, bass.ds(j * T + t, 1), :]
                                                   .rearrange("p a d -> p (a d)"), mv[:, t, 0:1], rstd[:, t:t + 1],
                                                   ALU.subtract, ALU.mult)
                last.then_inc(xn_ready, 1)

            def evacuate_x(turn):
                dve.wait_ge(psum_filled, turn.filled("xnT"))
                nc.vector.tensor_copy(xnT[:], slot(turn.slot("xnT"))[:, 0:T * P]).then_inc(psum_read["dve"], 1)

            def split(turn, j):
                if whole:
                    dve.wait_ge(rotated, j + 1)
                else:
                    wait_read(dve, turn, "qkv1")
                source = rot if whole else qkv

                def part(c, n):
                    return stk[:, c, :, n * DH:(n + 1) * DH].rearrange("p (t h) e -> p t h e", h=H)

                def whole_value(c):
                    return source[:, :, c * D:(c + 1) * D].rearrange("p t (h e) -> p t h e", e=DH)

                def left(c):
                    return rest[:, c, :, :].rearrange("p t (h e) -> p t h e", e=DH)

                for c in range(2):
                    chain.add(nc.vector.tensor_copy(part(c, 0), whole_value(c)))
                chain.wait(dve)
                for c in range(2):
                    chain.add(nc.vector.tensor_tensor(left(c), whole_value(c), part(c, 0), ALU.subtract))
                chain.wait(dve)
                for c in range(2):
                    chain.add(nc.vector.tensor_copy(part(c, 4), left(c)))
                chain.wait(dve)
                for c, n in ((0, 5), (1, 2)):
                    last = nc.vector.tensor_tensor(part(c, n), left(c), part(c, 4), ALU.subtract)
                last.then_inc(split_done, 1)

            def turned(turn, label, out, c):
                dve.wait_ge(psum_filled, turn.filled(label))
                nc.vector.tensor_copy(out[:, 4 * c:4 * c + 4, :],
                                      slot(turn.slot(label)).bitcast(BF16).rearrange("p (a x) -> p a x", a=4))\
                    .then_inc(psum_read["dve"], 1)

            def main(i, with_next):
                turn = turn_at(i, with_next)
                turned(turn, "k1", kT, 1)
                turned(turn, "q1", qT, 1)
                for g, (t, h0, heads, n_keys, pitch) in enumerate(max_groups):
                    dve.wait_ge(psum_filled, turn.filled(f"max{g}"))
                    nc.vector.tensor_reduce(mx[:, t * H + h0:t * H + h0 + heads].rearrange("p (x a) -> p a x", a=2),
                                            slot(turn.slot(f"max{g}")).rearrange("p (a x k) -> p a x k", a=2, k=pitch)
                                            [:, :, :, 0:n_keys], AX.X, ALU.max).then_inc(psum_read["dve"], 1)
                q_max = [stk[:, 0, :, MAX_AT + c] for c in range(3)]
                chain = main_chain
                chain.turn(i)
                wait_read(dve, turn, f"max{NM - 1}")
                chain.add(nc.vector.tensor_scalar(mrest[:, 0, :], mx[:], -1.0, None, ALU.mult))
                chain.wait(dve)
                chain.add(nc.vector.tensor_copy(q_max[0], mrest[:, 0, :]))
                chain.wait(dve)
                chain.add(nc.vector.tensor_tensor(mrest[:, 1, :], mrest[:, 0, :], q_max[0], ALU.subtract))
                chain.wait(dve)
                chain.add(nc.vector.tensor_copy(q_max[1], mrest[:, 1, :]))
                chain.wait(dve)
                nc.vector.tensor_tensor(q_max[2], mrest[:, 1, :], q_max[1], ALU.subtract).then_inc(neg_max_ready, 1)
                turned(turn, "r1", qT, 1)
                if with_next:
                    normalise(i + 1)
                    evacuate_x(turn)
                    split(turn, i + 1)
                dve.wait_ge(pv_done, NPV * (i + 1))
                sums = ps[:, 6:8, 0:T // 2 * H * (DH + 1)].rearrange("p a (x e) -> p a x e", e=DH + 1)
                chain.add(nc.vector.reciprocal(osum[:, :, :], sums[:, :, :, DH]))
                chain.wait(dve)
                nc.vector.tensor_tensor(on[:, :, :].rearrange("p (a t) (h e) -> p a (t h) e", a=2, e=DH),
                                        sums[:, :, :, 0:DH],
                                        osum[:, :, :].unsqueeze(3).to_broadcast([P, 2, T // 2 * H, DH]), ALU.mult)\
                    .then_inc(o_ready, 1)
                dve.wait_ge(psum_filled, turn.filled("proj"))
                dve.wait_ge(y_free, i + 1)
                nc.vector.tensor_tensor(y[:, :, :],
                                        slot(turn.slot("proj"))[:, 0:T * D].rearrange("p (t d) -> p t d", d=D),
                                        xr[:, bass.ds(i * T, T), :], ALU.add).then_inc(psum_read["dve"], 1)
                chain.end("maximum and sums")

            def first():
                normalise(0)
                evacuate_x(prologue)
                split(prologue, 0)

            run(dve, first, main)


def kernel(**inputs):
    import concourse.bacc as _bacc
    from concourse.bass_utils import run_bass_kernel_spmd as _run

    nc = _bacc.Bacc("TRN2", target_bir_lowering=False, num_devices=1)
    arrays = {}

    def put(name, a):
        a = np.ascontiguousarray(a)
        arrays[name] = a
        return nc.dram_tensor(name, a.shape, mybir.dt.from_np(a.dtype), kind="ExternalInput").ap()

    g = {k: np.asarray(v) for k, v in inputs.items()}
    x = put("x", g["L0_attn_a_x"])
    gate = put("gate_wT", g["L0_ffn_gate_w"].T)
    f = "L0_ffn_"
    wd = g[f + "Wd"].transpose(0, 2, 1).reshape(E, FJ, P, D).transpose(0, 2, 1, 3).reshape(E, P, FJ * D)
    w_exp = put("w_exp", np.concatenate([g[f + "Wg"].transpose(0, 2, 1), g[f + "Wu"].transpose(0, 2, 1), wd], axis=2))
    w_sh = put("w_sh", np.concatenate([g[f + "Ws_g"].T, g[f + "Ws_u"].T], axis=1))
    wd_sh = put("wd_sh", g[f + "Ws_d"].T)
    f = "L0_attn_a_"
    wa = put("wa_inT", g[f + "w_in"].T)
    oa = put("wa_outT", g[f + "w_out"].T)
    bias = put("bias_a", np.concatenate([g[f + "b_in"], g[f + "b_out"]])[None, :])
    f = "L0_attn_b_"
    wb = put("wb_inT", g[f + "Wqkv"].T)
    ob = put("wb_outT", g[f + "Wo"].T)
    gates = [put(n, g[f + n]) for n in ("log_xi", "pi_gate_logit", "e_gate_logit")]
    out = nc.dram_tensor("out", (B, N, D), F32, kind="ExternalOutput").ap()
    xn = nc.dram_tensor("xn", (B, N, D), F32, kind="Internal").ap()
    x1, x2, x3 = (nc.dram_tensor(f"x{n}", (B, N, D), F32, kind="Internal").ap() for n in (1, 2, 3))
    every4, every4_out = (a.rearrange("b (p r) d -> p b r d", r=STRIDE_A) for a in (x, x1))
    others, others_out = (a.rearrange("b (p r) d -> (b p) (r d)", r=STRIDE_A)[:, D:] for a in (x, x1))
    attention_block(nc, "a", lambda i: every4[:, bass.ds(i * T, T), 0, :],
                    lambda i: every4_out[:, bass.ds(i * T, T), 0, :], B // T, wa, oa, False, bias=bias,
                    keep=(others_out, others))
    moe_block(nc, "f1", x1, x2, xn, gate, w_exp, w_sh, wd_sh)
    attention_block(nc, "b", lambda i: x2[i].rearrange("(t p) d -> p t d", p=P),
                    lambda i: x3[i].rearrange("(t p) d -> p t d", p=P), B, wb, ob, True, gates=gates)
    moe_block(nc, "f2", x3, out, xn, gate, w_exp, w_sh, wd_sh)
    r = _run(nc, [arrays], core_ids=[0])
    return r.results[0]["out"]
```

```python
from contextlib import ExitStack
import math

import numpy as np
import concourse.bass as bass
from concourse import mybir

F32 = mybir.dt.float32
BF16 = mybir.dt.bfloat16
U32 = mybir.dt.uint32
I32 = mybir.dt.int32
ALU = mybir.AluOpType
ACT = mybir.ActivationFunctionType
AX = mybir.AxisListType

P = 128
B, N, D = 16, 512, 128
H, DH = 16, 8
T = N // P
E, FE, CAP = 16, 256, 64
FJ = FE // P
EPS = 1e-5
MASKED = -1.0e30
STRIDE_A, SEG_A = 4, 64
SLOT = 64
DECAY_AT, MAX_AT = 6 * DH, 6 * DH + 3
ROWS1, ROWS2 = MAX_AT, MAX_AT + 3
ANGLE_STEPS = (25, 32)
POOL_SETUP = {True: 26, False: 24}
SCALE = 1.0 / math.sqrt(DH)


def need(eng, sem, value):
    if isinstance(value, int) and value <= 0:
        return
    eng.wait_ge(sem, value)


def need_apart(eng, sem, value, least):
    if isinstance(value, int):
        return need(eng, sem, value)
    at = eng.to_reg(value)
    eng.wait_ge(sem, least)
    eng.wait_ge(sem, at)


class Count:

    def __init__(self, sem, per_turn):
        self.sem, self.per_turn = sem, per_turn

    def turn(self, i):
        self.base, self.n = self.per_turn * i, 0

    def add(self, ins):
        ins.then_inc(self.sem, 1)
        self.n += 1

    def wait(self, eng):
        eng.wait_ge(self.sem, self.base + self.n)

    def wait_apart(self, eng):
        need_apart(eng, self.sem, self.base + self.n, self.n)

    def end(self, what):
        assert self.n == self.per_turn, (what, self.n, self.per_turn)


def live(m, count):
    return not isinstance(m, int) or 0 <= m < count


def pipeline(eng, body, count, peel, drain):
    for n in range(peel):
        body(n, n % 2, n // 2)
    with eng.Fori(peel // 2, count // 2) as j:
        body(2 * j, 0, j)
        body(2 * j + 1, 1, j)
    for n in range(count, count + drain):
        body(n, n % 2, n // 2)


def moe_block(nc, tag, src, dst, xn_dram, gate_w, w_exp, w_sh, wd_sh):
    UNITS = 2 * FJ
    PAIRS = B // 2
    xn_rows = xn_dram.rearrange("b n d -> (b n) d")
    dst_rows = dst.rearrange("b n d -> (b n) d")
    with ExitStack() as ctx:
        def sb(name, shape, dt=F32):
            return ctx.enter_context(nc.sbuf_tensor(f"{tag}_{name}", shape, dt))

        def sem(name):
            return ctx.enter_context(nc.semaphore(f"{tag}_{name}"))

        ps = ctx.enter_context(nc.psum_tensor(f"{tag}_ps", [P, 8, 512], F32))
        ident = sb("ident", [P, P])
        xr = sb("xr", [P, B * T, D])
        gw = sb("gw", [P, E])
        wsh = sb("wsh", [P, 2 * FE])
        wdsh = sb("wdsh", [P, FJ, D])
        stats = sb("stats", [P, 2, T, 6])
        mv = sb("mv", [P, 2, T, 2])
        ve = sb("ve", [P, 2, T])
        expo = sb("expo", [P, T])
        rstd = sb("rstd", [P, 2, T])
        xn = sb("xn", [P, 2, T, D])
        xnT = sb("xnT", [P, 2, N])
        gel = sb("gel", [P, 2, 512])
        hT = sb("hT", [P, 2, FJ, 2 * 512])
        y = sb("y", [P, 2, T, D])
        lg = sb("lg", [P, B * T, E])
        pr = sb("pr", [P, 2, T, P])
        red = sb("red", [P, B * T])
        rows = sb("rows", [P, 2, N])
        top = sb("top", [P, 2, CAP])
        pos = sb("pos", [P, 2, CAP], U32)
        topd = sb("topd", [P, 2, 2, CAP])
        posd = sb("posd", [P, 2, 2, CAP])
        roff_i = sb("roff_i", [P, 1], I32)
        roff = sb("roff", [P, 2])
        tokens = sb("tokens", [P, E * PAIRS], U32)
        weight = sb("weight", [P, E, PAIRS])
        xg = sb("xg", [P, 2, PAIRS, D])
        xgT = sb("xgT", [P, 2, 1024])
        wexp = sb("wexp", [P, 2, 2 * FE + FJ * D])
        eo = sb("eo", [P, 2, PAIRS, D])

        consts_loaded = sem("consts_loaded")
        x_loaded = sem("x_loaded")
        pool_setup = sem("pool_setup")
        vchain = sem("vchain")
        var_ready = sem("var_ready")
        rstd_ready = sem("rstd_ready")
        xn_ready = sem("xn_ready")
        xn_stored = [sem(f"xn_stored{s}") for s in range(2)]
        turned = sem("turned")
        xnT_ready = sem("xnT_ready")
        logits_done = sem("logits_done")
        logits_read = sem("logits_read")
        gu_done = sem("gu_done")
        gelu_done = sem("gelu_done")
        h_ready = sem("h_ready")
        down_done = sem("down_done")
        y_ready = sem("y_ready")
        y_stored = [sem(f"y_stored{s}") for s in range(2)]
        shifted = sem("shifted")
        exped = sem("exped")
        probs_ready = sem("probs_ready")
        rows_turned = sem("rows_turned")
        rows_ready = sem("rows_ready")
        top_ready = sem("top_ready")
        top_turned = sem("top_turned")
        tokens_ready = sem("tokens_ready")
        gathered = [sem(f"gathered{s}") for s in range(2)]
        w_loaded = [sem(f"w_loaded{s}") for s in range(2)]
        e_turned = sem("e_turned")
        xgT_ready = sem("xgT_ready")
        e_gu = sem("e_gu")
        e_gelu = sem("e_gelu")
        e_h = sem("e_h")
        e_down = sem("e_down")
        eo_ready = sem("eo_ready")
        scattered = sem("scattered")
        block = ctx.enter_context(nc.Block())

        @block.sync
        def _(sp):
            sp.dma_start(gw[:], gate_w).then_inc(consts_loaded, 16)
            sp.dma_start(wsh[:], w_sh).then_inc(consts_loaded, 16)
            sp.dma_start(wdsh[:], wd_sh.rearrange("(j p) d -> p j d", p=P)).then_inc(consts_loaded, 16)

            def load_x(b):
                sp.dma_start(xr[:, bass.ds(b * T, T), :],
                             src[b].rearrange("(t p) d -> p t d", p=P)).then_inc(x_loaded, 16)

            def shared_step(n, s, half):
                if live(n + 1, B):
                    need(sp, x_loaded, 16 * (n + 1))
                    load_x(n + 1)
                if live(n, B):
                    sp.wait_ge(xn_ready, n + 1)
                    sp.dma_start(xn_dram[n].rearrange("(t p) d -> p t d", p=P), xn[:, s, :, :])\
                        .then_inc(xn_stored[s], 16)
                m = n - 2
                if live(m, B):
                    sp.wait_ge(y_ready, m + 1)
                    sp.dma_start(dst[m].rearrange("(t p) d -> p t d", p=P), y[:, s, :, :])\
                        .then_inc(y_stored[s], 16)

            load_x(0)
            for n in range(4):
                shared_step(n, n % 2, n // 2)
            with sp.Fori(2, B // 2 - 1) as j:
                shared_step(2 * j, 0, j)
                shared_step(2 * j + 1, 1, j)
            for n in range(B - 2, B + 2):
                shared_step(n, n % 2, n // 2)

            def expert_load(n, s, half):
                if live(n, E):
                    need(sp, e_down, n - 1)
                    sp.dma_start(wexp[:, s, :], w_exp[n]).then_inc(w_loaded[s], 16)

            pipeline(sp, expert_load, E, 2, 0)
            sp.wait_ge(scattered, 16 * PAIRS * E)

        @block.gpsimd
        def _(pool):
            nc.gpsimd.memset(ident[:], 0.0).then_inc(pool_setup, 1)
            nc.gpsimd.memset(expo[:], -0.5).then_inc(pool_setup, 1)
            nc.gpsimd.iota(roff_i[:], [[0, 1]], base=0, channel_multiplier=1).then_inc(pool_setup, 1)
            pool.wait_ge(pool_setup, 3)
            nc.gpsimd.affine_select(out=ident[:], in_=ident[:], compare_op=ALU.not_equal, fill=1.0, base=0,
                                    pattern=[[-1, P]], channel_multiplier=1).then_inc(pool_setup, 1)

            def rstd_step(n, s, half):
                if live(n, B):
                    pool.wait_ge(var_ready, n + 1)
                    nc.gpsimd.tensor_tensor(rstd[:, s, :], ve[:, s, :], expo[:], ALU.pow).then_inc(rstd_ready, 1)

            pipeline(pool, rstd_step, B, 2, 0)

            pool.wait_ge(tokens_ready, 1)
            for s in range(2):
                pool.wait_ge(xn_stored[s], 16 * B // 2)
                pool.wait_ge(y_stored[s], 16 * B // 2)

            def indices(e, k):
                return bass.IndirectOffsetOnAxis(ap=tokens[:, e * PAIRS + k:e * PAIRS + k + 1], axis=0)

            def gather(e):
                need(pool, e_turned, e - 1)
                for k in range(PAIRS):
                    nc.gpsimd.indirect_dma_start(xg[:, e % 2, k, :], None, xn_rows, indices(e, k))\
                        .then_inc(gathered[e % 2], 16)

            gather(0)
            gather(1)
            for e in range(E):
                if e + 2 < E:
                    gather(e + 2)
                pool.wait_ge(eo_ready, e + 1)
                need(pool, scattered, 16 * PAIRS * e)
                for k in range(PAIRS):
                    nc.gpsimd.indirect_dma_start(dst_rows, indices(e, k), eo[:, e % 2, k, :], None,
                                                 compute_op=ALU.add).then_inc(scattered, 16)

        @block.scalar
        def _(act):
            def shared_step(n, s, half):
                if not live(n, B):
                    return
                act.wait_ge(turned, n + 1)
                need(act, gu_done, FJ * (n - 1))
                nc.scalar.activation(xnT[:, s, :], ps[:, 0, :], ACT.Copy).then_inc(xnT_ready, 1)
                for j in range(FJ):
                    act.wait_ge(gu_done, FJ * n + j + 1)
                    need(act, h_ready, FJ * (n - 1) + j + 1)
                    nc.scalar.activation(gel[:, j, :], ps[:, 2 + 2 * j, :], ACT.Gelu).then_inc(gelu_done, 1)

            pipeline(act, shared_step, B, 4, 0)
            act.wait_ge(shifted, 1)
            nc.scalar.activation(lg[:, :, :], lg[:, :, :], ACT.Exp).then_inc(exped, 1)

            def expert_step(n, s, half):
                if not live(n, E):
                    return
                act.wait_ge(e_turned, n + 1)
                need(act, e_gu, UNITS * (n - 1))
                nc.scalar.activation(xgT[:, s, :].rearrange("p (a c) -> p a c", a=2), ps[:, 0:2, :], ACT.Copy)\
                    .then_inc(xgT_ready, 1)
                for u in range(UNITS):
                    act.wait_ge(e_gu, UNITS * n + u + 1)
                    if u >= 2 or not isinstance(n, int) or n > 0:
                        act.wait_ge(e_h, UNITS * n + u - 1)
                    elif n == 0:
                        act.wait_ge(h_ready, FJ * B)
                    nc.scalar.activation(gel[:, u % 2, :], ps[:, 2 + 2 * (u % 2), :], ACT.Gelu).then_inc(e_gelu, 1)

            pipeline(act, expert_step, E, 2, 0)

        @block.tensor
        def _(pe):
            pe.wait_ge(pool_setup, 4)
            pe.wait_ge(consts_loaded, 48)

            def shared_step(n, s, half):
                if live(n, B):
                    pe.wait_ge(xn_ready, n + 1)
                    need(pe, xnT_ready, n)
                    for t in range(T):
                        last = nc.tensor.transpose(ps[:, 0, t * P:(t + 1) * P], xn[:, s, t, :], ident[:])
                    last.then_inc(turned, 1)
                m, ms = n - 1, 1 - s
                if live(m, B):
                    pe.wait_ge(h_ready, FJ * (m + 1))
                    need(pe, y_ready, m - 1)
                    for t in range(T):
                        for j in range(FJ):
                            last = nc.tensor.matmul(ps[:, 6 + ms, t * D:(t + 1) * D],
                                                    hT[:, ms, j, t * P:(t + 1) * P], wdsh[:, j, :],
                                                    start=(j == 0), stop=(j == FJ - 1))
                    last.then_inc(down_done, 1)
                if live(n, B):
                    pe.wait_ge(xnT_ready, n + 1)
                    need(pe, logits_read, n)
                    for t in range(T):
                        last = nc.tensor.matmul(ps[:, 1, t * E:(t + 1) * E], xnT[:, s, t * P:(t + 1) * P], gw[:],
                                                start=True, stop=True)
                    last.then_inc(logits_done, 1)
                    for j in range(FJ):
                        need(pe, h_ready, FJ * (n - 1) + j + 1)
                        for half_w in range(2):
                            last = nc.tensor.matmul(ps[:, 2 + 2 * j + half_w, :],
                                                    wsh[:, half_w * FE + j * P:half_w * FE + (j + 1) * P],
                                                    xnT[:, s, :], start=True, stop=True)
                        last.then_inc(gu_done, 1)

            pipeline(pe, shared_step, B, 4, 2)

            pe.wait_ge(probs_ready, 1)
            for g in range(2):
                for t in range(T):
                    last = nc.tensor.transpose(ps[:, g, t * P:(t + 1) * P], pr[:, g, t, :], ident[:])
            last.then_inc(rows_turned, 1)
            pe.wait_ge(top_ready, 1)
            for g in range(2):
                nc.tensor.transpose(ps[:, 2, g * P:(g + 1) * P],
                                    topd[:, g, :, :].rearrange("p a c -> p (a c)"), ident[:])
                last = nc.tensor.transpose(ps[:, 3, g * P:(g + 1) * P],
                                           posd[:, g, :, :].rearrange("p a c -> p (a c)"), ident[:])
            last.then_inc(top_turned, 1)

            def expert_step(n, s, half):
                if live(n, E):
                    pe.wait_ge(gathered[s], 16 * PAIRS * (half + 1))
                    need(pe, xgT_ready, n)
                    if isinstance(n, int) and n == 0:
                        pe.wait_ge(tokens_ready, 1)
                    for k in range(PAIRS):
                        last = nc.tensor.transpose(ps[:, k // 4, (k % 4) * P:(k % 4 + 1) * P], xg[:, s, k, :],
                                                   ident[:])
                    last.then_inc(e_turned, 1)
                m, ms = n - 1, 1 - s
                if live(m, E):
                    pe.wait_ge(e_h, UNITS * (m + 1))
                    need(pe, eo_ready, m)
                    for k in range(PAIRS):
                        for j in range(FJ):
                            last = nc.tensor.matmul(ps[:, 6 + k // 4, (k % 4) * D:(k % 4 + 1) * D],
                                                    hT[:, ms, j, k * P:(k + 1) * P],
                                                    wexp[:, ms, 2 * FE + j * D:2 * FE + (j + 1) * D],
                                                    start=(j == 0), stop=(j == FJ - 1))
                    last.then_inc(e_down, 1)
                if live(n, E):
                    pe.wait_ge(xgT_ready, n + 1)
                    pe.wait_ge(w_loaded[s], 16 * (half + 1))
                    for u in range(UNITS):
                        a, j = u // FJ, u % FJ
                        if u >= 2 or not isinstance(n, int) or n > 0:
                            pe.wait_ge(e_h, UNITS * n + u - 1)
                        for half_w in range(2):
                            last = nc.tensor.matmul(ps[:, 2 + 2 * (u % 2) + half_w, :],
                                                    wexp[:, s, half_w * FE + j * P:half_w * FE + (j + 1) * P],
                                                    xgT[:, s, a * 512:(a + 1) * 512], start=True, stop=True)
                        last.then_inc(e_gu, 1)

            pipeline(pe, expert_step, E, 2, 2)

        @block.vector
        def _(dve):
            chain = Count(vchain, 2 * T)

            def shared_step(n, s, half):
                if live(n, B):
                    chain.turn(n)
                    dve.wait_ge(x_loaded, 16 * (n + 1))
                    for t in range(T):
                        chain.add(nc.vector.bn_stats(stats[:, s, t, :], xr[:, bass.ds(n * T + t, 1), :]
                                                     .rearrange("p a d -> p (a d)")))
                    chain.wait_apart(dve)
                    for t in range(T):
                        chain.add(nc.vector.bn_aggr(mv[:, s, t, :], stats[:, s, t, :]))
                    chain.wait(dve)
                    nc.vector.tensor_scalar(ve[:, s, :], mv[:, s, :, 1], EPS, None, ALU.add).then_inc(var_ready, 1)
                    dve.wait_ge(rstd_ready, n + 1)
                    need(dve, turned, n - 1)
                    need(dve, xn_stored[s], 16 * half)
                    for t in range(T):
                        last = nc.vector.tensor_scalar(xn[:, s, t, :], xr[:, bass.ds(n * T + t, 1), :]
                                                       .rearrange("p a d -> p (a d)"),
                                                       mv[:, s, t, 0:1], rstd[:, s, t:t + 1],
                                                       ALU.subtract, ALU.mult)
                    last.then_inc(xn_ready, 1)
                    chain.end("normalisation")
                m, ms = n - 1, 1 - s
                if live(m, B):
                    dve.wait_ge(logits_done, m + 1)
                    nc.vector.tensor_copy(lg[:, bass.ds(m * T, T), :],
                                          ps[:, 1, 0:T * E].rearrange("p (t e) -> p t e", e=E))\
                        .then_inc(logits_read, 1)
                    need(dve, down_done, m - 1)
                    for j in range(FJ):
                        dve.wait_ge(gelu_done, FJ * m + j + 1)
                        nc.vector.tensor_tensor(hT[:, ms, j, 0:512], gel[:, j, :], ps[:, 3 + 2 * j, :], ALU.mult)\
                            .then_inc(h_ready, 1)
                m, ms = n - 2, s
                if live(m, B):
                    dve.wait_ge(down_done, m + 1)
                    if not isinstance(half, int) or half >= 2:
                        dve.wait_ge(y_stored[ms], 16 * (half - 1))
                    nc.vector.tensor_tensor(y[:, ms, :, :], ps[:, 6 + ms, :].rearrange("p (t d) -> p t d", d=D),
                                            xr[:, bass.ds(m * T, T), :], ALU.add).then_inc(y_ready, 1)

            pipeline(dve, shared_step, B, 4, 2)

            at = [2 * T * B]

            def link(ins):
                ins.then_inc(vchain, 1)
                at[0] += 1
                dve.wait_ge(vchain, at[0])

            dve.wait_ge(logits_read, B)
            link(nc.vector.tensor_reduce(red[:], lg[:, :, :], AX.X, ALU.max))
            nc.vector.tensor_tensor(lg[:, :, :], lg[:, :, :], red[:].unsqueeze(2).to_broadcast([P, B * T, E]),
                                    ALU.subtract).then_inc(shifted, 1)
            dve.wait_ge(exped, 1)
            link(nc.vector.tensor_reduce(red[:], lg[:, :, :], AX.X, ALU.add))
            link(nc.vector.reciprocal(red[:], red[:]))
            for g in range(2):
                half_b = slice(g * B // 2 * T, (g + 1) * B // 2 * T)
                last = nc.vector.tensor_tensor(
                    pr[:, g, :, :].rearrange("p t (b e) -> p b t e", e=E),
                    lg[:, half_b, :].rearrange("p (b t) e -> p b t e", t=T),
                    red[:, half_b].rearrange("p (b t) -> p b t", t=T).unsqueeze(3).to_broadcast([P, B // 2, T, E]),
                    ALU.mult)
            last.then_inc(probs_ready, 1)
            dve.wait_ge(pool_setup, 4)
            link(nc.vector.tensor_scalar(roff_i[:], roff_i[:], int(math.log2(E)), int(math.log2(N)),
                                         ALU.logical_shift_right, ALU.logical_shift_left))
            for g in range(2):
                link(nc.vector.tensor_scalar(roff[:, g:g + 1], roff_i[:], float(g * B // 2 * N), None, ALU.add))
            dve.wait_ge(rows_turned, 1)
            link(nc.vector.tensor_copy(rows[:], ps[:, 0:2, :]))
            for r in range(CAP // 8):
                at8 = slice(8 * r, 8 * r + 8)
                for g in range(2):
                    last = nc.vector.max(top[:, g, at8], rows[:, g, :])
                    last.then_inc(vchain, 1)
                    at[0] += 1
                for g in range(2):
                    dve.wait_ge(vchain, at[0] - 1 + g)
                    nc.vector.max_index(pos[:, g, at8], top[:, g, at8], rows[:, g, :]).then_inc(vchain, 1)
                at[0] += 2
                if r < CAP // 8 - 1:
                    for g in range(2):
                        dve.wait_ge(vchain, at[0] - 1 + g)
                        nc.vector.match_replace(rows[:, g, :], top[:, g, at8], rows[:, g, :], -1.0)\
                            .then_inc(vchain, 1)
                    at[0] += 2
                dve.wait_ge(vchain, at[0])
            for g in range(2):
                for a in range(2):
                    nc.vector.tensor_copy(topd[:, g, a, :], top[:, g, :])
                    last = nc.vector.tensor_scalar(posd[:, g, a, :], pos[:, g, :], roff[:, g:g + 1], None, ALU.add)
            last.then_inc(top_ready, 1)
            dve.wait_ge(top_turned, 1)
            tok_v = tokens[:].rearrange("p (e k) -> p e k", k=PAIRS)
            for g in range(2):
                for a in range(2):
                    rows_a = slice(a * CAP, (a + 1) * CAP)
                    for bank, out in ((2, weight), (3, tok_v)):
                        v = ps[rows_a, bank, g * P:(g + 1) * P].rearrange("p (k a e) -> p a e k", a=2, e=E)
                        last = nc.vector.tensor_copy(out[rows_a, :, g * 4:(g + 1) * 4], v[:, a, :, :])
                        link(last)
            nc.vector.tensor_copy(red[:, 0:1], red[:, 1:2]).then_inc(tokens_ready, 1)

            def expert_step(n, s, half):
                m, ms = n - 1, 1 - s
                if live(m, E):
                    dve.wait_ge(e_down, m + 1)
                    if not isinstance(m, int) or m >= 2:
                        dve.wait_ge(scattered, 16 * PAIRS * (m - 1))
                    for c in range(2):
                        last = nc.vector.tensor_tensor(
                            eo[:, ms, 4 * c:4 * c + 4, :], ps[:, 6 + c, :].rearrange("p (k d) -> p k d", d=D),
                            weight[:, bass.ds(m, 1), 4 * c:4 * c + 4].rearrange("p a k -> p (a k)")
                            .unsqueeze(2).to_broadcast([P, 4, D]), ALU.mult)
                    last.then_inc(eo_ready, 1)
                if live(n, E):
                    need(dve, e_down, n - 1)
                    for u in range(UNITS):
                        a, j = u // FJ, u % FJ
                        dve.wait_ge(e_gelu, UNITS * n + u + 1)
                        nc.vector.tensor_tensor(hT[:, s, j, a * 512:(a + 1) * 512], gel[:, u % 2, :],
                                                ps[:, 3 + 2 * (u % 2), :], ALU.mult).then_inc(e_h, 1)

            pipeline(dve, expert_step, E, 4, 2)


class Step:

    def __init__(self, i, odd, now, before, filled0, read0, first_slot, least=None):
        self.i, self.odd, self.now, self.before = i, odd, now, before
        self.filled0, self.read0, self.first_slot = filled0, read0, first_slot
        self.least = least or self
        self.uses = [u for u in now if u[1]]
        self.uses_before = [u for u in before if u[1]]
        self.at = {label: k for k, (label, _) in enumerate(self.uses)}

    def slot(self, label):
        return (self.first_slot + self.at[label]) % 3

    def filled(self, label):
        return self.filled0 + self.at[label] + 1

    def read(self, label):
        k = self.at[label]
        reader = self.uses[k][1]
        return reader, self.read0[reader] + sum(r == reader for _, r in self.uses[:k + 1])

    def read_before(self, label):
        k = [u[0] for u in self.uses_before].index(label)
        reader = self.uses_before[k][1]
        return reader, self.read0[reader] - sum(r == reader for _, r in self.uses_before[k + 1:])

    def freed(self, label):
        k = self.at[label] - 3
        if k >= 0:
            return self.read(self.uses[k][0])
        if len(self.uses_before) + k >= 0:
            return self.read_before(self.uses_before[k][0])
        return None


def attention_block(nc, tag, src, dst, turns, w_qkv, w_o, causal_tiles, bias=None, gates=None, keep=None):
    whole = causal_tiles
    SETS = H // 4
    WIDE = P // 4
    BANKS = ((0, 1, 2), (3,))
    bank_of = {s: b for b, sets in enumerate(BANKS) for s in sets}
    seen = (lambda t: range(t + 1)) if whole else (lambda t: range(t, t + 1))
    askers = (lambda k: range(k, T)) if whole else (lambda k: range(k, k + 1))
    max_groups = []
    for half in range(2):
        for t in range(T):
            n_keys = P * len(seen(t))
            pitch = {128: 128, 256: 256}.get(n_keys, 512)
            heads = 1024 // pitch
            max_groups += [(t, h, heads, n_keys, pitch) for h in range(8 * half, 8 * half + 8, heads)]
    exp_groups = []
    for s in range(SETS):
        heads = range(4 * s, 4 * s + 4)
        if whole:
            exp_groups.append([(h, 2, 512 * (h % 2) + 256 * (h % 4 // 2)) for h in heads])
            exp_groups += [[(h, 0, 0), (h, 1, 512), (h, 3, 896)] for h in heads]
        else:
            exp_groups += [[(h, k, 512 * (h % 2) + 256 * (k % 2) + P * (h % 4 // 2)) for h in heads
                            for k in (2 * a, 2 * a + 1)] for a in range(2)]
    where = {(h, k): (g, col) for g, parts in enumerate(exp_groups) for h, k, col in parts}
    NG, NM = len(exp_groups), len(max_groups)
    GS = NG // SETS
    RING = 2 * GS
    max_half, exp_half = NM // 2, NG // 2
    split_at, turn_at = (9, 14) if whole else (4, 7)
    LEAD = 3

    def events(i):
        x, m, e, f = (0 <= i + d < turns for d in (2, 1, 0, -1))
        out = []

        def add(stage, *named):
            if stage:
                out.extend(named)

        def max_group(g):
            add(m and g < NM, (f"max{g}", "dve"))

        max_group(0)
        add(x, ("stats", None))
        add(f, ("pv30", None), ("ot0", None))
        max_group(1)
        add(x, ("aggregate", None))
        add(f, ("pv31", None))
        add(e, ("r0", "act"))
        add(f, ("pv32", None))
        max_group(2)
        add(x, ("xn", None))
        add(f, ("pv33", None))
        for g in range(NG):
            add(e, (f"exp{g}", "act"))
            max_group(g + LEAD)
            add(f and g == 0, ("ot1", None))
            add(m and g == (1 if whole else 0), ("k1", "act"))
            add(m and g == (2 if whole else 0), ("q1", "dve"))
            add(e and g == (4 if whole else 1), ("r1", "act"))
            add(f and g == 1, ("sums", "dve"))
            add(x and g == 1, ("xnT", "dve"))
            add(f and g == 3, ("oT", "act"))
            add(x and g == 2, ("qkv0", "act"))
            add(x and g == 3, ("qkv1", "act"))
            add(f and g == 4, ("proj", "dve"))
            for s in range(SETS - 1):
                for k in range(T):
                    add(e and g == GS * (s + 1) + 1 + (k if whole else 0), (f"pv{s}{k}", None))
            for c in range(4):
                add(x and g == min(split_at + c, NG - 1), (f"split{c}", None))
            add(x and g == min(split_at + 4, NG - 1), ("stack", None))
            add(x and g == turn_at, ("k0", "act"))
            add(x and g == min(turn_at + 1, NG - 1), ("q0", "dve"))
        add(m, ("negative_max", None))
        return out

    loop_pairs = max(0, (turns - 4) // 2)

    def counts(i):
        uses = [r for _, r in events(i) if r]
        return {"filled": len(uses), **{r: uses.count(r) for r in ("act", "dve")}}

    def step_of(i):
        before = [counts(j) for j in range(-2, i)]
        total = {key: sum(c[key] for c in before) for key in ("filled", "act", "dve")}
        return Step(i, i % 2, events(i), events(i - 1), total["filled"], total, total["filled"] % 3)

    def step_in_loop(n, odd):
        least, full = step_of(2 + odd), counts(2)
        ahead = {key: least.read0[key] + 2 * full[key] * (n - 1) for key in full}
        assert 2 * full["filled"] % 3 == 0
        return Step(2 * n + odd, odd, least.now, least.before, ahead["filled"], ahead, least.first_slot, least)

    def run(eng, work):
        start = turns if loop_pairs == 0 else 1
        for i in range(-2, start + 1):
            work(step_of(i))
        if loop_pairs:
            with eng.Fori(1, 1 + loop_pairs) as n:
                work(step_in_loop(n, 0))
                work(step_in_loop(n, 1))
            for i in range(2 + 2 * loop_pairs, turns + 1):
                work(step_of(i))

    with ExitStack() as ctx:
        def sb(name, shape, dt=F32):
            return ctx.enter_context(nc.sbuf_tensor(f"{tag}_{name}", shape, dt))

        def sem(name):
            return ctx.enter_context(nc.semaphore(f"{tag}_{name}"))

        ps = ctx.enter_context(nc.psum_tensor(f"{tag}_ps", [P, 8, 512], F32))
        ident = sb("ident", [P, P])
        identb = sb("identb", [P, P], BF16)
        select = sb("select", [P, 3, 4, DH + 1])
        mask_q = sb("mask_q", [P, P], BF16)
        mask_k = sb("mask_k", [P, P], BF16)
        wqkv = sb("wqkv", [P, 3 * D])
        wo = sb("wo", [P, D])
        xr = sb("xr", [P, turns * T, D])
        stats = sb("stats", [P, T, 6])
        mv = sb("mv", [P, T, 2])
        ve = sb("ve", [P, T])
        expo = sb("expo", [P, T])
        rstd = sb("rstd", [P, T])
        xn = sb("xn", [P, T, D])
        xnT = sb("xnT", [P, T * P])
        qkv = sb("qkv", [P, 2, T, 3 * D])
        rest = sb("rest", [P, 2, T, D])
        stk = sb("stk", [P, 2, 2, T * H, SLOT], BF16)
        qT = sb("qT", [P, 2, H // 2, T * P], BF16)
        kT = sb("kT", [P, 2, H // 2, T * P], BF16)
        v1 = sb("v1", [P, T, H, WIDE])
        v1_sets = [(4 * s, (DH + 1) * (s % 3)) for s in range(SETS)]
        mx = sb("mx", [P, T * H])
        mrest = sb("mrest", [P, 2, T * H])
        pT = sb("pT", [P, RING, 1024])
        ot = sb("ot", [P, 2, T * P])
        osum = sb("osum", [P, 2, T * H // 2])
        on = sb("on", [P, T, D])
        oT = sb("oT", [P, T * P])
        y = sb("y", [P, T, D])
        consts_loaded = sem("consts_loaded")
        pool_setup = sem("pool_setup")
        setup_chain = sem("setup_chain")
        setup_act = sem("setup_act")
        setup_done = sem("setup_done")
        x_loaded = sem("x_loaded")
        vchain = sem("vchain")
        max_chain = sem("max_chain")
        sums_chain = sem("sums_chain")
        var_ready = sem("var_ready")
        rstd_ready = sem("rstd_ready")
        xn_ready = sem("xn_ready")
        psum_filled = sem("psum_filled")
        psum_read = {"act": sem("psum_read_by_scalar"), "dve": sem("psum_read_by_vector")}
        v_copied = sem("v_copied")
        pool_chain = sem("pool_chain")
        rotated = sem("rotated")
        split_done = sem("split_done")
        stack_ready = {"act": sem("q_stack_ready"), "dve": sem("k_stack_ready")}
        neg_max_ready = sem("neg_max_ready")
        pv_done = sem("pv_done")
        ot_copied = sem("ot_copied")
        y_free = sem("y_free")
        kept = sem("kept")
        y_stored = sem("y_stored")
        if whole:
            lin = sb("lin", [P, 3, H])
            gts = sb("gts", [P, 3, H])
            pos_i = sb("pos_i", [P, T], I32)
            posf = sb("posf", [P, T])
            freq = sb("freq", [P, DH // 2])
            th0 = sb("th0", [P, T, DH // 2])
            th = sb("th", [P, T, H, DH // 2])
            turnsf = sb("turnsf", [P, T * H * DH // 2])
            ang = sb("ang", [P, T * H * DH // 2])
            cs = sb("cs", [P, 2, T, 2, H * DH // 2])
            rot = sb("rot", [P, T, 2 * D])
            tmp = sb("tmp", [P, 4, T, D])
            dec = sb("dec", [P, T * H])
            decr = sb("decr", [P, 2, T * H])
        else:
            brow = sb("brow", [1, 4 * D])
            ones1 = sb("ones1", [1, P])
        block = ctx.enter_context(nc.Block())

        def slot(k):
            return ps[:, 2 * k:2 * k + 2, :].rearrange("p a c -> p (a c)")

        def wait_read(eng, step, label):
            reader, count = step.read(label)
            eng.wait_ge(psum_read[reader], count)

        @block.sync
        def _(sp):
            def load(j):
                sp.dma_start(xr[:, bass.ds(j * T, T), :], src(j)).then_inc(x_loaded, 16)

            load(0)
            sp.dma_start(wqkv[:], w_qkv).then_inc(consts_loaded, 16)
            sp.dma_start(wo[:], w_o).then_inc(consts_loaded, 16)
            if whole:
                for c in range(3):
                    sp.dma_start(lin[:, c, :], gates[c].unsqueeze(0).to_broadcast([P, H]))\
                        .then_inc(consts_loaded, 16)
            else:
                sp.dma_start(brow[:], bias).then_inc(consts_loaded, 16)
            if keep:
                sp.dma_start(*keep).then_inc(kept, 16)
            sp.sem_inc(y_free, 1)

            def work(step):
                i = step.i
                for label, _ in step.now:
                    if label == "stats":
                        if not isinstance(i, int) or i > -2:
                            sp.wait_ge(x_loaded, 16 * (i + 2))
                            load(i + 2)
                    elif label == "proj":
                        wait_read(sp, step, "proj")
                        sp.dma_start(dst(i - 1), y[:, :, :]).then_inc(y_stored, 16)
                        sp.wait_ge(y_stored, 16 * i)
                        sp.sem_inc(y_free, 1)

            run(sp, work)
            if keep:
                sp.wait_ge(kept, 16)

        @block.gpsimd
        def _(pool):
            nc.gpsimd.memset(expo[:], -0.5).then_inc(pool_setup, 1)
            nc.gpsimd.memset(ident[:], 0.0).then_inc(pool_setup, 1)
            nc.gpsimd.memset(mask_q[:], 0.0).then_inc(pool_setup, 1)
            nc.gpsimd.memset(mask_k[:], 0.0).then_inc(pool_setup, 1)
            nc.gpsimd.memset(stk[:, :, :, :, DECAY_AT:SLOT].rearrange("p a b n s -> p (a b n) s"), 0.0)\
                .then_inc(pool_setup, 1)
            nc.gpsimd.memset(v1[:], 0.0).then_inc(pool_setup, 1)
            pool.wait_ge(pool_setup, 6)
            nc.gpsimd.affine_select(out=ident[:], in_=ident[:], compare_op=ALU.not_equal, fill=1.0, base=0,
                                    pattern=[[-1, P]], channel_multiplier=1).then_inc(pool_setup, 1)
            nc.gpsimd.affine_select(out=mask_q[:], in_=mask_q[:], compare_op=ALU.is_ge, fill=MASKED, base=0,
                                    pattern=[[-1, P]], channel_multiplier=1).then_inc(pool_setup, 1)
            nc.gpsimd.affine_select(out=mask_k[:], in_=mask_k[:], compare_op=ALU.is_ge, fill=MASKED, base=0,
                                    pattern=[[1, P]], channel_multiplier=-1).then_inc(pool_setup, 1)
            for h, c in v1_sets:
                nc.gpsimd.memset(v1[:, :, h:h + 4, c + DH:c + DH + 1], 1.0).then_inc(pool_setup, 1)
            for turn in range(2):
                nc.gpsimd.memset(stk[:, turn, 0, :, DECAY_AT:DECAY_AT + 3], 1.0).then_inc(pool_setup, 1)
                nc.gpsimd.memset(stk[:, turn, 1, :, MAX_AT:MAX_AT + 3], 1.0).then_inc(pool_setup, 1)
            pool.wait_ge(pool_setup, 17)
            nc.gpsimd.tensor_copy(identb[:], ident[:]).then_inc(pool_setup, 1)
            for n in range(3):
                c = (DH + 1) * n
                nc.gpsimd.tensor_copy(select[:, n, :, :],
                                      ident[:].rearrange("p (j c) -> p j c", c=WIDE)[:, :, c:c + DH + 1])\
                    .then_inc(pool_setup, 1)
            if whole:
                nc.gpsimd.iota(pos_i[:], [[P, T]], base=0, channel_multiplier=1).then_inc(pool_setup, 1)
                for f in range(DH // 2):
                    value = float(np.float32(math.pi) ** np.float32(1.0 - 2 * f / DH))
                    nc.gpsimd.memset(freq[:, f:f + 1], value).then_inc(pool_setup, 1)
            else:
                nc.gpsimd.memset(ones1[:], 1.0).then_inc(pool_setup, 1)
                pool.wait_ge(pool_setup, 22)
                nc.gpsimd.memset(mask_q[SEG_A:P, 0:SEG_A], MASKED).then_inc(pool_setup, 1)
                pool.wait_ge(pool_setup, 23)
                nc.gpsimd.memset(mask_k[0:SEG_A, SEG_A:P], MASKED).then_inc(pool_setup, 1)
            chain = Count(pool_chain, 4)

            def work(step):
                i, j, odd = step.i, step.i + 2, step.odd
                labels = [label for label, _ in step.now]
                if "aggregate" in labels:
                    pool.wait_ge(var_ready, j + 1)
                    nc.gpsimd.tensor_tensor(rstd[:], ve[:], expo[:], ALU.pow).then_inc(rstd_ready, 1)
                if "exp0" in labels:
                    if "pv33" in labels:
                        need_apart(pool, pv_done, SETS * i, SETS * step.least.i)
                    for h, c in v1_sets:
                        last = nc.gpsimd.tensor_copy(v1[:, :, h:h + 4, c:c + DH],
                                                     qkv[:, odd, :, 2 * D + h * DH:2 * D + (h + 4) * DH]
                                                     .rearrange("p t (h e) -> p t h e", e=DH))
                    last.then_inc(v_copied, 1)
                if "qkv1" in labels and whole:
                    if isinstance(i, int) and i == -2:
                        pool.wait_ge(setup_done, 1)
                    chain.turn(j)
                    wait_read(pool, step, "qkv1")
                    even, one = (qkv[:, odd, :, bass.ds(o, D, step=2)] for o in range(2))
                    cos, sin = (cs[:, c, :, :, :].rearrange("p t a x -> p t (a x)") for c in range(2))
                    for c, (a, b) in enumerate(((even, cos), (one, sin), (even, sin), (one, cos))):
                        chain.add(nc.gpsimd.tensor_tensor(tmp[:, c, :, :], a, b, ALU.mult))
                    chain.wait(pool)
                    need(pool, split_done, j)
                    nc.gpsimd.tensor_tensor(rot[:, :, bass.ds(0, D, step=2)], tmp[:, 0, :, :], tmp[:, 1, :, :],
                                            ALU.subtract)
                    nc.gpsimd.tensor_tensor(rot[:, :, bass.ds(1, D, step=2)], tmp[:, 2, :, :], tmp[:, 3, :, :],
                                            ALU.add).then_inc(rotated, 1)
                    chain.end("rotation")

            run(pool, work)

        @block.scalar
        def _(act):
            if whole:
                act.wait_ge(consts_loaded, 80)
                nc.scalar.activation(gts[:, :, :], lin[:, :, :], ACT.Exp, scale=-1.0).then_inc(setup_act, 1)
                for c in range(2):
                    act.wait_ge(setup_chain, ANGLE_STEPS[c])
                    nc.scalar.activation(cs[:, c, :, 0, :], ang[:].rearrange("p (t x) -> p t x", t=T), ACT.Sin)
                    nc.scalar.activation(cs[:, c, :, 1, :], ang[:].rearrange("p (t x) -> p t x", t=T), ACT.Sin)\
                        .then_inc(setup_act, 1)

            def work(step):
                i, odd = step.i, step.odd
                for label, reader in step.now:
                    if label == "stack":
                        act.wait_ge(split_done, i + 3)
                        for a, b in ((0, 1), (0, 2), (4, 3)):
                            last = nc.scalar.activation(stk[:, odd, 0, :, b * DH:(b + 1) * DH],
                                                        stk[:, odd, 0, :, a * DH:(a + 1) * DH], ACT.Copy)
                        last.then_inc(stack_ready["act"], 1)
                    if label[:2] == "ot":
                        b = int(label[2:])
                        act.wait_ge(pv_done, SETS * (i - 1) + BANKS[b][-1] + 1)
                        nc.scalar.activation(ot[:, b, :], ps[:, 6 + b, :], ACT.Copy).then_inc(ot_copied, 1)
                    if reader != "act":
                        continue
                    here = slot(step.slot(label))
                    act.wait_ge(psum_filled, step.filled(label))
                    if label[:3] == "exp":
                        g = int(label[3:])
                        if g % GS == 0:
                            need(act, pv_done, SETS * i + g // GS - 1)
                        nc.scalar.activation(pT[:, g % RING, :], here, ACT.Exp, scale=SCALE)\
                            .then_inc(psum_read["act"], 1)
                    elif label[:3] == "qkv":
                        c = int(label[3:])
                        if c == 0:
                            need(act, v_copied, i + 1)
                            need(act, split_done, i + 1)
                        nc.scalar.activation(qkv[:, odd, 2 * c:2 * c + 2, :],
                                             here.rearrange("p (a x) -> p a x", a=2)[:, :, 0:3 * D],
                                             ACT.Copy).then_inc(psum_read["act"], 1)
                    elif label == "oT":
                        nc.scalar.activation(oT[:], here[:, 0:T * P], ACT.Copy).then_inc(psum_read["act"], 1)
                    else:
                        out, turn = {"k0": (kT, odd), "k1": (kT, 1 - odd), "r0": (qT, odd), "r1": (qT, odd)}[label]
                        c = int(label[1])
                        nc.scalar.activation(out[:, turn, 4 * c:4 * c + 4, :],
                                             here.bitcast(BF16).rearrange("p (a x) -> p a x", a=4),
                                             ACT.Copy).then_inc(psum_read["act"], 1)

            run(act, work)

        @block.tensor
        def _(pe):
            pe.wait_ge(pool_setup, POOL_SETUP[whole])
            pe.wait_ge(consts_loaded, 80 if whole else 48)

            def side(x, turn, h, rows, c0, n):
                r0 = SLOT * (h % 2)
                return x[r0:r0 + rows, turn, h // 2, c0:c0 + n]

            def wait_reads(step, *uses):
                for reader in psum_read:
                    found = [(use(step.least)[1], use) for use in uses
                             if use(step.least) is not None and use(step.least)[0] == reader]
                    if found:
                        count, use = max(found, key=lambda x: x[0])
                        need_apart(pe, psum_read[reader], use(step)[1], count)

            def work(step):
                i, odd, least = step.i, step.odd, step.least.i
                for label, reader in step.now:
                    if label[:2] == "pv":
                        s, k = int(label[2]), int(label[3])
                        if k > 0:
                            pass
                        elif s < SETS - 1:
                            wait_reads(step, lambda x: x.read(f"exp{GS * (s + 1) - 1}"))
                        else:
                            wait_reads(step, lambda x: x.read_before(f"exp{NG - 1}"))
                        if s == 0 and k == 0:
                            need_apart(pe, v_copied, i + 1, least + 1)
                            need_apart(pe, ot_copied, 2 * i, 2 * least)
                        b = bank_of[s]
                        for h in range(4 * s, 4 * s + 4):
                            g, col = where[h, k]
                            n_q, row = len(askers(k)) * P, WIDE * (h % 4)
                            last = nc.tensor.matmul(ps[row:row + WIDE, 6 + b, k * P:k * P + n_q],
                                                    v1[:, k, h, :], pT[:, g % RING, col:col + n_q],
                                                    start=(s == BANKS[b][0] and k == 0),
                                                    stop=(s == BANKS[b][-1] and k == T - 1),
                                                    tile_position=(0, row))
                        if k == T - 1:
                            last.then_inc(pv_done, 1)
                    if not reader:
                        continue
                    out = slot(step.slot(label))
                    needed = {"max0": [lambda x: x.read_before("k0"), lambda x: x.read_before("q0")],
                              f"max{max_half}": [lambda x: x.read("k1"), lambda x: x.read("q1")],
                              "exp0": [lambda x: x.read("r0")], f"exp{exp_half}": [lambda x: x.read("r1")],
                              "qkv0": [lambda x: x.read("xnT")], "oT": [lambda x: x.read("sums")],
                              "proj": [lambda x: x.read("oT")]}.get(label, [])
                    wait_reads(step, lambda x: x.freed(label), *needed)
                    kind, number = label.rstrip("0123456789"), int("0" + label.lstrip("abcdefghijklmnopqrstuvwxyzTN"))
                    if kind in ("k", "q", "r"):
                        turn = 1 - odd if label in ("k1", "q1") else odd
                        if label == "k0":
                            need_apart(pe, stack_ready["dve"], i + 3, least + 3)
                        if label == "q0":
                            need_apart(pe, stack_ready["act"], i + 3, least + 3)
                        if label == "r0":
                            need_apart(pe, neg_max_ready, i + 1, least + 1)
                        for pair in range(4 * number, 4 * number + 4):
                            for t in range(T):
                                at = ((pair % 4) * T + t) * P
                                last = nc.tensor.transpose(
                                    out.bitcast(BF16)[:, at:at + P],
                                    stk[:, turn, int(kind == "k"), t * H + 2 * pair:t * H + 2 * pair + 2, :]
                                    .rearrange("p a s -> p (a s)"), identb[:])
                    elif kind == "max":
                        t, h0, heads, n_keys, pitch = max_groups[number]
                        for h in range(h0, h0 + heads):
                            col = 512 * (h % 2) + pitch * ((h - h0) // 2)
                            nc.tensor.matmul(out[:, col:col + n_keys], side(qT, 1 - odd, h, ROWS1, t * P, P),
                                             side(kT, 1 - odd, h, ROWS1, seen(t)[0] * P, n_keys),
                                             start=True, stop=False)
                            diag = col + n_keys - P
                            last = nc.tensor.matmul(out[:, diag:diag + P], identb[:], mask_q[:],
                                                    start=False, stop=True)
                    elif kind == "exp":
                        for h, k, col in exp_groups[number]:
                            n_q = len(askers(k)) * P
                            nc.tensor.matmul(out[:, col:col + n_q], side(kT, odd, h, ROWS2, k * P, P),
                                             side(qT, odd, h, ROWS2, k * P, n_q), start=True, stop=False)
                            last = nc.tensor.matmul(out[:, col:col + P], identb[:], mask_k[:], start=False, stop=True)
                    elif kind == "xnT":
                        need_apart(pe, xn_ready, i + 3, least + 3)
                        for t in range(T):
                            last = nc.tensor.transpose(out[:, t * P:(t + 1) * P], xn[:, t, :], ident[:])
                    elif kind == "qkv":
                        for a in range(2):
                            t = 2 * number + a
                            part = out[:, 512 * a:512 * a + 3 * D]
                            last = nc.tensor.matmul(part, xnT[:, t * P:(t + 1) * P], wqkv[:], start=True, stop=whole)
                            if not whole:
                                last = nc.tensor.matmul(part, ones1[:], brow[0:1, 0:3 * D], start=False, stop=True)
                    elif kind == "sums":
                        need_apart(pe, ot_copied, 2 * i, 2 * least)
                        for b, sets in enumerate(BANKS):
                            for t in range(T):
                                at = 512 * (t // 2) + ((t % 2) * H + 4 * sets[0]) * (DH + 1)
                                last = nc.tensor.matmul(out[:, at:at + 4 * len(sets) * (DH + 1)],
                                                        ot[:, b, t * P:(t + 1) * P],
                                                        select[:, 0:len(sets), :, :]
                                                        .rearrange("p s j e -> p (s j e)"), start=True, stop=True)
                    elif kind == "oT":
                        for t in range(T):
                            last = nc.tensor.transpose(out[:, t * P:(t + 1) * P], on[:, t, :], ident[:])
                    elif kind == "proj":
                        for t in range(T):
                            part = out[:, t * D:(t + 1) * D]
                            last = nc.tensor.matmul(part, oT[:, t * P:(t + 1) * P], wo[:], start=True, stop=whole)
                            if not whole:
                                last = nc.tensor.matmul(part, ones1[:], brow[0:1, 3 * D:4 * D],
                                                        start=False, stop=True)
                    last.then_inc(psum_filled, 1)

            run(pe, work)

        @block.vector
        def _(dve):
            if whole:
                at = [0]

                def link(ins):
                    ins.then_inc(setup_chain, 1)
                    at[0] += 1
                    dve.wait_ge(setup_chain, at[0])

                dve.wait_ge(setup_act, 1)
                link(nc.vector.tensor_scalar(gts[:, 1:3, :], gts[:, 1:3, :], 1.0, None, ALU.add))
                link(nc.vector.reciprocal(gts[:, 1:3, :], gts[:, 1:3, :]))
                dve.wait_ge(pool_setup, POOL_SETUP[whole])
                link(nc.vector.tensor_copy(posf[:], pos_i[:]))
                link(nc.vector.tensor_tensor(gts[:, 0, :], gts[:, 0, :], gts[:, 2, :], ALU.mult))
                dec_v = dec[:].rearrange("p (t h) -> p t h", h=H)
                link(nc.vector.tensor_tensor(dec_v, posf[:].unsqueeze(2).to_broadcast([P, T, H]),
                                             gts[:, 0:1, :].to_broadcast([P, T, H]), ALU.mult))
                link(nc.vector.tensor_scalar(dec[:], dec[:], 1.0 / SCALE, None, ALU.mult))
                k_dec = [[stk[:, turn, 1, :, DECAY_AT + c] for c in range(3)] for turn in range(2)]
                link(nc.vector.tensor_copy(k_dec[0][0], dec[:]))
                link(nc.vector.tensor_tensor(decr[:, 0, :], dec[:], k_dec[0][0], ALU.subtract))
                link(nc.vector.tensor_copy(k_dec[0][1], decr[:, 0, :]))
                link(nc.vector.tensor_tensor(k_dec[0][2], decr[:, 0, :], k_dec[0][1], ALU.subtract))
                for c in range(3):
                    link(nc.vector.tensor_copy(k_dec[1][c], k_dec[0][c]))
                link(nc.vector.tensor_tensor(th0[:, :, :], posf[:].unsqueeze(2).to_broadcast([P, T, DH // 2]),
                                             freq[:].unsqueeze(1).to_broadcast([P, T, DH // 2]), ALU.mult))
                for t in range(T):
                    link(nc.vector.tensor_tensor(th[:, t, :, :], th0[:, t:t + 1, :].to_broadcast([P, H, DH // 2]),
                                                 gts[:, 1, :].unsqueeze(2).to_broadcast([P, H, DH // 2]), ALU.mult))
                flat = th[:, :, :, :].rearrange("p t h f -> p (t h f)")
                turn_hi = 6.28125
                turn_lo = float(np.float32(2 * math.pi - turn_hi))
                for c, quarter in enumerate((0.25, 0.0)):
                    if c:
                        dve.wait_ge(setup_act, 2)
                    link(nc.vector.tensor_scalar(turnsf[:], flat, 1.0 / (2 * math.pi), quarter, ALU.mult, ALU.add))
                    link(nc.vector.tensor_scalar(turnsf[:], turnsf[:], 12582912.0, None, ALU.add))
                    link(nc.vector.tensor_scalar(turnsf[:], turnsf[:], 12582912.0, None, ALU.subtract))
                    link(nc.vector.scalar_tensor_tensor(ang[:], turnsf[:], -turn_hi, flat, ALU.mult, ALU.add))
                    link(nc.vector.scalar_tensor_tensor(ang[:], turnsf[:], -turn_lo, ang[:], ALU.mult, ALU.add))
                    link(nc.vector.tensor_scalar(ang[:], ang[:], quarter * 2 * math.pi, None, ALU.add))
                    link(nc.vector.tensor_scalar(ang[:], ang[:], 3.1415925, -3.1415925, ALU.min, ALU.max))
                    assert at[0] == ANGLE_STEPS[c], at
                dve.wait_ge(setup_act, 3)
                nc.vector.tensor_copy(decr[:, 1, 0:1], decr[:, 0, 0:1]).then_inc(setup_done, 1)
            else:
                dve.wait_ge(pool_setup, POOL_SETUP[whole])
            PARTS_CHAIN = 2 * T + 6
            chain = Count(vchain, PARTS_CHAIN)
            neg_chain = Count(max_chain, 4)
            sum_chain = Count(sums_chain, 1)

            def parts_step(step, c_step):
                source = rot if whole else qkv[:, step.odd, :, :]

                def part(c, n):
                    return stk[:, step.odd, c, :, n * DH:(n + 1) * DH].rearrange("p (t h) e -> p t h e", h=H)

                def whole_value(c):
                    return source[:, :, c * D:(c + 1) * D].rearrange("p t (h e) -> p t h e", e=DH)

                def left(c):
                    return rest[:, c, :, :].rearrange("p t (h e) -> p t h e", e=DH)

                if c_step == 0:
                    if whole:
                        dve.wait_ge(rotated, step.i + 3)
                    else:
                        wait_read(dve, step, "qkv1")
                    if "r1" in step.at:
                        dve.wait_ge(psum_filled, step.filled("r1"))
                    for c in range(2):
                        chain.add(nc.vector.tensor_copy(part(c, 0), whole_value(c)))
                elif c_step == 1:
                    chain.wait(dve)
                    for c in range(2):
                        chain.add(nc.vector.tensor_tensor(left(c), whole_value(c), part(c, 0), ALU.subtract))
                elif c_step == 2:
                    chain.wait(dve)
                    for c in range(2):
                        chain.add(nc.vector.tensor_copy(part(c, 4), left(c)))
                else:
                    chain.wait(dve)
                    for c, n in ((0, 5), (1, 2)):
                        last = nc.vector.tensor_tensor(part(c, n), left(c), part(c, 4), ALU.subtract)
                    last.then_inc(split_done, 1)

            def work(step):
                i, j, odd = step.i, step.i + 2, step.odd

                def tile(t):
                    return xr[:, bass.ds(j * T + t, 1), :].rearrange("p a d -> p (a d)")

                for label, reader in step.now:
                    if label == "stats":
                        chain.turn(j)
                        dve.wait_ge(x_loaded, 16 * (j + 1))
                        for t in range(T):
                            chain.add(nc.vector.bn_stats(stats[:, t, :], tile(t)))
                    elif label == "aggregate":
                        need_apart(dve, vchain, chain.base + chain.n, PARTS_CHAIN * (step.least.i + 2) + chain.n)
                        for t in range(T):
                            chain.add(nc.vector.bn_aggr(mv[:, t, :], stats[:, t, :]))
                        chain.wait(dve)
                        nc.vector.tensor_scalar(ve[:], mv[:, :, 1], EPS, None, ALU.add).then_inc(var_ready, 1)
                    elif label == "xn":
                        dve.wait_ge(rstd_ready, j + 1)
                        for t in range(T):
                            last = nc.vector.tensor_scalar(xn[:, t, :], tile(t), mv[:, t, 0:1], rstd[:, t:t + 1],
                                                           ALU.subtract, ALU.mult)
                        last.then_inc(xn_ready, 1)
                    elif label[:5] == "split":
                        parts_step(step, int(label[5:]))
                    elif label == "stack":
                        dve.wait_ge(split_done, j + 1)
                        for a, b in ((0, 3), (0, 5), (4, 1)):
                            last = nc.vector.tensor_copy(stk[:, odd, 1, :, b * DH:(b + 1) * DH],
                                                         stk[:, odd, 1, :, a * DH:(a + 1) * DH])
                        last.then_inc(stack_ready["dve"], 1)
                        chain.end("norm and parts")
                    elif label == "negative_max":
                        q_max = [stk[:, 1 - odd, 0, :, MAX_AT + c] for c in range(3)]
                        neg_chain.turn(i + 1)
                        wait_read(dve, step, f"max{NM - 1}")
                        neg_chain.add(nc.vector.tensor_scalar(mrest[:, 0, :], mx[:], -1.0, None, ALU.mult))
                        neg_chain.wait(dve)
                        neg_chain.add(nc.vector.tensor_copy(q_max[0], mrest[:, 0, :]))
                        neg_chain.wait(dve)
                        neg_chain.add(nc.vector.tensor_tensor(mrest[:, 1, :], mrest[:, 0, :], q_max[0], ALU.subtract))
                        neg_chain.wait(dve)
                        neg_chain.add(nc.vector.tensor_copy(q_max[1], mrest[:, 1, :]))
                        neg_chain.wait(dve)
                        nc.vector.tensor_tensor(q_max[2], mrest[:, 1, :], q_max[1], ALU.subtract)\
                            .then_inc(neg_max_ready, 1)
                        neg_chain.end("maximum")
                    if reader != "dve":
                        continue
                    here = slot(step.slot(label))
                    dve.wait_ge(psum_filled, step.filled(label))
                    if label[:3] == "max":
                        t, h0, heads, n_keys, pitch = max_groups[int(label[3:])]
                        nc.vector.tensor_reduce(
                            mx[:, t * H + h0:t * H + h0 + heads].rearrange("p (x a) -> p a x", a=2),
                            here.rearrange("p (a x k) -> p a x k", a=2, k=pitch)[:, :, :, 0:n_keys],
                            AX.X, ALU.max).then_inc(psum_read["dve"], 1)
                    elif label == "xnT":
                        nc.vector.tensor_copy(xnT[:], here[:, 0:T * P]).then_inc(psum_read["dve"], 1)
                    elif label in ("q0", "q1"):
                        c, turn = (0, odd) if label == "q0" else (1, 1 - odd)
                        nc.vector.tensor_copy(qT[:, turn, 4 * c:4 * c + 4, :],
                                              here.bitcast(BF16).rearrange("p (a x) -> p a x", a=4))\
                            .then_inc(psum_read["dve"], 1)
                    elif label == "sums":
                        sums = here.rearrange("p (a x) -> p a x", a=2)[:, :, 0:T // 2 * H * (DH + 1)]\
                            .rearrange("p a (x e) -> p a x e", e=DH + 1)
                        sum_chain.turn(i - 1)
                        sum_chain.add(nc.vector.reciprocal(osum[:, :, :], sums[:, :, :, DH]))
                        sum_chain.wait(dve)
                        nc.vector.tensor_tensor(on[:, :, :].rearrange("p (a t) (h e) -> p a (t h) e", a=2, e=DH),
                                                sums[:, :, :, 0:DH],
                                                osum[:, :, :].unsqueeze(3).to_broadcast([P, 2, T // 2 * H, DH]),
                                                ALU.mult).then_inc(psum_read["dve"], 1)
                    elif label == "proj":
                        dve.wait_ge(y_free, i)
                        nc.vector.tensor_tensor(y[:, :, :], here[:, 0:T * D].rearrange("p (t d) -> p t d", d=D),
                                                xr[:, bass.ds((i - 1) * T, T), :], ALU.add)\
                            .then_inc(psum_read["dve"], 1)

            run(dve, work)


def kernel(**inputs):
    import concourse.bacc as _bacc
    from concourse.bass_utils import run_bass_kernel_spmd as _run

    nc = _bacc.Bacc("TRN2", target_bir_lowering=False, num_devices=1)
    arrays = {}

    def put(name, a):
        a = np.ascontiguousarray(a)
        arrays[name] = a
        return nc.dram_tensor(name, a.shape, mybir.dt.from_np(a.dtype), kind="ExternalInput").ap()

    g = {k: np.asarray(v) for k, v in inputs.items()}
    x = put("x", g["L0_attn_a_x"])
    gate = put("gate_wT", g["L0_ffn_gate_w"].T)
    f = "L0_ffn_"
    wd = g[f + "Wd"].transpose(0, 2, 1).reshape(E, FJ, P, D).transpose(0, 2, 1, 3).reshape(E, P, FJ * D)
    w_exp = put("w_exp", np.concatenate([g[f + "Wg"].transpose(0, 2, 1), g[f + "Wu"].transpose(0, 2, 1), wd], axis=2))
    w_sh = put("w_sh", np.concatenate([g[f + "Ws_g"].T, g[f + "Ws_u"].T], axis=1))
    wd_sh = put("wd_sh", g[f + "Ws_d"].T)
    f = "L0_attn_a_"
    wa = put("wa_inT", g[f + "w_in"].T)
    oa = put("wa_outT", g[f + "w_out"].T)
    bias = put("bias_a", np.concatenate([g[f + "b_in"], g[f + "b_out"]])[None, :])
    f = "L0_attn_b_"
    wb = put("wb_inT", g[f + "Wqkv"].T)
    ob = put("wb_outT", g[f + "Wo"].T)
    gates = [put(n, g[f + n]) for n in ("log_xi", "pi_gate_logit", "e_gate_logit")]
    out = nc.dram_tensor("out", (B, N, D), F32, kind="ExternalOutput").ap()
    xn = nc.dram_tensor("xn", (B, N, D), F32, kind="Internal").ap()
    x1, x2, x3 = (nc.dram_tensor(f"x{n}", (B, N, D), F32, kind="Internal").ap() for n in (1, 2, 3))
    every4, every4_out = (a.rearrange("b (p r) d -> p b r d", r=STRIDE_A) for a in (x, x1))
    others, others_out = (a.rearrange("b (p r) d -> (b p) (r d)", r=STRIDE_A)[:, D:] for a in (x, x1))
    attention_block(nc, "a", lambda i: every4[:, bass.ds(i * T, T), 0, :],
                    lambda i: every4_out[:, bass.ds(i * T, T), 0, :], B // T, wa, oa, False, bias=bias,
                    keep=(others_out, others))
    moe_block(nc, "f1", x1, x2, xn, gate, w_exp, w_sh, wd_sh)
    attention_block(nc, "b", lambda i: x2[i].rearrange("(t p) d -> p t d", p=P),
                    lambda i: x3[i].rearrange("(t p) d -> p t d", p=P), B, wb, ob, True, gates=gates)
    moe_block(nc, "f2", x3, out, xn, gate, w_exp, w_sh, wd_sh)
    r = _run(nc, [arrays], core_ids=[0])
    return r.results[0]["out"]
```

```python
from contextlib import ExitStack
import math

import numpy as np
import concourse.bass as bass
from concourse import mybir

F32 = mybir.dt.float32
BF16 = mybir.dt.bfloat16
U32 = mybir.dt.uint32
I32 = mybir.dt.int32
ALU = mybir.AluOpType
ACT = mybir.ActivationFunctionType
AX = mybir.AxisListType

P = 128
B, N, D = 16, 512, 128
H, DH = 16, 8
T = N // P
E, FE, CAP = 16, 256, 64
FJ = FE // P
EPS = 1e-5
MASKED = -1.0e30
STRIDE_A, SEG_A = 4, 64
SLOT = 64
DECAY_AT, MAX_AT = 6 * DH, 6 * DH + 3
ROWS1, ROWS2 = MAX_AT, MAX_AT + 3
ANGLE_STEPS = (15, 22)
POSITIONS = 1 + DH // 2
POOL_SETUP = {True: 26, False: 24}
SCALE = 1.0 / math.sqrt(DH)


def need(eng, sem, value):
    if isinstance(value, int) and value <= 0:
        return
    eng.wait_ge(sem, value)


def need_apart(eng, sem, value, least):
    if isinstance(value, int):
        return need(eng, sem, value)
    at = eng.to_reg(value)
    eng.wait_ge(sem, least)
    eng.wait_ge(sem, at)


class Count:

    def __init__(self, sem, per_turn):
        self.sem, self.per_turn = sem, per_turn

    def turn(self, i):
        self.base, self.n = self.per_turn * i, 0

    def add(self, ins):
        ins.then_inc(self.sem, 1)
        self.n += 1

    def wait(self, eng):
        eng.wait_ge(self.sem, self.base + self.n)

    def wait_apart(self, eng):
        need_apart(eng, self.sem, self.base + self.n, self.n)

    def end(self, what):
        assert self.n == self.per_turn, (what, self.n, self.per_turn)


def live(m, count):
    return not isinstance(m, int) or 0 <= m < count


def pipeline(eng, body, count, peel, drain):
    for n in range(peel):
        body(n, n % 2, n // 2)
    with eng.Fori(peel // 2, count // 2) as j:
        body(2 * j, 0, j)
        body(2 * j + 1, 1, j)
    for n in range(count, count + drain):
        body(n, n % 2, n // 2)


def moe_block(nc, tag, src, dst, xn_dram, gate_w, w_exp, w_sh, wd_sh):
    UNITS = 2 * FJ
    ROUNDS = CAP // 8
    EARLY = 2
    AHEAD = 6
    PAIRS = B // 2
    HALF = B // 2
    xn_rows = xn_dram.rearrange("b n d -> (b n) d")
    dst_rows = dst.rearrange("b n d -> (b n) d")
    with ExitStack() as ctx:
        def sb(name, shape, dt=F32):
            return ctx.enter_context(nc.sbuf_tensor(f"{tag}_{name}", shape, dt))

        def sem(name):
            return ctx.enter_context(nc.semaphore(f"{tag}_{name}"))

        ps = ctx.enter_context(nc.psum_tensor(f"{tag}_ps", [P, 8, 512], F32))
        ident = sb("ident", [P, P])
        xr = sb("xr", [P, B * T, D])
        gw = sb("gw", [P, E])
        wsh = sb("wsh", [P, 2 * FE])
        wdsh = sb("wdsh", [P, FJ, D])
        stats = sb("stats", [P, 2, T, 6])
        mv = sb("mv", [P, 2, T, 2])
        ve = sb("ve", [P, 2, T])
        expo = sb("expo", [P, T])
        rstd = sb("rstd", [P, 2, T])
        xn = sb("xn", [P, 2, T, D])
        xn_again = sb("xn_again", [P, 2, T, D])
        xnT = sb("xnT", [P, 2, N])
        againT = sb("againT", [P, 2, N])
        gel = sb("gel", [P, 2, 512])
        up = sb("up", [P, 2, 512])
        hT = sb("hT", [P, 2, FJ, 2 * 512])
        y = sb("y", [P, 2, T, D])
        lg = sb("lg", [P, B * T, E])
        pr = sb("pr", [P, 2, T, P])
        red = sb("red", [P, B * T])
        rows = sb("rows", [P, 2, N])
        top = sb("top", [P, 2, CAP])
        pos = sb("pos", [P, 2, CAP], U32)
        topd = sb("topd", [P, 2, 2, CAP])
        posd = sb("posd", [P, 2, 2, CAP])
        roff_i = sb("roff_i", [P, 1], I32)
        roff = sb("roff", [P, 2])
        tokens = sb("tokens", [P, E * PAIRS], U32)
        weight = sb("weight", [P, E, PAIRS])
        xg = sb("xg", [P, E, PAIRS, D])
        xgT = sb("xgT", [P, 2, 1024])
        wexp = sb("wexp", [P, 2, 2 * FE + FJ * D])
        eo = sb("eo", [P, 2, PAIRS, D])

        consts_loaded = sem("consts_loaded")
        x_loaded = [sem(f"x_loaded{s}") for s in range(2)]
        pool_setup = sem("pool_setup")
        vchain = sem("vchain")
        var_ready = sem("var_ready")
        rstd_ready = sem("rstd_ready")
        xn_ready = sem("xn_ready")
        xn_stored = [sem(f"xn_stored{s}") for s in range(2)]
        xn_back = [sem(f"xn_back{s}") for s in range(2)]
        turned = sem("turned")
        turned_again = sem("turned_again")
        again_ready = sem("again_ready")
        xnT_ready = sem("xnT_ready")
        logits_done = sem("logits_done")
        logits_read = sem("logits_read")
        gu_done = sem("gu_done")
        gelu_done = sem("gelu_done")
        h_ready = sem("h_ready")
        h_early = sem("h_early")
        down_done = sem("down_done")
        y_copied = sem("y_copied")
        y_ready = sem("y_ready")
        y_early = sem("y_early")
        y_stored = [sem(f"y_stored{s}") for s in range(2)]
        shifted = sem("shifted")
        exped = sem("exped")
        probs_ready = sem("probs_ready")
        rows_turned = sem("rows_turned")
        top_ready = sem("top_ready")
        top_turned = sem("top_turned")
        tokens_ready = sem("tokens_ready")
        gathered = [[sem(f"gathered{g}{s}") for s in range(2)] for g in range(2)]
        router_chain = sem("router_chain")
        w_loaded = [sem(f"w_loaded{s}") for s in range(2)]
        e_turned = sem("e_turned")
        xgT_ready = sem("xgT_ready")
        e_gu = sem("e_gu")
        e_gelu = sem("e_gelu")
        e_h = sem("e_h")
        e_down = sem("e_down")
        eo_ready = sem("eo_ready")
        scattered = [sem(f"scattered{g}") for g in range(2)]
        block = ctx.enter_context(nc.Block())

        def wait_h(eng, n, j):
            if isinstance(n, int) and n < EARLY:
                need(eng, h_early, FJ * n + j + 1 if n >= 0 else 0)
            else:
                eng.wait_ge(h_ready, FJ * (n - EARLY) + j + 1)

        def wait_y(eng, n):
            if isinstance(n, int) and n < EARLY:
                need(eng, y_early, n + 1)
            else:
                eng.wait_ge(y_ready, n - EARLY + 1)

        def beside(eng, step):
            step(HALF, EARLY, 0)
            step(HALF + 1, EARLY + 1, 1)
            with eng.Fori(1, HALF // 2 - 1) as j:
                step(2 * j + HALF, 2 * j + EARLY, 0)
                step(2 * j + HALF + 1, 2 * j + EARLY + 1, 1)
            step(B - 2, EARLY + HALF - 2, 0)
            step(B - 1, EARLY + HALF - 1, 1)

        @block.sync
        def _(sp):
            def load_x(b, s):
                sp.dma_start(xr[:, bass.ds(b * T, T), :],
                             src[b].rearrange("(t p) d -> p t d", p=P)).then_inc(x_loaded[s], 16)

            load_x(0, 0)
            load_x(1, 1)
            sp.dma_start(gw[:], gate_w).then_inc(consts_loaded, 16)
            sp.dma_start(wsh[:], w_sh).then_inc(consts_loaded, 16)
            sp.dma_start(wdsh[:], wd_sh.rearrange("(j p) d -> p j d", p=P)).then_inc(consts_loaded, 16)

            def store_xn(n, s):
                sp.wait_ge(xn_ready, n + 1)
                sp.dma_start(xn_dram[n].rearrange("(t p) d -> p t d", p=P), xn[:, s, :, :])\
                    .then_inc(xn_stored[s], 16)

            def norm_step(n, s, half):
                if live(n + 2, B):
                    sp.wait_ge(x_loaded[s], 16 * (half + 1))
                    load_x(n + 2, s)
                store_xn(n, s)

            norm_step(0, 0, 0)
            norm_step(1, 1, 0)
            with sp.Fori(1, HALF // 2) as j:
                norm_step(2 * j, 0, j)
                norm_step(2 * j + 1, 1, j)

            def expert_load(n, s, half):
                need(sp, e_down, n - 1)
                sp.dma_start(wexp[:, s, :], w_exp[n]).then_inc(w_loaded[s], 16)

            def load_again(n, s):
                need(sp, turned_again, n - 1)
                sp.dma_start(xn_again[:, s, :, :], xn_dram[n].rearrange("(t p) d -> p t d", p=P))\
                    .then_inc(xn_back[s], 16)

            def store_y(m, ms):
                wait_y(sp, m)
                sp.dma_start(dst[m].rearrange("(t p) d -> p t d", p=P), y[:, ms, :, :]).then_inc(y_stored[ms], 16)

            def beside_step(n, q, s):
                if not isinstance(n, int) or n + 2 < B:
                    sp.wait_ge(x_loaded[s], 8 * (n - s) + 16)
                    load_x(n + 2, s)
                load_again(q + 2, s)
                if not isinstance(n, int) or n > HALF:
                    store_xn(n - 1, 1 - s)
                if not isinstance(n, int) or q > EARLY:
                    store_y(q - 1, 1 - s)

            for s in range(2):
                expert_load(s, s, 0)
                sp.wait_ge(xn_stored[s], 16 * HALF // 2)
            for n in range(EARLY + 2):
                load_again(n, n % 2)
                if n >= 2:
                    store_y(n - 2, n % 2)
            beside(sp, beside_step)
            store_xn(B - 1, 1)
            for n in range(EARLY + HALF + 2, B):
                load_again(n, n % 2)
                store_y(n - 3, 1 - n % 2)
            for m in range(B - 3, B):
                store_y(m, m % 2)
            with sp.Fori(1, E // 2) as j:
                expert_load(2 * j, 0, j)
                expert_load(2 * j + 1, 1, j)
            for g in range(2):
                sp.wait_ge(scattered[g], 16 * PAIRS // 2 * E)

        @block.gpsimd
        def _(pool):
            nc.gpsimd.memset(ident[:], 0.0).then_inc(pool_setup, 1)
            nc.gpsimd.memset(expo[:], -0.5).then_inc(pool_setup, 1)
            nc.gpsimd.iota(roff_i[:], [[0, 1]], base=0, channel_multiplier=1).then_inc(pool_setup, 1)
            pool.wait_ge(pool_setup, 3)
            nc.gpsimd.affine_select(out=ident[:], in_=ident[:], compare_op=ALU.not_equal, fill=1.0, base=0,
                                    pattern=[[-1, P]], channel_multiplier=1).then_inc(pool_setup, 1)

            def rstd_step(n, s, half):
                if live(n, B):
                    pool.wait_ge(var_ready, n + 1)
                    nc.gpsimd.tensor_tensor(rstd[:, s, :], ve[:, s, :], expo[:], ALU.pow).then_inc(rstd_ready, 1)

            pipeline(pool, rstd_step, HALF, 2, 0)

            for n in range(EARLY + 1):
                for j in range(FJ):
                    if n < EARLY:
                        if j == 0:
                            need(pool, down_done, n - 1)
                        pool.wait_ge(gelu_done, FJ * n + j + 1)
                        nc.gpsimd.tensor_tensor(hT[:, n % 2, j, 0:512], gel[:, j, :], up[:, j, :], ALU.mult)\
                            .then_inc(h_early, 1)
                    if j == 0 and n > 0:
                        pool.wait_ge(y_copied, n)
                        y_m = y[:, (n - 1) % 2, :, :]
                        nc.gpsimd.tensor_tensor(y_m, y_m, xr[:, (n - 1) * T:n * T, :], ALU.add).then_inc(y_early, 1)

            def indices(e, k):
                return bass.IndirectOffsetOnAxis(ap=tokens[:, e * PAIRS + k:e * PAIRS + k + 1], axis=0)

            def gather(e, k):
                g = k // (PAIRS // 2)
                if k % (PAIRS // 2) == 0:
                    need(pool, gathered[g][e % 2], 16 * PAIRS // 2 * (e // 2))
                written = xn_rows[0:(g + 1) * HALF * N, :]
                nc.gpsimd.indirect_dma_start(xg[:, e, k, :], None, written, indices(e, k))\
                    .then_inc(gathered[g][e % 2], 16)

            pool.wait_ge(tokens_ready, 1)
            for s in range(2):
                pool.wait_ge(xn_stored[s], 16 * HALF // 2)
            first_half = [(e, k) for e in range(E) for k in range(PAIRS // 2)]
            for n in range(HALF, B):
                rstd_step(n, n % 2, n // 2)
                for e, k in first_half[5 * (n - HALF):5 * (n - HALF) + 5]:
                    gather(e, k)
            for e, k in first_half[5 * HALF:]:
                gather(e, k)
            pool.wait_ge(tokens_ready, 2)
            for s in range(2):
                pool.wait_ge(xn_stored[s], 16 * B // 2)
            for e in range(AHEAD):
                for k in range(PAIRS // 2, PAIRS):
                    gather(e, k)
            for s in range(2):
                pool.wait_ge(y_stored[s], 16 * B // 2)
            for e in range(E):
                for k in range(PAIRS):
                    g = k // (PAIRS // 2)
                    if k % (PAIRS // 2) == 0:
                        pool.wait_ge(eo_ready, 2 * e + g + 1)
                        need(pool, scattered[g], 16 * PAIRS // 2 * e)
                    nc.gpsimd.indirect_dma_start(dst_rows, indices(e, k), eo[:, e % 2, k, :], None,
                                                 compute_op=ALU.add).then_inc(scattered[g], 16)
                if AHEAD + e < E:
                    for k in range(PAIRS // 2, PAIRS):
                        gather(AHEAD + e, k)

        @block.scalar
        def _(act):
            def copy_xnT(n, s, bank):
                act.wait_ge(turned, n + 1)
                need(act, logits_done, n - 1)
                nc.scalar.activation(xnT[:, s, :], ps[:, bank, :], ACT.Copy).then_inc(xnT_ready, 1)

            def copy_logits(m, bank):
                act.wait_ge(logits_done, m + 1)
                nc.scalar.activation(lg[:, bass.ds(m * T, T), :],
                                     ps[:, bank, 0:T * E].rearrange("p (t e) -> p t e", e=E), ACT.Copy)\
                    .then_inc(logits_read, 1)

            def norm_step(n, s, half):
                if live(n, HALF):
                    copy_xnT(n, s, s)
                if live(n - 1, HALF):
                    copy_logits(n - 1, 3 - s)

            def exp_half(g):
                act.wait_ge(shifted, g + 1)
                part = lg[:, g * HALF * T:(g + 1) * HALF * T, :]
                nc.scalar.activation(part, part, ACT.Exp).then_inc(exped, 1)

            def copy_again(n, s):
                act.wait_ge(turned_again, n + 1)
                need(act, gu_done, FJ * (n - 1))
                nc.scalar.activation(againT[:, s, :], ps[:, 0, :], ACT.Copy).then_inc(again_ready, 1)

            def copy_y(m):
                act.wait_ge(down_done, m + 1)
                need(act, y_stored[m % 2], 16 * (m // 2))
                nc.scalar.activation(y[:, m % 2, :, :], ps[:, 6, :].rearrange("p (t d) -> p t d", d=D), ACT.Copy)\
                    .then_inc(y_copied, 1)

            def shared_step(n, s, early, stop=False):
                for j in range(FJ):
                    act.wait_ge(gu_done, FJ * n + j + 1)
                    wait_h(act, n - 1, j)
                    last = nc.scalar.activation(gel[:, j, :], ps[:, 2 + 2 * j, :], ACT.Gelu)
                    if early:
                        last = nc.scalar.activation(up[:, j, :], ps[:, 3 + 2 * j, :], ACT.Copy)
                    last.then_inc(gelu_done, 1)
                    if j == 0 and not stop:
                        copy_again(n + 1, 1 - s)
                    if j == 0 and early and n > 0:
                        copy_y(n - 1)

            def beside_step(n, q, s):
                shared_step(q, s, False)
                if not isinstance(n, int) or n > HALF:
                    copy_xnT(n - 1, 1 - s, 1)
                if not isinstance(n, int) or n > HALF + 1:
                    copy_logits(n - 2, 7)

            pipeline(act, norm_step, HALF, 4, 1)
            exp_half(0)
            copy_again(0, 0)
            for n in range(EARLY):
                shared_step(n, n % 2, True, n == EARLY - 1)
            copy_y(EARLY - 1)
            copy_again(EARLY, 0)
            beside(act, beside_step)
            copy_xnT(B - 1, 1, 1)
            copy_logits(B - 2, 7)
            copy_logits(B - 1, 7)
            exp_half(1)
            shared_step(EARLY + HALF, 0, False)
            for n in range(EARLY + HALF + 1, B):
                shared_step(n, n % 2, False, n == B - 1)

            def copy_gathered(n, s):
                act.wait_ge(e_turned, n + 1)
                need(act, e_gu, UNITS * (n - 1))
                nc.scalar.activation(xgT[:, s, :].rearrange("p (a c) -> p a c", a=2), ps[:, 0:2, :], ACT.Copy)\
                    .then_inc(xgT_ready, 1)

            def expert_step(n, s, last_expert=False):
                for u in range(UNITS):
                    act.wait_ge(e_gu, UNITS * n + u + 1)
                    if isinstance(n, int) and n == 0 and u < 2:
                        wait_h(act, B - 1, FJ - 1)
                    else:
                        act.wait_ge(e_h, UNITS * n + u - 1)
                    nc.scalar.activation(gel[:, u % 2, :], ps[:, 2 + 2 * (u % 2), :], ACT.Gelu).then_inc(e_gelu, 1)
                    if u == UNITS - 2 and not last_expert:
                        copy_gathered(n + 1, 1 - s)

            copy_gathered(0, 0)
            expert_step(0, 0)
            expert_step(1, 1)
            with act.Fori(1, E // 2 - 1) as j:
                expert_step(2 * j, 0)
                expert_step(2 * j + 1, 1)
            expert_step(E - 2, 0)
            expert_step(E - 1, 1, True)

        @block.tensor
        def _(pe):
            pe.wait_ge(pool_setup, 4)
            pe.wait_ge(consts_loaded, 48)

            def turn(n, s, bank):
                pe.wait_ge(xn_ready, n + 1)
                for t in range(T):
                    last = nc.tensor.transpose(ps[:, bank, t * P:(t + 1) * P], xn[:, s, t, :], ident[:])
                last.then_inc(turned, 1)

            def logits(m, ms, bank):
                pe.wait_ge(xnT_ready, m + 1)
                for t in range(T):
                    last = nc.tensor.matmul(ps[:, bank, t * E:(t + 1) * E], xnT[:, ms, t * P:(t + 1) * P],
                                            gw[:], start=True, stop=True)
                last.then_inc(logits_done, 1)

            def norm_step(n, s, half):
                if live(n, HALF):
                    need(pe, xnT_ready, n - 1)
                    turn(n, s, s)
                if live(n - 1, HALF):
                    need(pe, logits_read, n - 2)
                    logits(n - 1, 1 - s, 3 - s)

            def turn_beside(m, ms):
                pe.wait_ge(xnT_ready, m)
                turn(m, ms, 1)

            def logits_beside(m, ms):
                pe.wait_ge(logits_read, m)
                logits(m, ms, 7)

            def turn_rows(g):
                pe.wait_ge(probs_ready, g + 1)
                pe.wait_ge(logits_read, (g + 1) * HALF)
                for t in range(T):
                    last = nc.tensor.transpose(ps[:, 7, t * P:(t + 1) * P], pr[:, g, t, :], ident[:])
                last.then_inc(rows_turned, 1)

            def turn_top(g):
                pe.wait_ge(top_ready, g + 1)
                nc.tensor.transpose(ps[:, 7, 0:P], topd[:, g, :, :].rearrange("p a c -> p (a c)"), ident[:])
                nc.tensor.transpose(ps[:, 7, P:2 * P], posd[:, g, :, :].rearrange("p a c -> p (a c)"), ident[:])\
                    .then_inc(top_turned, 1)

            def turn_again(n, s):
                pe.wait_ge(xn_back[s], 8 * (n - s) + 16)
                need(pe, again_ready, n)
                for t in range(T):
                    last = nc.tensor.transpose(ps[:, 0, t * P:(t + 1) * P], xn_again[:, s, t, :], ident[:])
                last.then_inc(turned_again, 1)

            def down(m, ms):
                wait_h(pe, m, FJ - 1)
                wait_y(pe, m - 1)
                for t in range(T):
                    for j in range(FJ):
                        last = nc.tensor.matmul(ps[:, 6, t * D:(t + 1) * D], hT[:, ms, j, t * P:(t + 1) * P],
                                                wdsh[:, j, :], start=(j == 0), stop=(j == FJ - 1))
                last.then_inc(down_done, 1)

            def shared_step(n, s, start=False, stop=False):
                pe.wait_ge(again_ready, n + 1)
                for j in range(FJ):
                    wait_h(pe, n - 1, j)
                    for half_w in range(2):
                        last = nc.tensor.matmul(ps[:, 2 + 2 * j + half_w, :],
                                                wsh[:, half_w * FE + j * P:half_w * FE + (j + 1) * P],
                                                againT[:, s, :], start=True, stop=True)
                    last.then_inc(gu_done, 1)
                    if j == 0 and not stop:
                        turn_again(n + 1, 1 - s)
                    if j == 0 and not start:
                        down(n - 1, 1 - s)

            def beside_step(n, q, s):
                shared_step(q, s, isinstance(n, int) and n == HALF)
                if not isinstance(n, int) or n > HALF:
                    turn_beside(n - 1, 1 - s)
                if not isinstance(n, int) or n > HALF + 1:
                    logits_beside(n - 2, s)

            pipeline(pe, norm_step, HALF, 4, 1)
            turn_rows(0)
            pe.wait_ge(xnT_ready, HALF)
            turn_again(0, 0)
            for n in range(EARLY):
                shared_step(n, n % 2, n == 0, n == EARLY - 1)
            down(EARLY - 1, 1)
            turn_top(0)
            turn_again(EARLY, 0)
            pe.wait_ge(tokens_ready, 1)
            beside(pe, beside_step)
            turn_beside(B - 1, 1)
            logits_beside(B - 2, 0)
            logits_beside(B - 1, 1)
            shared_step(EARLY + HALF, 0)
            turn_rows(1)
            for n in range(EARLY + HALF + 1, B - 1):
                shared_step(n, n % 2)
            turn_top(1)
            shared_step(B - 1, 1, False, True)
            down(B - 1, 1)

            def turn_expert(n):
                for g in range(2):
                    pe.wait_ge(gathered[g][n % 2], 16 * PAIRS // 2 * (n // 2 + 1))
                if n == 0:
                    pe.wait_ge(xnT_ready, B)
                    pe.wait_ge(again_ready, B)
                need(pe, xgT_ready, n)
                for k in range(PAIRS):
                    last = nc.tensor.transpose(ps[:, k // 4, (k % 4) * P:(k % 4 + 1) * P], xg[:, n, k, :], ident[:])
                last.then_inc(e_turned, 1)

            def down_expert(m, ms):
                pe.wait_ge(e_h, UNITS * (m + 1))
                if m == 0:
                    wait_y(pe, B - 1)
                    pe.wait_ge(tokens_ready, 2)
                need(pe, eo_ready, 2 * m)
                for k in range(PAIRS):
                    for j in range(FJ):
                        last = nc.tensor.matmul(ps[:, 6 + k // 4, (k % 4) * D:(k % 4 + 1) * D],
                                                hT[:, ms, j, k * P:(k + 1) * P],
                                                wexp[:, ms, 2 * FE + j * D:2 * FE + (j + 1) * D],
                                                start=(j == 0), stop=(j == FJ - 1))
                last.then_inc(e_down, 1)

            turn_expert(0)
            for n in range(E):
                s = n % 2
                pe.wait_ge(xgT_ready, n + 1)
                pe.wait_ge(w_loaded[s], 16 * (n // 2 + 1))
                for u in range(UNITS):
                    a, j = u // FJ, u % FJ
                    if n == 0 and u < 2:
                        wait_h(pe, B - 1, u)
                    else:
                        pe.wait_ge(e_h, UNITS * n + u - 1)
                    for half_w in range(2):
                        last = nc.tensor.matmul(ps[:, 2 + 2 * (u % 2) + half_w, :],
                                                wexp[:, s, half_w * FE + j * P:half_w * FE + (j + 1) * P],
                                                xgT[:, s, a * 512:(a + 1) * 512], start=True, stop=True)
                    last.then_inc(e_gu, 1)
                    if u == 0 and n > 0:
                        down_expert(n - 1, 1 - s)
                    if u == UNITS - 2 and n + 1 < E:
                        turn_expert(n + 1)
            down_expert(E - 1, (E - 1) % 2)

        @block.vector
        def _(dve):
            chain = Count(vchain, 2 * T)

            def measure(n, s):
                chain.turn(n)
                dve.wait_ge(x_loaded[s], 8 * (n - s) + 16)
                for t in range(T):
                    chain.add(nc.vector.bn_stats(stats[:, s, t, :], xr[:, bass.ds(n * T + t, 1), :]
                                                 .rearrange("p a d -> p (a d)")))
                chain.wait_apart(dve)
                for t in range(T):
                    chain.add(nc.vector.bn_aggr(mv[:, s, t, :], stats[:, s, t, :]))
                chain.wait(dve)
                nc.vector.tensor_scalar(ve[:, s, :], mv[:, s, :, 1], EPS, None, ALU.add).then_inc(var_ready, 1)
                chain.end("normalisation")

            def norm(m, ms):
                dve.wait_ge(rstd_ready, m + 1)
                need(dve, turned, m - 1)
                need(dve, xn_stored[ms], 8 * (m - ms))
                for t in range(T):
                    last = nc.vector.tensor_scalar(xn[:, ms, t, :], xr[:, bass.ds(m * T + t, 1), :]
                                                   .rearrange("p a d -> p (a d)"),
                                                   mv[:, ms, t, 0:1], rstd[:, ms, t:t + 1],
                                                   ALU.subtract, ALU.mult)
                last.then_inc(xn_ready, 1)

            def norm_step(n, s, half):
                if live(n, HALF):
                    measure(n, s)
                if live(n - 1, HALF):
                    norm(n - 1, 1 - s)

            at = [0]

            def link(ins):
                ins.then_inc(router_chain, 1)
                at[0] += 1
                dve.wait_ge(router_chain, at[0])

            def softmax(g):
                part = slice(g * HALF * T, (g + 1) * HALF * T)
                dve.wait_ge(logits_read, (g + 1) * HALF)
                link(nc.vector.tensor_reduce(red[:, part], lg[:, part, :], AX.X, ALU.max))
                nc.vector.tensor_tensor(lg[:, part, :], lg[:, part, :],
                                        red[:, part].unsqueeze(2).to_broadcast([P, HALF * T, E]), ALU.subtract)\
                    .then_inc(shifted, 1)
                dve.wait_ge(exped, g + 1)
                link(nc.vector.tensor_reduce(red[:, part], lg[:, part, :], AX.X, ALU.add))
                link(nc.vector.reciprocal(red[:, part], red[:, part]))
                nc.vector.tensor_tensor(
                    pr[:, g, :, :].rearrange("p t (b e) -> p b t e", e=E),
                    lg[:, part, :].rearrange("p (b t) e -> p b t e", t=T),
                    red[:, part].rearrange("p (b t) -> p b t", t=T).unsqueeze(3).to_broadcast([P, HALF, T, E]),
                    ALU.mult).then_inc(probs_ready, 1)

            def take_rows(g):
                dve.wait_ge(rows_turned, g + 1)
                link(nc.vector.tensor_copy(rows[:, g, :], ps[:, 7, :]))

            def top_round(g, r):
                at8 = slice(8 * r, 8 * r + 8)
                link(nc.vector.max(top[:, g, at8], rows[:, g, :]))
                link(nc.vector.max_index(pos[:, g, at8], top[:, g, at8], rows[:, g, :]))
                if r < ROUNDS - 1:
                    link(nc.vector.match_replace(rows[:, g, :], top[:, g, at8], rows[:, g, :], -1.0))

            def tokens_of(g):
                for a in range(2):
                    nc.vector.tensor_copy(topd[:, g, a, :], top[:, g, :])
                    last = nc.vector.tensor_scalar(posd[:, g, a, :], pos[:, g, :], roff[:, g:g + 1], None, ALU.add)
                last.then_inc(top_ready, 1)
                dve.wait_ge(top_turned, g + 1)
                tok_v = tokens[:].rearrange("p (e k) -> p e k", k=PAIRS)
                for a in range(2):
                    rows_a = slice(a * CAP, (a + 1) * CAP)
                    for c, out in ((0, weight), (1, tok_v)):
                        v = ps[rows_a, 7, c * P:(c + 1) * P].rearrange("p (k a e) -> p a e k", a=2, e=E)
                        last = nc.vector.tensor_copy(out[rows_a, :, g * 4:(g + 1) * 4], v[:, a, :, :])
                        if (a, c) != (1, 1):
                            link(last)
                last.then_inc(tokens_ready, 1)

            def add_x(m, ms):
                dve.wait_ge(down_done, m + 1)
                dve.wait_ge(y_stored[ms], 8 * (m - ms))
                nc.vector.tensor_tensor(y[:, ms, :, :], ps[:, 6, :].rearrange("p (t d) -> p t d", d=D),
                                        xr[:, bass.ds(m * T, T), :], ALU.add).then_inc(y_ready, 1)

            def shared_step(n, s):
                dve.wait_ge(down_done, n - 1)
                for j in range(FJ):
                    dve.wait_ge(gelu_done, FJ * n + j + 1)
                    nc.vector.tensor_tensor(hT[:, s, j, 0:512], gel[:, j, :], ps[:, 3 + 2 * j, :], ALU.mult)\
                        .then_inc(h_ready, 1)
                    if j == 0 and not (isinstance(n, int) and n == EARLY):
                        add_x(n - 1, 1 - s)

            pipeline(dve, norm_step, HALF, 4, 1)
            dve.wait_ge(pool_setup, 4)
            link(nc.vector.tensor_scalar(roff_i[:], roff_i[:], int(math.log2(E)), int(math.log2(N)),
                                         ALU.logical_shift_right, ALU.logical_shift_left))
            for g in range(2):
                link(nc.vector.tensor_scalar(roff[:, g:g + 1], roff_i[:], float(g * HALF * N), None, ALU.add))
            softmax(0)
            take_rows(0)
            for rnd in range(ROUNDS):
                top_round(0, rnd)
            tokens_of(0)
            def beside_step(n, q, s):
                measure(n, s)
                if not isinstance(n, int) or n > HALF:
                    norm(n - 1, 1 - s)
                shared_step(q, s)

            beside(dve, beside_step)
            norm(B - 1, 1)
            softmax(1)
            shared_step(EARLY + HALF, 0)
            take_rows(1)
            for rnd in range(ROUNDS):
                top_round(1, rnd)
                if rnd % 2 and rnd + 1 < ROUNDS:
                    shared_step(EARLY + HALF + (rnd + 1) // 2, (rnd + 1) // 2 % 2)
            tokens_of(1)
            for n in range(EARLY + HALF + ROUNDS // 2, B):
                shared_step(n, n % 2)
            add_x(B - 1, 1)

            def weigh(m, ms):
                dve.wait_ge(e_down, m + 1)
                for c in range(2):
                    if not isinstance(m, int) or m >= 2:
                        dve.wait_ge(scattered[c], 16 * PAIRS // 2 * (m - 1))
                    nc.vector.tensor_tensor(
                        eo[:, ms, 4 * c:4 * c + 4, :], ps[:, 6 + c, :].rearrange("p (k d) -> p k d", d=D),
                        weight[:, bass.ds(m, 1), 4 * c:4 * c + 4].rearrange("p a k -> p (a k)")
                        .unsqueeze(2).to_broadcast([P, 4, D]), ALU.mult).then_inc(eo_ready, 1)

            def expert_step(n, s):
                need(dve, e_down, n - 1)
                for u in range(UNITS):
                    a, j = u // FJ, u % FJ
                    dve.wait_ge(e_gelu, UNITS * n + u + 1)
                    nc.vector.tensor_tensor(hT[:, s, j, a * 512:(a + 1) * 512], gel[:, u % 2, :],
                                            ps[:, 3 + 2 * (u % 2), :], ALU.mult).then_inc(e_h, 1)
                    if u == 0 and not (isinstance(n, int) and n == 0):
                        weigh(n - 1, 1 - s)

            for n in range(4):
                expert_step(n, n % 2)
            with dve.Fori(2, E // 2) as j:
                expert_step(2 * j, 0)
                expert_step(2 * j + 1, 1)
            weigh(E - 1, 1)


class Step:

    def __init__(self, i, odd, now, before, filled0, read0, first_slot, least=None):
        self.i, self.odd, self.now, self.before = i, odd, now, before
        self.filled0, self.read0, self.first_slot = filled0, read0, first_slot
        self.least = least or self
        self.uses = [u for u in now if u[1]]
        self.uses_before = [u for u in before if u[1]]
        self.at = {label: k for k, (label, _) in enumerate(self.uses)}

    def slot(self, label):
        return (self.first_slot + self.at[label]) % 3

    def filled(self, label):
        return self.filled0 + self.at[label] + 1

    def read(self, label):
        k = self.at[label]
        reader = self.uses[k][1]
        return reader, self.read0[reader] + sum(r == reader for _, r in self.uses[:k + 1])

    def read_before(self, label):
        k = [u[0] for u in self.uses_before].index(label)
        reader = self.uses_before[k][1]
        return reader, self.read0[reader] - sum(r == reader for _, r in self.uses_before[k + 1:])

    def freed(self, label):
        k = self.at[label] - 3
        if k >= 0:
            return self.read(self.uses[k][0])
        if len(self.uses_before) + k >= 0:
            return self.read_before(self.uses_before[k][0])
        return None


def attention_block(nc, tag, src, dst, turns, w_qkv, w_o, causal_tiles, bias=None, gates=None, keep=None):
    whole = causal_tiles
    SETS = H // 4
    WIDE = P // 4
    BANKS = ((0, 1, 2), (3,))
    bank_of = {s: b for b, sets in enumerate(BANKS) for s in sets}
    seen = (lambda t: range(t + 1)) if whole else (lambda t: range(t, t + 1))
    askers = (lambda k: range(k, T)) if whole else (lambda k: range(k, k + 1))
    max_groups = []
    for half in range(2):
        for t in range(T):
            n_keys = P * len(seen(t))
            pitch = {128: 128, 256: 256}.get(n_keys, 512)
            heads = 1024 // pitch
            max_groups += [(t, h, heads, n_keys, pitch) for h in range(8 * half, 8 * half + 8, heads)]
    exp_groups = []
    for s in range(SETS):
        heads = range(4 * s, 4 * s + 4)
        if whole:
            exp_groups.append([(h, 2, 512 * (h % 2) + 256 * (h % 4 // 2)) for h in heads])
            exp_groups += [[(h, 0, 0), (h, 1, 512), (h, 3, 896)] for h in heads]
        else:
            exp_groups += [[(h, k, 512 * (h % 2) + 256 * (k % 2) + P * (h % 4 // 2)) for h in heads
                            for k in (2 * a, 2 * a + 1)] for a in range(2)]
    where = {(h, k): (g, col) for g, parts in enumerate(exp_groups) for h, k, col in parts}
    NG, NM = len(exp_groups), len(max_groups)
    GS = NG // SETS
    RING = 2 * GS
    max_half, exp_half = NM // 2, NG // 2
    split_at, turn_at = (9, 14) if whole else (4, 7)
    LEAD = 3

    def events(i):
        x, m, e, f = (0 <= i + d < turns for d in (2, 1, 0, -1))
        out = []

        def add(stage, *named):
            if stage:
                out.extend(named)

        def max_group(g):
            add(m and g < NM, (f"max{g}", "dve"))

        max_group(0)
        add(x, ("stats", None))
        add(f, ("pv30", None), ("ot0", None))
        max_group(1)
        add(x, ("aggregate", None))
        add(f, ("pv31", None))
        add(e, ("r0", "act"))
        add(f, ("pv32", None))
        max_group(2)
        add(x, ("xn", None))
        add(f, ("pv33", None))
        for g in range(NG):
            add(e, (f"exp{g}", "act"))
            max_group(g + LEAD)
            add(f and g == 0, ("ot1", None))
            add(m and g == (1 if whole else 0), ("k1", "act"))
            add(m and g == (2 if whole else 0), ("q1", "dve"))
            add(e and g == (4 if whole else 1), ("r1", "act"))
            add(f and g == 1, ("sums", "dve"))
            add(x and g == 1, ("xnT", "dve"))
            add(f and g == 3, ("oT", "act"))
            add(x and g == 2, ("qkv0", "act"))
            add(x and g == 3, ("qkv1", "act"))
            add(f and g == 4, ("proj", "dve"))
            for s in range(SETS - 1):
                for k in range(T):
                    add(e and g == GS * (s + 1) + 1 + (k if whole else 0), (f"pv{s}{k}", None))
            for c in range(4):
                add(x and g == min(split_at + c, NG - 1), (f"split{c}", None))
            add(x and g == min(split_at + 4, NG - 1), ("stack", None))
            add(x and g == turn_at, ("k0", "act"))
            add(x and g == min(turn_at + 1, NG - 1), ("q0", "dve"))
        add(m, ("negative_max", None))
        return out

    loop_pairs = max(0, (turns - 4) // 2)

    def counts(i):
        uses = [r for _, r in events(i) if r]
        return {"filled": len(uses), **{r: uses.count(r) for r in ("act", "dve")}}

    def step_of(i):
        before = [counts(j) for j in range(-2, i)]
        total = {key: sum(c[key] for c in before) for key in ("filled", "act", "dve")}
        return Step(i, i % 2, events(i), events(i - 1), total["filled"], total, total["filled"] % 3)

    def step_in_loop(n, odd):
        least, full = step_of(2 + odd), counts(2)
        ahead = {key: least.read0[key] + 2 * full[key] * (n - 1) for key in full}
        assert 2 * full["filled"] % 3 == 0
        return Step(2 * n + odd, odd, least.now, least.before, ahead["filled"], ahead, least.first_slot, least)

    def run(eng, work):
        start = turns if loop_pairs == 0 else 1
        for i in range(-2, start + 1):
            work(step_of(i))
        if loop_pairs:
            with eng.Fori(1, 1 + loop_pairs) as n:
                work(step_in_loop(n, 0))
                work(step_in_loop(n, 1))
            for i in range(2 + 2 * loop_pairs, turns + 1):
                work(step_of(i))

    with ExitStack() as ctx:
        def sb(name, shape, dt=F32):
            return ctx.enter_context(nc.sbuf_tensor(f"{tag}_{name}", shape, dt))

        def sem(name):
            return ctx.enter_context(nc.semaphore(f"{tag}_{name}"))

        ps = ctx.enter_context(nc.psum_tensor(f"{tag}_ps", [P, 8, 512], F32))
        ident = sb("ident", [P, P])
        identb = sb("identb", [P, P], BF16)
        select = sb("select", [P, 3, 4, DH + 1])
        mask_q = sb("mask_q", [P, P], BF16)
        mask_k = sb("mask_k", [P, P], BF16)
        wqkv = sb("wqkv", [P, 3 * D])
        wo = sb("wo", [P, D])
        xr = sb("xr", [P, turns * T, D])
        stats = sb("stats", [P, T, 6])
        mv = sb("mv", [P, T, 2])
        ve = sb("ve", [P, T])
        expo = sb("expo", [P, T])
        rstd = sb("rstd", [P, T])
        xn = sb("xn", [P, T, D])
        xnT = sb("xnT", [P, T * P])
        qkv = sb("qkv", [P, 2, T, 3 * D])
        rest = sb("rest", [P, 2, T, D])
        stk = sb("stk", [P, 2, 2, T * H, SLOT], BF16)
        qT = sb("qT", [P, 2, H // 2, T * P], BF16)
        kT = sb("kT", [P, 2, H // 2, T * P], BF16)
        v1 = sb("v1", [P, T, H, WIDE])
        v1_sets = [(4 * s, (DH + 1) * (s % 3)) for s in range(SETS)]
        mx = sb("mx", [P, T * H])
        mrest = sb("mrest", [P, 2, T * H])
        pT = sb("pT", [P, RING, 1024])
        ot = sb("ot", [P, 2, T * P])
        osum = sb("osum", [P, 2, T * H // 2])
        on = sb("on", [P, T, D])
        oT = sb("oT", [P, T * P])
        y = sb("y", [P, T, D])
        consts_loaded = sem("consts_loaded")
        pool_setup = sem("pool_setup")
        x_loaded = sem("x_loaded")
        vchain = sem("vchain")
        max_chain = sem("max_chain")
        sums_chain = sem("sums_chain")
        var_ready = sem("var_ready")
        rstd_ready = sem("rstd_ready")
        xn_ready = sem("xn_ready")
        psum_filled = sem("psum_filled")
        psum_read = {"act": sem("psum_read_by_scalar"), "dve": sem("psum_read_by_vector")}
        v_copied = sem("v_copied")
        split_done = sem("split_done")
        stack_ready = {"act": sem("q_stack_ready"), "dve": sem("k_stack_ready")}
        neg_max_ready = sem("neg_max_ready")
        pv_done = sem("pv_done")
        ot_copied = sem("ot_copied")
        y_free = sem("y_free")
        kept = sem("kept") if keep else None
        y_stored = sem("y_stored")
        setup_chain, setup_act, pool_chain, rotated = (
            sem(name) if whole else None for name in ("setup_chain", "setup_act", "pool_chain", "rotated"))
        if whole:
            lin = sb("lin", [P, 3, H])
            gts = sb("gts", [P, 3, H])
            pos_i = sb("pos_i", [P, T], I32)
            posf = sb("posf", [P, T])
            freq = sb("freq", [P, DH // 2])
            th0 = sb("th0", [P, T, DH // 2])
            th = sb("th", [P, T, H, DH // 2])
            turnsf = sb("turnsf", [P, T * H * DH // 2])
            ang = sb("ang", [P, T * H * DH // 2])
            cs = sb("cs", [P, 2, T, 2, H * DH // 2])
            rot = sb("rot", [P, T, 2 * D])
            tmp = sb("tmp", [P, 4, T, D])
            dec = sb("dec", [P, T * H])
            decr = sb("decr", [P, T * H])
        else:
            brow = sb("brow", [1, 4 * D])
            ones1 = sb("ones1", [1, P])
        block = ctx.enter_context(nc.Block())

        def slot(k):
            return ps[:, 2 * k:2 * k + 2, :].rearrange("p a c -> p (a c)")

        def wait_read(eng, step, label):
            reader, count = step.read(label)
            eng.wait_ge(psum_read[reader], count)

        @block.sync
        def _(sp):
            def load(j):
                sp.dma_start(xr[:, bass.ds(j * T, T), :], src(j)).then_inc(x_loaded, 16)

            load(0)
            sp.dma_start(wqkv[:], w_qkv).then_inc(consts_loaded, 16)
            sp.dma_start(wo[:], w_o).then_inc(consts_loaded, 16)
            if whole:
                for c in range(3):
                    sp.dma_start(lin[:, c, :], gates[c].unsqueeze(0).to_broadcast([P, H]))\
                        .then_inc(consts_loaded, 16)
            else:
                sp.dma_start(brow[:], bias).then_inc(consts_loaded, 16)
            if keep:
                sp.dma_start(*keep).then_inc(kept, 16)
            sp.sem_inc(y_free, 1)

            def work(step):
                i = step.i
                for label, _ in step.now:
                    if label == "stats":
                        if not isinstance(i, int) or i > -2:
                            sp.wait_ge(x_loaded, 16 * (i + 2))
                            load(i + 2)
                    elif label == "proj":
                        wait_read(sp, step, "proj")
                        sp.dma_start(dst(i - 1), y[:, :, :]).then_inc(y_stored, 16)
                        sp.wait_ge(y_stored, 16 * i)
                        sp.sem_inc(y_free, 1)

            run(sp, work)
            if keep:
                sp.wait_ge(kept, 16)

        @block.gpsimd
        def _(pool):
            if whole:
                nc.gpsimd.iota(pos_i[:], [[P, T]], base=0, channel_multiplier=1).then_inc(pool_setup, 1)
                for f in range(DH // 2):
                    value = float(np.float32(math.pi) ** np.float32(1.0 - 2 * f / DH))
                    nc.gpsimd.memset(freq[:, f:f + 1], value).then_inc(pool_setup, 1)
            first = POSITIONS if whole else 0
            nc.gpsimd.memset(expo[:], -0.5).then_inc(pool_setup, 1)
            nc.gpsimd.memset(ident[:], 0.0).then_inc(pool_setup, 1)
            nc.gpsimd.memset(mask_q[:], 0.0).then_inc(pool_setup, 1)
            nc.gpsimd.memset(mask_k[:], 0.0).then_inc(pool_setup, 1)
            nc.gpsimd.memset(stk[:, :, :, :, DECAY_AT:SLOT].rearrange("p a b n s -> p (a b n) s"), 0.0)\
                .then_inc(pool_setup, 1)
            nc.gpsimd.memset(v1[:], 0.0).then_inc(pool_setup, 1)
            pool.wait_ge(pool_setup, first + 6)
            nc.gpsimd.affine_select(out=ident[:], in_=ident[:], compare_op=ALU.not_equal, fill=1.0, base=0,
                                    pattern=[[-1, P]], channel_multiplier=1).then_inc(pool_setup, 1)
            nc.gpsimd.affine_select(out=mask_q[:], in_=mask_q[:], compare_op=ALU.is_ge, fill=MASKED, base=0,
                                    pattern=[[-1, P]], channel_multiplier=1).then_inc(pool_setup, 1)
            nc.gpsimd.affine_select(out=mask_k[:], in_=mask_k[:], compare_op=ALU.is_ge, fill=MASKED, base=0,
                                    pattern=[[1, P]], channel_multiplier=-1).then_inc(pool_setup, 1)
            for h, c in v1_sets:
                nc.gpsimd.memset(v1[:, :, h:h + 4, c + DH:c + DH + 1], 1.0).then_inc(pool_setup, 1)
            for turn in range(2):
                nc.gpsimd.memset(stk[:, turn, 0, :, DECAY_AT:DECAY_AT + 3], 1.0).then_inc(pool_setup, 1)
                nc.gpsimd.memset(stk[:, turn, 1, :, MAX_AT:MAX_AT + 3], 1.0).then_inc(pool_setup, 1)
            pool.wait_ge(pool_setup, first + 17)
            nc.gpsimd.tensor_copy(identb[:], ident[:]).then_inc(pool_setup, 1)
            for n in range(3):
                c = (DH + 1) * n
                nc.gpsimd.tensor_copy(select[:, n, :, :],
                                      ident[:].rearrange("p (j c) -> p j c", c=WIDE)[:, :, c:c + DH + 1])\
                    .then_inc(pool_setup, 1)
            if not whole:
                nc.gpsimd.memset(ones1[:], 1.0).then_inc(pool_setup, 1)
                pool.wait_ge(pool_setup, 22)
                nc.gpsimd.memset(mask_q[SEG_A:P, 0:SEG_A], MASKED).then_inc(pool_setup, 1)
                pool.wait_ge(pool_setup, 23)
                nc.gpsimd.memset(mask_k[0:SEG_A, SEG_A:P], MASKED).then_inc(pool_setup, 1)
            chain = Count(pool_chain, 4)

            def work(step):
                i, j, odd = step.i, step.i + 2, step.odd
                labels = [label for label, _ in step.now]
                if "aggregate" in labels:
                    pool.wait_ge(var_ready, j + 1)
                    nc.gpsimd.tensor_tensor(rstd[:], ve[:], expo[:], ALU.pow).then_inc(rstd_ready, 1)
                if "exp0" in labels:
                    if "pv33" in labels:
                        need_apart(pool, pv_done, SETS * i, SETS * step.least.i)
                    for h, c in v1_sets:
                        last = nc.gpsimd.tensor_copy(v1[:, :, h:h + 4, c:c + DH],
                                                     qkv[:, odd, :, 2 * D + h * DH:2 * D + (h + 4) * DH]
                                                     .rearrange("p t (h e) -> p t h e", e=DH))
                    last.then_inc(v_copied, 1)
                if "qkv1" in labels and whole:
                    if isinstance(i, int) and i == -2:
                        pool.wait_ge(setup_act, 3)
                    chain.turn(j)
                    wait_read(pool, step, "qkv1")
                    even, one = (qkv[:, odd, :, bass.ds(o, D, step=2)] for o in range(2))
                    cos, sin = (cs[:, c, :, :, :].rearrange("p t a x -> p t (a x)") for c in range(2))
                    for c, (a, b) in enumerate(((even, cos), (one, sin), (even, sin), (one, cos))):
                        chain.add(nc.gpsimd.tensor_tensor(tmp[:, c, :, :], a, b, ALU.mult))
                    chain.wait(pool)
                    need(pool, split_done, j)
                    nc.gpsimd.tensor_tensor(rot[:, :, bass.ds(0, D, step=2)], tmp[:, 0, :, :], tmp[:, 1, :, :],
                                            ALU.subtract)
                    nc.gpsimd.tensor_tensor(rot[:, :, bass.ds(1, D, step=2)], tmp[:, 2, :, :], tmp[:, 3, :, :],
                                            ALU.add).then_inc(rotated, 1)
                    chain.end("rotation")

            run(pool, work)

        @block.scalar
        def _(act):
            if whole:
                act.wait_ge(consts_loaded, 80)
                nc.scalar.activation(gts[:, :, :], lin[:, :, :], ACT.Exp, scale=-1.0).then_inc(setup_act, 1)
                for c in range(2):
                    act.wait_ge(setup_chain, ANGLE_STEPS[c])
                    nc.scalar.activation(cs[:, c, :, 0, :], ang[:].rearrange("p (t x) -> p t x", t=T), ACT.Sin)
                    nc.scalar.activation(cs[:, c, :, 1, :], ang[:].rearrange("p (t x) -> p t x", t=T), ACT.Sin)\
                        .then_inc(setup_act, 1)

            def work(step):
                i, odd = step.i, step.odd
                for label, reader in step.now:
                    if label == "stack":
                        act.wait_ge(split_done, i + 3)
                        for a, b in ((0, 1), (0, 2), (4, 3)):
                            last = nc.scalar.activation(stk[:, odd, 0, :, b * DH:(b + 1) * DH],
                                                        stk[:, odd, 0, :, a * DH:(a + 1) * DH], ACT.Copy)
                        last.then_inc(stack_ready["act"], 1)
                    if label[:2] == "ot":
                        b = int(label[2:])
                        act.wait_ge(pv_done, SETS * (i - 1) + BANKS[b][-1] + 1)
                        nc.scalar.activation(ot[:, b, :], ps[:, 6 + b, :], ACT.Copy).then_inc(ot_copied, 1)
                    if reader != "act":
                        continue
                    here = slot(step.slot(label))
                    act.wait_ge(psum_filled, step.filled(label))
                    if label[:3] == "exp":
                        g = int(label[3:])
                        if g % GS == 0:
                            need(act, pv_done, SETS * i + g // GS - 1)
                        nc.scalar.activation(pT[:, g % RING, :], here, ACT.Exp, scale=SCALE)\
                            .then_inc(psum_read["act"], 1)
                    elif label[:3] == "qkv":
                        c = int(label[3:])
                        if c == 0:
                            need(act, v_copied, i + 1)
                            need(act, split_done, i + 1)
                        nc.scalar.activation(qkv[:, odd, 2 * c:2 * c + 2, :],
                                             here.rearrange("p (a x) -> p a x", a=2)[:, :, 0:3 * D],
                                             ACT.Copy).then_inc(psum_read["act"], 1)
                    elif label == "oT":
                        nc.scalar.activation(oT[:], here[:, 0:T * P], ACT.Copy).then_inc(psum_read["act"], 1)
                    else:
                        out, turn = {"k0": (kT, odd), "k1": (kT, 1 - odd), "r0": (qT, odd), "r1": (qT, odd)}[label]
                        c = int(label[1])
                        nc.scalar.activation(out[:, turn, 4 * c:4 * c + 4, :],
                                             here.bitcast(BF16).rearrange("p (a x) -> p a x", a=4),
                                             ACT.Copy).then_inc(psum_read["act"], 1)

            run(act, work)

        @block.tensor
        def _(pe):
            pe.wait_ge(pool_setup, POOL_SETUP[whole])
            pe.wait_ge(consts_loaded, 80 if whole else 48)

            def side(x, turn, h, rows, c0, n):
                r0 = SLOT * (h % 2)
                return x[r0:r0 + rows, turn, h // 2, c0:c0 + n]

            def wait_reads(step, *uses):
                for reader in psum_read:
                    found = [(use(step.least)[1], use) for use in uses
                             if use(step.least) is not None and use(step.least)[0] == reader]
                    if found:
                        count, use = max(found, key=lambda x: x[0])
                        need_apart(pe, psum_read[reader], use(step)[1], count)

            def work(step):
                i, odd, least = step.i, step.odd, step.least.i
                for label, reader in step.now:
                    if label[:2] == "pv":
                        s, k = int(label[2]), int(label[3])
                        if k == 0 and s < SETS - 1:
                            wait_reads(step, lambda x: x.read(f"exp{GS * (s + 1) - 1}"))
                        elif k == 0:
                            wait_reads(step, lambda x: x.read_before(f"exp{NG - 1}"))
                        if s == 0 and k == 0:
                            need_apart(pe, v_copied, i + 1, least + 1)
                            need_apart(pe, ot_copied, 2 * i, 2 * least)
                        b = bank_of[s]
                        for h in range(4 * s, 4 * s + 4):
                            g, col = where[h, k]
                            n_q, row = len(askers(k)) * P, WIDE * (h % 4)
                            last = nc.tensor.matmul(ps[row:row + WIDE, 6 + b, k * P:k * P + n_q],
                                                    v1[:, k, h, :], pT[:, g % RING, col:col + n_q],
                                                    start=(s == BANKS[b][0] and k == 0),
                                                    stop=(s == BANKS[b][-1] and k == T - 1),
                                                    tile_position=(0, row))
                        if k == T - 1:
                            last.then_inc(pv_done, 1)
                    if not reader:
                        continue
                    out = slot(step.slot(label))
                    needed = {"max0": [lambda x: x.read_before("k0"), lambda x: x.read_before("q0")],
                              f"max{max_half}": [lambda x: x.read("k1"), lambda x: x.read("q1")],
                              "exp0": [lambda x: x.read("r0")], f"exp{exp_half}": [lambda x: x.read("r1")],
                              "qkv0": [lambda x: x.read("xnT")], "oT": [lambda x: x.read("sums")],
                              "proj": [lambda x: x.read("oT")]}.get(label, [])
                    wait_reads(step, lambda x: x.freed(label), *needed)
                    kind, number = label.rstrip("0123456789"), int("0" + label.lstrip("abcdefghijklmnopqrstuvwxyzTN"))
                    if kind in ("k", "q", "r"):
                        turn = 1 - odd if label in ("k1", "q1") else odd
                        if label == "k0":
                            need_apart(pe, stack_ready["dve"], i + 3, least + 3)
                        if label == "q0":
                            need_apart(pe, stack_ready["act"], i + 3, least + 3)
                        if label == "r0":
                            need_apart(pe, neg_max_ready, i + 1, least + 1)
                        for pair in range(4 * number, 4 * number + 4):
                            for t in range(T):
                                at = ((pair % 4) * T + t) * P
                                last = nc.tensor.transpose(
                                    out.bitcast(BF16)[:, at:at + P],
                                    stk[:, turn, int(kind == "k"), t * H + 2 * pair:t * H + 2 * pair + 2, :]
                                    .rearrange("p a s -> p (a s)"), identb[:])
                    elif kind == "max":
                        t, h0, heads, n_keys, pitch = max_groups[number]
                        for h in range(h0, h0 + heads):
                            col = 512 * (h % 2) + pitch * ((h - h0) // 2)
                            nc.tensor.matmul(out[:, col:col + n_keys], side(qT, 1 - odd, h, ROWS1, t * P, P),
                                             side(kT, 1 - odd, h, ROWS1, seen(t)[0] * P, n_keys),
                                             start=True, stop=False)
                            diag = col + n_keys - P
                            last = nc.tensor.matmul(out[:, diag:diag + P], identb[:], mask_q[:],
                                                    start=False, stop=True)
                    elif kind == "exp":
                        for h, k, col in exp_groups[number]:
                            n_q = len(askers(k)) * P
                            nc.tensor.matmul(out[:, col:col + n_q], side(kT, odd, h, ROWS2, k * P, P),
                                             side(qT, odd, h, ROWS2, k * P, n_q), start=True, stop=False)
                            last = nc.tensor.matmul(out[:, col:col + P], identb[:], mask_k[:], start=False, stop=True)
                    elif kind == "xnT":
                        need_apart(pe, xn_ready, i + 3, least + 3)
                        for t in range(T):
                            last = nc.tensor.transpose(out[:, t * P:(t + 1) * P], xn[:, t, :], ident[:])
                    elif kind == "qkv":
                        for a in range(2):
                            t = 2 * number + a
                            part = out[:, 512 * a:512 * a + 3 * D]
                            last = nc.tensor.matmul(part, xnT[:, t * P:(t + 1) * P], wqkv[:], start=True, stop=whole)
                            if not whole:
                                last = nc.tensor.matmul(part, ones1[:], brow[0:1, 0:3 * D], start=False, stop=True)
                    elif kind == "sums":
                        need_apart(pe, ot_copied, 2 * i, 2 * least)
                        for b, sets in enumerate(BANKS):
                            for t in range(T):
                                at = 512 * (t // 2) + ((t % 2) * H + 4 * sets[0]) * (DH + 1)
                                last = nc.tensor.matmul(out[:, at:at + 4 * len(sets) * (DH + 1)],
                                                        ot[:, b, t * P:(t + 1) * P],
                                                        select[:, 0:len(sets), :, :]
                                                        .rearrange("p s j e -> p (s j e)"), start=True, stop=True)
                    elif kind == "oT":
                        for t in range(T):
                            last = nc.tensor.transpose(out[:, t * P:(t + 1) * P], on[:, t, :], ident[:])
                    elif kind == "proj":
                        for t in range(T):
                            part = out[:, t * D:(t + 1) * D]
                            last = nc.tensor.matmul(part, oT[:, t * P:(t + 1) * P], wo[:], start=True, stop=whole)
                            if not whole:
                                last = nc.tensor.matmul(part, ones1[:], brow[0:1, 3 * D:4 * D],
                                                        start=False, stop=True)
                    last.then_inc(psum_filled, 1)

            run(pe, work)

        @block.vector
        def _(dve):
            if not whole:
                dve.wait_ge(pool_setup, POOL_SETUP[whole])
            at = [0]

            def link(ins):
                ins.then_inc(setup_chain, 1)
                at[0] += 1
                dve.wait_ge(setup_chain, at[0])

            def angles(c):
                flat = th[:, :, :, :].rearrange("p t h f -> p (t h f)")
                turn_hi = 6.28125
                turn_lo = float(np.float32(2 * math.pi - turn_hi))
                quarter = (0.25, 0.0)[c]
                link(nc.vector.tensor_scalar(turnsf[:], flat, 1.0 / (2 * math.pi), quarter, ALU.mult, ALU.add))
                link(nc.vector.tensor_scalar(turnsf[:], turnsf[:], 12582912.0, None, ALU.add))
                link(nc.vector.tensor_scalar(turnsf[:], turnsf[:], 12582912.0, None, ALU.subtract))
                if c:
                    dve.wait_ge(setup_act, 2)
                link(nc.vector.scalar_tensor_tensor(ang[:], turnsf[:], -turn_hi, flat, ALU.mult, ALU.add))
                link(nc.vector.scalar_tensor_tensor(ang[:], turnsf[:], -turn_lo, ang[:], ALU.mult, ALU.add))
                link(nc.vector.tensor_scalar(ang[:], ang[:], quarter * 2 * math.pi, None, ALU.add))
                link(nc.vector.tensor_scalar(ang[:], ang[:], 3.1415925, -3.1415925, ALU.min, ALU.max))
                assert at[0] == ANGLE_STEPS[c], at

            def setup_gates():
                dve.wait_ge(setup_act, 1)
                link(nc.vector.tensor_scalar(gts[:, 1:3, :], gts[:, 1:3, :], 1.0, None, ALU.add))
                link(nc.vector.reciprocal(gts[:, 1:3, :], gts[:, 1:3, :]))
                dve.wait_ge(pool_setup, POSITIONS)
                link(nc.vector.tensor_copy(posf[:], pos_i[:]))
                link(nc.vector.tensor_tensor(th0[:, :, :], posf[:].unsqueeze(2).to_broadcast([P, T, DH // 2]),
                                             freq[:].unsqueeze(1).to_broadcast([P, T, DH // 2]), ALU.mult))
                for t in range(T):
                    link(nc.vector.tensor_tensor(th[:, t, :, :], th0[:, t:t + 1, :].to_broadcast([P, H, DH // 2]),
                                                 gts[:, 1, :].unsqueeze(2).to_broadcast([P, H, DH // 2]), ALU.mult))
                angles(0)

            def setup_decay():
                link(nc.vector.tensor_tensor(gts[:, 0, :], gts[:, 0, :], gts[:, 2, :], ALU.mult))
                dec_v = dec[:].rearrange("p (t h) -> p t h", h=H)
                link(nc.vector.tensor_tensor(dec_v, posf[:].unsqueeze(2).to_broadcast([P, T, H]),
                                             gts[:, 0:1, :].to_broadcast([P, T, H]), ALU.mult))
                link(nc.vector.tensor_scalar(dec[:], dec[:], 1.0 / SCALE, None, ALU.mult))
                dve.wait_ge(pool_setup, POOL_SETUP[whole])
                k_dec = [[stk[:, turn, 1, :, DECAY_AT + c] for c in range(3)] for turn in range(2)]
                link(nc.vector.tensor_copy(k_dec[0][0], dec[:]))
                link(nc.vector.tensor_tensor(decr[:], dec[:], k_dec[0][0], ALU.subtract))
                link(nc.vector.tensor_copy(k_dec[0][1], decr[:]))
                link(nc.vector.tensor_tensor(k_dec[0][2], decr[:], k_dec[0][1], ALU.subtract))
                for c in range(3):
                    link(nc.vector.tensor_copy(k_dec[1][c], k_dec[0][c]))

            PARTS_CHAIN = 2 * T + 6
            chain = Count(vchain, PARTS_CHAIN)
            neg_chain = Count(max_chain, 4)
            sum_chain = Count(sums_chain, 1)

            def parts_step(step, c_step):
                source = rot if whole else qkv[:, step.odd, :, :]

                def part(c, n):
                    return stk[:, step.odd, c, :, n * DH:(n + 1) * DH].rearrange("p (t h) e -> p t h e", h=H)

                def whole_value(c):
                    return source[:, :, c * D:(c + 1) * D].rearrange("p t (h e) -> p t h e", e=DH)

                def left(c):
                    return rest[:, c, :, :].rearrange("p t (h e) -> p t h e", e=DH)

                if c_step == 0:
                    if whole:
                        dve.wait_ge(rotated, step.i + 3)
                    else:
                        wait_read(dve, step, "qkv1")
                    if "r1" in step.at:
                        dve.wait_ge(psum_filled, step.filled("r1"))
                    for c in range(2):
                        chain.add(nc.vector.tensor_copy(part(c, 0), whole_value(c)))
                elif c_step == 1:
                    chain.wait(dve)
                    for c in range(2):
                        chain.add(nc.vector.tensor_tensor(left(c), whole_value(c), part(c, 0), ALU.subtract))
                elif c_step == 2:
                    chain.wait(dve)
                    for c in range(2):
                        chain.add(nc.vector.tensor_copy(part(c, 4), left(c)))
                else:
                    chain.wait(dve)
                    for c, n in ((0, 5), (1, 2)):
                        last = nc.vector.tensor_tensor(part(c, n), left(c), part(c, 4), ALU.subtract)
                    last.then_inc(split_done, 1)

            def work(step):
                i, j, odd = step.i, step.i + 2, step.odd

                setup_now = whole and isinstance(i, int) and i == -2

                def tile(t):
                    return xr[:, bass.ds(j * T + t, 1), :].rearrange("p a d -> p (a d)")

                for label, reader in step.now:
                    if label == "stats":
                        chain.turn(j)
                        dve.wait_ge(x_loaded, 16 * (j + 1))
                        for t in range(T):
                            chain.add(nc.vector.bn_stats(stats[:, t, :], tile(t)))
                    elif label == "aggregate":
                        need_apart(dve, vchain, chain.base + chain.n, PARTS_CHAIN * (step.least.i + 2) + chain.n)
                        for t in range(T):
                            chain.add(nc.vector.bn_aggr(mv[:, t, :], stats[:, t, :]))
                        chain.wait(dve)
                        nc.vector.tensor_scalar(ve[:], mv[:, :, 1], EPS, None, ALU.add).then_inc(var_ready, 1)
                    elif label == "xn":
                        if setup_now:
                            setup_gates()
                        dve.wait_ge(rstd_ready, j + 1)
                        for t in range(T):
                            last = nc.vector.tensor_scalar(xn[:, t, :], tile(t), mv[:, t, 0:1], rstd[:, t:t + 1],
                                                           ALU.subtract, ALU.mult)
                        last.then_inc(xn_ready, 1)
                    elif label[:5] == "split":
                        parts_step(step, int(label[5:]))
                    elif label == "stack":
                        dve.wait_ge(split_done, j + 1)
                        for a, b in ((0, 3), (0, 5), (4, 1)):
                            last = nc.vector.tensor_copy(stk[:, odd, 1, :, b * DH:(b + 1) * DH],
                                                         stk[:, odd, 1, :, a * DH:(a + 1) * DH])
                        last.then_inc(stack_ready["dve"], 1)
                        chain.end("norm and parts")
                    elif label == "negative_max":
                        q_max = [stk[:, 1 - odd, 0, :, MAX_AT + c] for c in range(3)]
                        neg_chain.turn(i + 1)
                        wait_read(dve, step, f"max{NM - 1}")
                        neg_chain.add(nc.vector.tensor_scalar(mrest[:, 0, :], mx[:], -1.0, None, ALU.mult))
                        neg_chain.wait(dve)
                        neg_chain.add(nc.vector.tensor_copy(q_max[0], mrest[:, 0, :]))
                        neg_chain.wait(dve)
                        neg_chain.add(nc.vector.tensor_tensor(mrest[:, 1, :], mrest[:, 0, :], q_max[0], ALU.subtract))
                        neg_chain.wait(dve)
                        neg_chain.add(nc.vector.tensor_copy(q_max[1], mrest[:, 1, :]))
                        neg_chain.wait(dve)
                        nc.vector.tensor_tensor(q_max[2], mrest[:, 1, :], q_max[1], ALU.subtract)\
                            .then_inc(neg_max_ready, 1)
                        neg_chain.end("maximum")
                    if reader != "dve":
                        continue
                    here = slot(step.slot(label))
                    dve.wait_ge(psum_filled, step.filled(label))
                    if label[:3] == "max":
                        t, h0, heads, n_keys, pitch = max_groups[int(label[3:])]
                        nc.vector.tensor_reduce(
                            mx[:, t * H + h0:t * H + h0 + heads].rearrange("p (x a) -> p a x", a=2),
                            here.rearrange("p (a x k) -> p a x k", a=2, k=pitch)[:, :, :, 0:n_keys],
                            AX.X, ALU.max).then_inc(psum_read["dve"], 1)
                    elif label == "xnT":
                        nc.vector.tensor_copy(xnT[:], here[:, 0:T * P]).then_inc(psum_read["dve"], 1)
                        if setup_now:
                            angles(1)
                            setup_decay()
                    elif label in ("q0", "q1"):
                        c, turn = (0, odd) if label == "q0" else (1, 1 - odd)
                        nc.vector.tensor_copy(qT[:, turn, 4 * c:4 * c + 4, :],
                                              here.bitcast(BF16).rearrange("p (a x) -> p a x", a=4))\
                            .then_inc(psum_read["dve"], 1)
                    elif label == "sums":
                        sums = here.rearrange("p (a x) -> p a x", a=2)[:, :, 0:T // 2 * H * (DH + 1)]\
                            .rearrange("p a (x e) -> p a x e", e=DH + 1)
                        sum_chain.turn(i - 1)
                        sum_chain.add(nc.vector.reciprocal(osum[:, :, :], sums[:, :, :, DH]))
                        sum_chain.wait(dve)
                        nc.vector.tensor_tensor(on[:, :, :].rearrange("p (a t) (h e) -> p a (t h) e", a=2, e=DH),
                                                sums[:, :, :, 0:DH],
                                                osum[:, :, :].unsqueeze(3).to_broadcast([P, 2, T // 2 * H, DH]),
                                                ALU.mult).then_inc(psum_read["dve"], 1)
                    elif label == "proj":
                        dve.wait_ge(y_free, i)
                        nc.vector.tensor_tensor(y[:, :, :], here[:, 0:T * D].rearrange("p (t d) -> p t d", d=D),
                                                xr[:, bass.ds((i - 1) * T, T), :], ALU.add)\
                            .then_inc(psum_read["dve"], 1)

            run(dve, work)


def kernel(**inputs):
    import concourse.bacc as _bacc
    from concourse.bass_utils import run_bass_kernel_spmd as _run

    nc = _bacc.Bacc("TRN2", target_bir_lowering=False, num_devices=1)
    arrays = {}

    def put(name, a):
        a = np.ascontiguousarray(a)
        arrays[name] = a
        return nc.dram_tensor(name, a.shape, mybir.dt.from_np(a.dtype), kind="ExternalInput").ap()

    g = {k: np.asarray(v) for k, v in inputs.items()}
    x = put("x", g["L0_attn_a_x"])
    gate = put("gate_wT", g["L0_ffn_gate_w"].T)
    f = "L0_ffn_"
    wd = g[f + "Wd"].transpose(0, 2, 1).reshape(E, FJ, P, D).transpose(0, 2, 1, 3).reshape(E, P, FJ * D)
    w_exp = put("w_exp", np.concatenate([g[f + "Wg"].transpose(0, 2, 1), g[f + "Wu"].transpose(0, 2, 1), wd], axis=2))
    w_sh = put("w_sh", np.concatenate([g[f + "Ws_g"].T, g[f + "Ws_u"].T], axis=1))
    wd_sh = put("wd_sh", g[f + "Ws_d"].T)
    f = "L0_attn_a_"
    wa = put("wa_inT", g[f + "w_in"].T)
    oa = put("wa_outT", g[f + "w_out"].T)
    bias = put("bias_a", np.concatenate([g[f + "b_in"], g[f + "b_out"]])[None, :])
    f = "L0_attn_b_"
    wb = put("wb_inT", g[f + "Wqkv"].T)
    ob = put("wb_outT", g[f + "Wo"].T)
    gates = [put(n, g[f + n]) for n in ("log_xi", "pi_gate_logit", "e_gate_logit")]
    out = nc.dram_tensor("out", (B, N, D), F32, kind="ExternalOutput").ap()
    xn = nc.dram_tensor("xn", (B, N, D), F32, kind="Internal").ap()
    x1, x2, x3 = (nc.dram_tensor(f"x{n}", (B, N, D), F32, kind="Internal").ap() for n in (1, 2, 3))
    every4, every4_out = (a.rearrange("b (p r) d -> p b r d", r=STRIDE_A) for a in (x, x1))
    others, others_out = (a.rearrange("b (p r) d -> (b p) (r d)", r=STRIDE_A)[:, D:] for a in (x, x1))
    attention_block(nc, "a", lambda i: every4[:, bass.ds(i * T, T), 0, :],
                    lambda i: every4_out[:, bass.ds(i * T, T), 0, :], B // T, wa, oa, False, bias=bias,
                    keep=(others_out, others))
    moe_block(nc, "f1", x1, x2, xn, gate, w_exp, w_sh, wd_sh)
    attention_block(nc, "b", lambda i: x2[i].rearrange("(t p) d -> p t d", p=P),
                    lambda i: x3[i].rearrange("(t p) d -> p t d", p=P), B, wb, ob, True, gates=gates)
    moe_block(nc, "f2", x3, out, xn, gate, w_exp, w_sh, wd_sh)
    r = _run(nc, [arrays], core_ids=[0])
    return r.results[0]["out"]
```
